# Optimizing a Trainium2 kernel written in Bass

```python
import numpy as np
import jax
import jax.numpy as jnp

def _softmax(x, axis=-1):
    return jax.nn.softmax(x, axis=axis)

def _gelu(x):
    return jax.nn.gelu(x, approximate=True)

def _silu(x):
    return jax.nn.silu(x)

def _sigmoid(x):
    return jax.nn.sigmoid(x)

def _layernorm(x, axis=-1, eps=1e-05):
    m = jnp.mean(x, axis=axis, keepdims=True)
    v = jnp.var(x, axis=axis, keepdims=True)
    return (x - m) / jnp.sqrt(v + eps)

def _scatter_add(tgt, idx, src, axis=0):
    return tgt.at[idx].add(src)

def _segment_sum(src, seg, n):
    return jax.ops.segment_sum(src, seg, n)
kernel_name = 'mk_prb_d2_jaxref_r8_f5b2c4'

def setup_inputs(seed: int=0):
    np.random.seed(seed)
    _w = jnp.asarray

    def _L0_attn_setup():
        import jax, jax.numpy as jnp
        import numpy as np
        D_MODEL = 128
        N_HEADS = 16
        DH = D_MODEL // N_HEADS
        B, T = (4, 256)
        ROPE_BASE = 10000.0
        EPS = 1e-06

        def _rope(q, k, base=ROPE_BASE):
            half = q.shape[-1] // 2
            freqs = jnp.arange(half, dtype=q.dtype)
            inv_freq = base ** (-freqs / half)
            pos = jnp.arange(q.shape[2], dtype=q.dtype)
            ang = pos[:, None] * inv_freq[None, :]
            c = jnp.cos(ang)[None, None]
            s = jnp.sin(ang)[None, None]

            def rot(x):
                x1 = x[..., :half]
                x2 = x[..., half:2 * half]
                return jnp.concatenate([x1 * c - x2 * s, x1 * s + x2 * c], axis=-1)
            return (rot(q), rot(k))

        def _phi(x):
            return jax.nn.elu(x) + 1.0

        def _forward(x, Wq, Wk, Wv, Wo):
            Bx, Tx, D = x.shape
            H, dh = (N_HEADS, D // N_HEADS)
            q = (x @ Wq.T).reshape(Bx, Tx, H, dh).transpose(0, 2, 1, 3)
            k = (x @ Wk.T).reshape(Bx, Tx, H, dh).transpose(0, 2, 1, 3)
            v = (x @ Wv.T).reshape(Bx, Tx, H, dh).transpose(0, 2, 1, 3)
            q, k = _rope(q, k)
            q = _phi(q)
            k = _phi(k)
            qT = q.transpose(2, 0, 1, 3)
            kT = k.transpose(2, 0, 1, 3)
            vT = v.transpose(2, 0, 1, 3)

            def step(carry, qkv):
                K_sum, KV = carry
                q_t, k_t, v_t = qkv
                K_sum = K_sum + k_t
                KV = KV + k_t[..., :, None] * v_t[..., None, :]
                num = jnp.einsum('bhd,bhde->bhe', q_t, KV)
                den = jnp.maximum(jnp.einsum('bhd,bhd->bh', q_t, K_sum), EPS)
                return ((K_sum, KV), num / den[..., None])
            init = (jnp.zeros((Bx, H, dh), x.dtype), jnp.zeros((Bx, H, dh, dh), x.dtype))
            _, Y = jax.lax.scan(step, init, (qT, kT, vT))
            Y = Y.transpose(1, 0, 2, 3).reshape(Bx, Tx, D)
            return Y @ Wo.T
        key = jax.random.key(seed)
        kx, kq, kk, kv, ko = jax.random.split(key, 5)
        scale = 0.02
        return {'x': jax.random.normal(kx, (B, T, D_MODEL), jnp.float32), 'Wq': jax.random.normal(kq, (D_MODEL, D_MODEL), jnp.float32) * scale, 'Wk': jax.random.normal(kk, (D_MODEL, D_MODEL), jnp.float32) * scale, 'Wv': jax.random.normal(kv, (D_MODEL, D_MODEL), jnp.float32) * scale, 'Wo': jax.random.normal(ko, (D_MODEL, D_MODEL), jnp.float32) * scale}
    _L0_attn_in = _L0_attn_setup()

    def _L0_ffn_setup():
        import jax, jax.numpy as jnp
        import numpy as np
        B, S, F, E, K = (4, 128, 128, 8, 2)
        H = 4 * F
        key = jax.random.key(seed)
        ks = jax.random.split(key, 7)

        def xavier(k, shape):
            fan_in, fan_out = (shape[-2], shape[-1])
            scale = jnp.sqrt(6.0 / (fan_in + fan_out))
            return jax.random.uniform(k, shape, jnp.float32, -scale, scale)
        return {'x': jax.random.normal(ks[0], (B, S, F), jnp.float32), 'Wg': xavier(ks[1], (F, E)), 'bg': jnp.zeros((E,), jnp.float32), 'W1': xavier(ks[2], (E, F, H)), 'b1': jnp.zeros((E, H), jnp.float32), 'W2': xavier(ks[3], (E, H, F)), 'b2': jnp.zeros((E, F), jnp.float32)}
    _L0_ffn_in = _L0_ffn_setup()

    def _L1_attn_setup():
        import jax, jax.numpy as jnp
        import numpy as np
        NUM_HEADS = 16
        key = jax.random.key(seed)
        k1, k2, k3 = jax.random.split(key, 3)
        B, N, C = (4, 512, 128)
        x = jax.random.normal(k1, (B, N, C), dtype=jnp.float32)
        w_qkv = jax.random.normal(k2, (C, 3 * C), dtype=jnp.float32) * (2.0 / (C + 3 * C)) ** 0.5
        w_proj = jax.random.normal(k3, (C, C), dtype=jnp.float32) * (1.0 / C) ** 0.5
        b_proj = jnp.zeros((C,), dtype=jnp.float32)
        return {'x': x, 'w_qkv': w_qkv, 'w_proj': w_proj, 'b_proj': b_proj}
    _L1_attn_in = _L1_attn_setup()

    def _L1_ffn_setup():
        import jax, jax.numpy as jnp
        import numpy as np
        DIM = 128

        def _reference_tuple_inner(x, W_r, W_k, W_v, mu_r, mu_k):
            B, T, C = x.shape
            x_prev = jnp.concatenate([jnp.zeros((B, 1, C), x.dtype), x[:, :-1, :]], axis=1)
            xr = mu_r * x + (1.0 - mu_r) * x_prev
            xk = mu_k * x + (1.0 - mu_k) * x_prev
            r = jax.nn.sigmoid(jnp.einsum('btc,dc->btd', xr, W_r))
            k = jnp.einsum('btc,dc->btd', xk, W_k)
            k_act = jnp.square(jax.nn.relu(k))
            out = r * jnp.einsum('btc,dc->btd', k_act, W_v)
            new_state = x[:, -1, :]
            return (out, new_state)
        key = jax.random.key(seed)
        ks = jax.random.split(key, 6)
        B, T, C = (8, 256, DIM)
        x = jax.random.normal(ks[0], (B, T, C), dtype=jnp.float32)
        s = 1.0 / np.sqrt(C)
        W_r = jax.random.uniform(ks[1], (C, C), jnp.float32, -s, s)
        W_k = jax.random.uniform(ks[2], (C, C), jnp.float32, -s, s)
        W_v = jax.random.uniform(ks[3], (C, C), jnp.float32, -s, s)
        mu_r = jax.random.uniform(ks[4], (C,), jnp.float32)
        mu_k = jax.random.uniform(ks[5], (C,), jnp.float32)
        return {'x': x, 'W_r': W_r, 'W_k': W_k, 'W_v': W_v, 'mu_r': mu_r, 'mu_k': mu_k}
    _L1_ffn_in = _L1_ffn_setup()
    _d = {'L0_attn_x': _L0_attn_in['x'], 'L0_attn_Wq': _L0_attn_in['Wq'], 'L0_attn_Wk': _L0_attn_in['Wk'], 'L0_attn_Wv': _L0_attn_in['Wv'], 'L0_attn_Wo': _L0_attn_in['Wo'], 'L0_ffn_Wg': _L0_ffn_in['Wg'], 'L0_ffn_bg': _L0_ffn_in['bg'], 'L0_ffn_W1': _L0_ffn_in['W1'], 'L0_ffn_b1': _L0_ffn_in['b1'], 'L0_ffn_W2': _L0_ffn_in['W2'], 'L0_ffn_b2': _L0_ffn_in['b2'], 'L1_attn_w_qkv': _L1_attn_in['w_qkv'], 'L1_attn_w_proj': _L1_attn_in['w_proj'], 'L1_attn_b_proj': _L1_attn_in['b_proj'], 'L1_ffn_W_r': _L1_ffn_in['W_r'], 'L1_ffn_W_k': _L1_ffn_in['W_k'], 'L1_ffn_W_v': _L1_ffn_in['W_v'], 'L1_ffn_mu_r': _L1_ffn_in['mu_r'], 'L1_ffn_mu_k': _L1_ffn_in['mu_k']}
    _x0 = _d['L0_attn_x']
    _d['L0_attn_x'] = jax.random.normal(jax.random.fold_in(jax.random.key(seed), 1), (16, 256, 128), dtype=_x0.dtype)
    del _x0
    return _d

def reference(L0_attn_x, L0_attn_Wq, L0_attn_Wk, L0_attn_Wv, L0_attn_Wo, L0_ffn_Wg, L0_ffn_bg, L0_ffn_W1, L0_ffn_b1, L0_ffn_W2, L0_ffn_b2, L1_attn_w_qkv, L1_attn_w_proj, L1_attn_b_proj, L1_ffn_W_r, L1_ffn_W_k, L1_ffn_W_v, L1_ffn_mu_r, L1_ffn_mu_k):

    def _L0_attn_ref(x, Wq, Wk, Wv, Wo):
        import jax, jax.numpy as jnp
        import numpy as np
        D_MODEL = 128
        N_HEADS = 16
        DH = D_MODEL // N_HEADS
        B, T = (4, 256)
        ROPE_BASE = 10000.0
        EPS = 1e-06

        def _rope(q, k, base=ROPE_BASE):
            half = q.shape[-1] // 2
            freqs = jnp.arange(half, dtype=q.dtype)
            inv_freq = base ** (-freqs / half)
            pos = jnp.arange(q.shape[2], dtype=q.dtype)
            ang = pos[:, None] * inv_freq[None, :]
            c = jnp.cos(ang)[None, None]
            s = jnp.sin(ang)[None, None]

            def rot(x):
                x1 = x[..., :half]
                x2 = x[..., half:2 * half]
                return jnp.concatenate([x1 * c - x2 * s, x1 * s + x2 * c], axis=-1)
            return (rot(q), rot(k))

        def _phi(x):
            return jax.nn.elu(x) + 1.0

        def _forward(x, Wq, Wk, Wv, Wo):
            Bx, Tx, D = x.shape
            H, dh = (N_HEADS, D // N_HEADS)
            q = (x @ Wq.T).reshape(Bx, Tx, H, dh).transpose(0, 2, 1, 3)
            k = (x @ Wk.T).reshape(Bx, Tx, H, dh).transpose(0, 2, 1, 3)
            v = (x @ Wv.T).reshape(Bx, Tx, H, dh).transpose(0, 2, 1, 3)
            q, k = _rope(q, k)
            q = _phi(q)
            k = _phi(k)
            qT = q.transpose(2, 0, 1, 3)
            kT = k.transpose(2, 0, 1, 3)
            vT = v.transpose(2, 0, 1, 3)

            def step(carry, qkv):
                K_sum, KV = carry
                q_t, k_t, v_t = qkv
                K_sum = K_sum + k_t
                KV = KV + k_t[..., :, None] * v_t[..., None, :]
                num = jnp.einsum('bhd,bhde->bhe', q_t, KV)
                den = jnp.maximum(jnp.einsum('bhd,bhd->bh', q_t, K_sum), EPS)
                return ((K_sum, KV), num / den[..., None])
            init = (jnp.zeros((Bx, H, dh), x.dtype), jnp.zeros((Bx, H, dh, dh), x.dtype))
            _, Y = jax.lax.scan(step, init, (qT, kT, vT))
            Y = Y.transpose(1, 0, 2, 3).reshape(Bx, Tx, D)
            return Y @ Wo.T
        return _forward(x, Wq, Wk, Wv, Wo)

    def _L0_ffn_ref(x, Wg, bg, W1, b1, W2, b2):
        import jax, jax.numpy as jnp
        import numpy as np
        B, S, F, E, K = (4, 128, 128, 8, 2)
        H = 4 * F
        gate_probs = jax.nn.softmax(x @ Wg + bg, axis=-1)
        k = K
        _, top_idx = jax.lax.top_k(gate_probs, k)
        expert_mask = jax.nn.one_hot(top_idx, gate_probs.shape[-1], dtype=gate_probs.dtype).sum(-2)
        selected = gate_probs * expert_mask
        selected = selected / (selected.sum(-1, keepdims=True) + 1e-08)
        h = jax.nn.gelu(jnp.einsum('bsf,efh->bseh', x, W1) + b1)
        expert_out = jnp.einsum('bseh,ehf->bsef', h, W2) + b2[None, None]
        return jnp.einsum('bsef,bse->bsf', expert_out, selected)

    def _L1_attn_ref(x, w_qkv, w_proj, b_proj):
        import jax, jax.numpy as jnp
        import numpy as np
        NUM_HEADS = 16
        B, N, C = x.shape
        H = NUM_HEADS
        D = C // H
        qkv = (x @ w_qkv).reshape(B, N, 3, H, D).transpose(2, 0, 3, 1, 4)
        q, k, v = (qkv[0], qkv[1], qkv[2])
        q = jax.nn.elu(q) + 1.0
        k = jax.nn.elu(k) + 1.0
        kv = jnp.einsum('bhnd,bhne->bhde', k, v)
        numerator = jnp.einsum('bhnd,bhde->bhne', q, kv)
        sum_k = k.sum(axis=-2)
        denominator = jnp.einsum('bhnd,bhd->bhn', q, sum_k)[..., None]
        y = numerator / denominator
        y = y.transpose(0, 2, 1, 3).reshape(B, N, C)
        out = y @ w_proj + b_proj
        return out

    def _L1_ffn_ref(x, W_r, W_k, W_v, mu_r, mu_k):
        import jax, jax.numpy as jnp
        import numpy as np
        DIM = 128

        def _reference_tuple_inner(x, W_r, W_k, W_v, mu_r, mu_k):
            B, T, C = x.shape
            x_prev = jnp.concatenate([jnp.zeros((B, 1, C), x.dtype), x[:, :-1, :]], axis=1)
            xr = mu_r * x + (1.0 - mu_r) * x_prev
            xk = mu_k * x + (1.0 - mu_k) * x_prev
            r = jax.nn.sigmoid(jnp.einsum('btc,dc->btd', xr, W_r))
            k = jnp.einsum('btc,dc->btd', xk, W_k)
            k_act = jnp.square(jax.nn.relu(k))
            out = r * jnp.einsum('btc,dc->btd', k_act, W_v)
            new_state = x[:, -1, :]
            return (out, new_state)
        return _reference_tuple_inner(x, W_r, W_k, W_v, mu_r, mu_k)[0]
    x = L0_attn_x
    xn = _layernorm(x, axis=-1)
    x = x + _L0_attn_ref(xn, L0_attn_Wq, L0_attn_Wk, L0_attn_Wv, L0_attn_Wo) + _L0_ffn_ref(xn, L0_ffn_Wg, L0_ffn_bg, L0_ffn_W1, L0_ffn_b1, L0_ffn_W2, L0_ffn_b2)
    xn = _layernorm(x, axis=-1)
    x = x + _L1_attn_ref(xn, L1_attn_w_qkv, L1_attn_w_proj, L1_attn_b_proj) + _L1_ffn_ref(xn, L1_ffn_W_r, L1_ffn_W_k, L1_ffn_W_v, L1_ffn_mu_r, L1_ffn_mu_k)
    return x

_drawn_inputs = setup_inputs


def setup_inputs(seed=0):
    import zlib

    import numpy as np

    out = dict(_drawn_inputs(seed))
    spreads = {'L0_ffn_bg': (0.0, 0.1),
     'L0_ffn_b1': (0.0, 0.1),
     'L0_ffn_b2': (0.0, 0.1),
     'L1_attn_b_proj': (0.0, 0.1)}
    factors = {'L0_attn_Wq': 8.0,
     'L0_attn_Wk': 8.0,
     'L0_attn_Wv': 7.211,
     'L0_attn_Wo': 7.258,
     'L1_ffn_W_r': 3.368,
     'L1_ffn_mu_r': 6.635}
    for name, (base, spread) in spreads.items():
        noise = np.random.default_rng([zlib.crc32(name.encode()), seed]).standard_normal(out[name].shape)
        drawn = base * np.exp(spread * noise) if base else spread * noise
        out[name] = jnp.asarray(drawn.astype(out[name].dtype))
    for name, factor in factors.items():
        out[name] = (out[name] * factor).astype(out[name].dtype)
    return out
```

```python
from contextlib import ExitStack

import numpy as np
import concourse.bass as bass
from concourse import mybir

P = 128
D = 128
H, DH = 16, 8
B, T = 16, 256
TOK = B * T
NT = TOK // P
GT = 4
NG = NT // GT
NE, HID, TOPK = 8, 512, 2
NC = HID // P
NS = TOK * TOPK // P + NE - 1
EPS_LN, EPS_DEN, EPS_GATE = 1e-5, 1e-6, 1e-8
BIG = 3.0e38
BIAS2, BIASP, NBIAS = NE * HID, NE * HID + NE * D, NE * HID + NE * D + D

CONSTS = {}
_at = 0
for _name, _n in (("ident", P), ("tri_incl", P), ("tri_excl", P), ("ones", P), ("head_block", P),
                  ("iota", P), ("cos", 2 * 2 * P), ("sin", 2 * 2 * P), ("first", NE), ("tile_no", NT),
                  ("pair_no", TOPK), ("slot_row", NS)):
    CONSTS[_name] = (_at, _at + _n)
    _at += _n
NCONST = _at


def constant_table():
    c = np.zeros((P, NCONST), np.float32)
    row, col = np.arange(P)[:, None], np.arange(P)[None, :]

    def put(name, a):
        lo, hi = CONSTS[name]
        c[:, lo:hi] = a

    put("ident", row == col)
    put("tri_incl", row <= col)
    put("tri_excl", row < col)
    put("ones", 1.0)
    put("head_block", row // DH == col // DH)
    put("iota", col + 0 * row)
    half = DH // 2
    inv = np.float32(10000.0) ** (-np.arange(half, dtype=np.float32) / np.float32(half))
    ang = (np.arange(T, dtype=np.float32)[:, None] * inv[None, :].astype(np.float32)).astype(np.float32)
    cos, sin = np.cos(ang), np.sin(ang)
    cos = np.tile(np.concatenate([cos, cos], 1), (1, 2 * H))
    sin = np.tile(np.concatenate([sin, -sin], 1), (1, 2 * H))
    put("cos", cos.reshape(2, P, 2 * D).transpose(1, 0, 2).reshape(P, -1))
    put("sin", sin.reshape(2, P, 2 * D).transpose(1, 0, 2).reshape(P, -1))
    put("first", NE - np.arange(NE))
    put("tile_no", 1 + np.arange(NT))
    put("pair_no", 2 * row + np.arange(TOPK))
    put("slot_row", TOK * TOPK + 256 + row + P * np.arange(NS))
    return c


def build(nc, x_in, Wq, Wk, Wv, Wo, Wg, bg, W1, b1, W2, b2, w_qkv, w_proj, b_proj, W_r, W_k, W_v,
          mu_r, mu_k, consts, out):
    f32, bf16, i32 = mybir.dt.float32, mybir.dt.bfloat16, mybir.dt.int32
    ALU, ACT, AX = mybir.AluOpType, mybir.ActivationFunctionType, mybir.AxisListType
    ds = bass.ds
    st = ExitStack()

    def sbuf(name, shape, dt=f32):
        return st.enter_context(nc.sbuf_tensor(name, shape, dt))

    def sem(name):
        return st.enter_context(nc.semaphore(name))

    xn_dram = nc.dram_tensor("xn_rows", (TOK, D), f32, kind="Internal").ap()
    y_dram = nc.dram_tensor("expert_rows", (TOK * TOPK + NS * P, D), f32, kind="Internal").ap()

    cst = sbuf("cst", [P, NCONST])

    def const(name):
        lo, hi = CONSTS[name]
        return cst[:, lo:hi]

    ident = const("ident")
    x_sb = sbuf("x_sb", [P, NT, D])
    xn = [sbuf(f"xn{p}", [P, GT, D]) for p in range(2)]
    xT = [sbuf(f"xT{p}", [P, GT, P]) for p in range(2)]
    qkv = sbuf("qkv", [P, NT * 3 * D])
    qkv3 = qkv[:, :].rearrange("p (n c) -> p n c", c=3 * D)
    w1_sb = sbuf("w1_sb", [P, NE, HID])
    w2_sb = sbuf("w2_sb", [P, NE * NC, D])
    w_raw = sbuf("w_raw", [P, 7, P])
    wT = sbuf("wT", [P, 7, P])
    wg_sb = sbuf("wg_sb", [P, NE])
    wqkv2 = sbuf("wqkv2", [P, 3 * D])
    wproj = sbuf("wproj", [P, D])
    mu = sbuf("mu", [P, 2])
    one_mu = sbuf("one_mu", [P, 2])
    bg_sb = sbuf("bg_sb", [P, NE])
    bias_sp = sbuf("bias_sp", [P, NBIAS // P])
    bias_rest = sbuf("bias_rest", [P, 2, NBIAS // P])
    bias_part = sbuf("bias_part", [P, 3, NBIAS // P], bf16)
    bias3 = sbuf("bias3", [3, NBIAS], bf16)
    ones_bf = sbuf("ones_bf", [P, P], bf16)
    tri_bf = sbuf("tri_bf", [P, P], bf16)
    iota_bf = sbuf("iota_bf", [P, P], bf16)
    stats = [sbuf(f"stats{p}", [P, GT, 6]) for p in range(2)]
    mv = [sbuf(f"mv{p}", [P, GT, 2]) for p in range(2)]
    ve = [sbuf(f"ve{p}", [P, GT]) for p in range(2)]
    rstd = [sbuf(f"rstd{p}", [P, GT]) for p in range(2)]
    mhalf = sbuf("mhalf", [P, GT])
    eps_ln = sbuf("eps_ln", [P, GT])
    scrap = sbuf("scrap", [1, 1])
    rope_a = [sbuf(f"rope_a{p}", [P, GT, 2 * D]) for p in range(2)]
    rope_b = [sbuf(f"rope_b{p}", [P, GT, 2 * D]) for p in range(2)]
    lg = sbuf("lg", [P, NT, NE])
    lgb = sbuf("lgb", [P, NT, NE])
    rt = [sbuf(f"rt{n}", [P, NT, NE]) for n in range(4)]
    oh = [sbuf(f"oh{n}", [P, NT, NE]) for n in range(TOPK)]
    r32 = sbuf("r32", [P, 12, NT])
    sel = [sbuf(f"sel{n}", [P, NT]) for n in range(TOPK)]
    m_bf = sbuf("m_bf", [P, NT, NE], bf16)
    cex_bf = sbuf("cex_bf", [P, NT, NE], bf16)
    cin_bf = sbuf("cin_bf", [P, NE], bf16)
    e8 = sbuf("e8", [P, 8, NE])
    e8i = sbuf("e8i", [P, 2, NE], i32)
    posi = sbuf("posi", [P, 3, TOPK, NT], i32)
    pos_lo = sbuf("pos_lo", [P, TOPK, NT])
    pos_hi = sbuf("pos_hi", [P, TOPK, NT])
    hot_lo = [sbuf(f"hot_lo{p}", [P, TOPK * GT, P], bf16) for p in range(2)]
    hot_hi = [sbuf(f"hot_hi{p}", [P, TOPK, GT, NS], bf16) for p in range(2)]
    hot_val = [sbuf(f"hot_val{p}", [P, 2, TOPK, GT, NS], bf16) for p in range(2)]
    cmp8 = sbuf("cmp8", [P, NS, NE])
    tab = sbuf("tab", [P, 4, NS])
    tabi = sbuf("tabi", [P, NS], i32)
    slot_exp = sbuf("slot_exp", [P, NS], i32)
    slot_tok = sbuf("slot_tok", [P, NS], i32)
    slot_dst = sbuf("slot_dst", [P, NS], i32)
    NX = 4
    AHEAD = 6
    xg = [sbuf(f"xg{n}", [P, D]) for n in range(NX)]
    ye = [sbuf(f"ye{n}", [P, D]) for n in range(NX)]
    xgT = [sbuf(f"xgT{n}", [P, P]) for n in range(2)]
    hid = [sbuf(f"hid{n}", [P, HID]) for n in range(2)]
    hidT = [sbuf(f"hidT{n}", [P, NC, P]) for n in range(2)]
    outer = [rope_a[p][:, :, :].rearrange("p a b -> p (a b)") for p in range(2)]
    cq = rope_b[0][:, :, :].rearrange("p a b -> p (a b)")
    cqk = rope_b[1][:, 0, 0:D]
    num = rope_b[1][:, 0, D:2 * D]
    y_tok = rope_b[1][:, 1, 0:D]
    yT0 = rope_b[1][:, 1, D:2 * D]
    den = rope_b[1][:, 2, 0:H]
    rden = rope_b[1][:, 2, H:2 * H]

    ps = [st.enter_context(nc.psum_tensor(f"bank{n}", [P, 512], f32)) for n in range(8)]
    for n in range(8):
        ps[n] = ps[n][:, :]

    consts_in, wts_in, late_in = sem("consts_in"), sem("wts_in"), sem("late_in")
    x_first, x_rest = sem("x_first"), sem("x_rest")
    wT_ps, wT_ready = sem("wT_ps"), sem("wT_ready")
    bias_in, bias_split, bias_rows = sem("bias_in"), sem("bias_split"), sem("bias_rows")
    small_ready, pool_const = sem("small_ready"), sem("pool_const")
    ln_stats, ln_mv, ve_ready, rstd_ready = sem("ln_stats"), sem("ln_mv"), sem("ve_ready"), sem("rstd_ready")
    xn_ready, xT_ps, xT_ready = sem("xn_ready"), sem("xT_ps"), sem("xT_ready")
    xn_saved = [sem("xn_saved0"), sem("xn_saved1")]
    lg_ps, lg_ready, qkv_ps, qkv_raw = sem("lg_ps"), sem("lg_ready"), sem("qkv_ps"), sem("qkv_raw")
    route, gate_in, gate_exp = sem("route"), sem("gate_in"), sem("gate_exp")
    rank_in, rank_ps = sem("rank_in"), sem("rank_ps")
    hot_half = sem("hot_half")
    hot_ready, tab_ps, exp_ready, idx_ready = sem("hot_ready"), sem("tab_ps"), sem("exp_ready"), sem("idx_ready")
    ropeb_ready, ropea_ready, rot_ready, phi_parts, phi_ready = (
        sem("ropeb_ready"), sem("ropea_ready"), sem("rot_ready"), sem("phi_parts"), sem("phi_ready"))
    xg_in = [sem(f"xg_in{n}") for n in range(NX)]
    xgT_ps, xgT_ready, up_ps, gelu_ready = sem("xgT_ps"), sem("xgT_ready"), sem("up_ps"), sem("gelu_ready")
    hT_ps, hT_ready, down_ps, ye_ready = sem("hT_ps"), sem("hT_ready"), sem("down_ps"), sem("ye_ready")
    ye_out = [sem(f"ye_out{n}") for n in range(NX)]
    outer_ready, cum_ps, cq_ready, num_ready, y_ready = (
        sem("outer_ready"), sem("cum_ps"), sem("cq_ready"), sem("num_ready"), sem("y_ready"))
    den_ready, rden_ready, yT_ps, yT_ready, o_ps, x_attn = (
        sem("den_ready"), sem("rden_ready"), sem("yT_ps"), sem("yT_ready"), sem("o_ps"), sem("x_attn"))

    ITS = NG // 2

    def after_first(it):
        return not (isinstance(it, int) and it == 0)

    def wait_alone(v, s, value):
        v.wait_ge(s, value)
        nc.vector.memset(scrap[:, :], 0.0)

    def norm1_vector(v, it):
        for p in range(2):
            g = it * 2 + p
            for k in range(GT):
                last = nc.vector.bn_stats(stats[p][:, k, :], x_sb[:, ds(g * GT + k, 1), :])
            last.then_inc(ln_stats, 1)
            wait_alone(v, ln_stats, g + 1)
            for k in range(GT):
                last = nc.vector.bn_aggr(mv[p][:, k, :], stats[p][:, k, :])
            last.then_inc(ln_mv, 1)
        for p in range(2):
            g = it * 2 + p
            v.wait_ge(rstd_ready, g + 1)
            if after_first(it):
                v.wait_ge(xT_ps, g - 1)
                v.wait_ge(xn_saved[p], it * 16)
            for k in range(GT):
                last = nc.vector.tensor_scalar(xn[p][:, k, :], x_sb[:, ds(g * GT + k, 1), :].rearrange("p a d -> p (a d)"),
                                               mv[p][:, k, 0:1], rstd[p][:, k:k + 1], ALU.subtract, ALU.mult)
            last.then_inc(xn_ready, 1)

    def rstd_pool(pool, g, p):
        pool.wait_ge(ln_mv, g + 1)
        nc.gpsimd.tensor_tensor(ve[p][:, :], mv[p][:, :, 1], eps_ln[:, :], ALU.add).then_inc(ve_ready, 1)
        pool.wait_ge(ve_ready, g + 1)
        nc.gpsimd.tensor_tensor(rstd[p][:, :], ve[p][:, :], mhalf[:, :],
                                ALU.pow).then_inc(rstd_ready, 1)

    def norm1_tensor(pe, it):
        for p in range(2):
            g = it * 2 + p
            pe.wait_ge(xn_ready, g + 1)
            if after_first(it):
                pe.wait_ge(xT_ready, g - 1)
            for k in range(GT):
                last = nc.tensor.transpose(ps[p][:, k * P:(k + 1) * P], xn[p][:, k, :], ident)
            last.then_inc(xT_ps, 1)
            pe.wait_ge(xT_ready, g + 1)
            if after_first(it):
                pe.wait_ge(lg_ready, g - 1)
            for k in range(GT):
                last = nc.tensor.matmul(ps[2 + p][:, k * NE:(k + 1) * NE], xT[p][:, k, :], wg_sb[:, :],
                                        start=True, stop=True)
            last.then_inc(lg_ps, 1)
            for k in range(GT):
                if after_first(it) or p:
                    pe.wait_ge(qkv_raw, g * GT + k - (GT - 1))
                nc.tensor.matmul(ps[4 + k][:, 0:3 * D], xT[p][:, k, :],
                                 wT[:, 0:3, :].rearrange("p a b -> p (a b)"), start=True, stop=True
                                 ).then_inc(qkv_ps, 1)

    def norm1_scalar(act, it):
        for p in range(2):
            g = it * 2 + p
            act.wait_ge(xT_ps, g + 1)
            if after_first(it):
                act.wait_ge(qkv_ps, (g - 1) * GT)
            nc.scalar.copy(xT[p][:, :, :].rearrange("p a b -> p (a b)"), ps[p]).then_inc(xT_ready, 1)
            act.wait_ge(lg_ps, g + 1)
            nc.scalar.copy(lg[:, ds(g * GT, GT), :].rearrange("p a e -> p (a e)"),
                           ps[2 + p][:, 0:GT * NE]).then_inc(lg_ready, 1)
            for k in range(GT):
                act.wait_ge(qkv_ps, g * GT + k + 1)
                nc.scalar.copy(qkv3[:, ds(g * GT + k, 1), :].rearrange("p a c -> p (a c)"),
                               ps[4 + k][:, 0:3 * D]).then_inc(qkv_raw, 1)

    def gather(pool, j):
        n = j % NX
        if j >= NX:
            pool.wait_ge(xgT_ps, j - NX + 1)
        pool.indirect_dma_start(out=xg[n][:, :], out_offset=None, in_=xn_dram,
                                in_offset=bass.IndirectOffsetOnAxis(ap=slot_tok[:, j:j + 1], axis=0)
                                ).then_inc(xg_in[n], 16)

    def scatter(pool, j):
        n = j % NX
        pool.wait_ge(ye_ready, j + 1)
        pool.indirect_dma_start(out=y_dram, out_offset=bass.IndirectOffsetOnAxis(ap=slot_dst[:, j:j + 1], axis=0),
                                in_=ye[n][:, :], in_offset=None).then_inc(ye_out[n], 16)

    def slot(base, s):
        return base + s

    def xg_transpose(pe, base, s):
        j, n = slot(base, s), s % NX
        q = s // NX
        pe.wait_ge(xg_in[n], (base // NX + q + 1) * 16)
        if not (isinstance(j, int) and j < 1):
            pe.wait_ge(xgT_ready, j)
        nc.tensor.transpose(ps[6][:, 0:P], xg[n][:, :], ident).then_inc(xgT_ps, 1)

    def up(pe, base, s, e):
        j, p = slot(base, s), s % 2
        pe.wait_ge(xgT_ready, j + 1)
        if not (isinstance(j, int) and j < 2):
            pe.wait_ge(gelu_ready, j - 1)
        nc.tensor.matmul(ps[3 + p], xgT[p][:, :], w1_sb[:, ds(e, 1), :], start=True, stop=False)
        nc.tensor.matmul(ps[3 + p], ones_bf[0:3, :], bias3[:, ds(e * HID, HID)],
                         start=False, stop=True).then_inc(up_ps, 1)

    def hid_transpose(pe, base, s):
        j, p = slot(base, s), s % 2
        pe.wait_ge(gelu_ready, j + 1)
        if not (isinstance(j, int) and j < 1):
            pe.wait_ge(hT_ready, j)
        for c in range(NC):
            last = nc.tensor.transpose(ps[5][:, c * P:(c + 1) * P], hid[p][:, c * P:(c + 1) * P], ident)
        last.then_inc(hT_ps, 1)

    def down(pe, base, s, e):
        j, p = slot(base, s), s % 2
        pe.wait_ge(hT_ready, j + 1)
        if not (isinstance(j, int) and j < 1):
            pe.wait_ge(ye_ready, j)
        y = ps[7][:, 0:D]
        nc.tensor.matmul(y, ones_bf[0:3, :], bias3[:, ds(e * D + BIAS2, D)], start=True, stop=False)
        for c in range(NC):
            last = nc.tensor.matmul(y, hidT[p][:, c, :], w2_sb[:, ds(e * NC + c, 1), :],
                                    start=False, stop=(c == NC - 1))
        last.then_inc(down_ps, 1)

    def out_copy(act, base, s):
        j, n = slot(base, s), s % NX
        act.wait_ge(down_ps, j + 1)
        if not (isinstance(j, int) and j < NX):
            act.wait_ge(ye_out[n], (base // NX + s // NX) * 16)
        nc.scalar.copy(ye[n][:, :], ps[7][:, 0:D]).then_inc(ye_ready, 1)

    def xgT_copy(act, base, s):
        j, p = slot(base, s), s % 2
        act.wait_ge(xgT_ps, j + 1)
        if not (isinstance(j, int) and j < 2):
            act.wait_ge(up_ps, j - 1)
        nc.scalar.copy(xgT[p][:, :], ps[6][:, 0:P]).then_inc(xgT_ready, 1)

    def gelu(act, base, s):
        j, p = slot(base, s), s % 2
        act.wait_ge(up_ps, j + 1)
        if not (isinstance(j, int) and j < 2):
            act.wait_ge(hT_ps, j - 1)
        nc.scalar.activation(hid[p][:, :], ps[3 + p], ACT.Gelu_apprx_tanh).then_inc(gelu_ready, 1)

    def hidT_copy(act, base, s):
        j, p = slot(base, s), s % 2
        act.wait_ge(hT_ps, j + 1)
        if not (isinstance(j, int) and j < 2):
            act.wait_ge(down_ps, j - 1)
        nc.scalar.copy(hidT[p][:, :, :].rearrange("p a b -> p (a b)"), ps[5]).then_inc(hT_ready, 1)

    def expert_scalar(act, base, s, last=NS):
        if 0 <= s + 3 < last:
            xgT_copy(act, base, s + 3)
        if 0 <= s + 2 < last:
            gelu(act, base, s + 2)
        if 0 <= s + 1 < last:
            hidT_copy(act, base, s + 1)
        if s >= 0:
            out_copy(act, base, s)

    def attn_outer(v, b, r):
        i = b * 2 + r
        k = qkv3[:, ds(i, 1), D:2 * D].rearrange("p a (h d) -> p (a h) d", d=DH)
        vv = qkv3[:, ds(i, 1), 2 * D:3 * D].rearrange("p a (h e) -> p (a h) e", e=DH)
        if not (isinstance(b, int) and b == 0):
            v.wait_ge(cum_ps, b * 2)
        nc.vector.tensor_tensor(outer[r].rearrange("p (h d e) -> p h d e", d=DH, e=DH),
                                k.unsqueeze(3).broadcast_to([P, H, DH, DH]),
                                vv.unsqueeze(2).broadcast_to([P, H, DH, DH]), ALU.mult).then_inc(outer_ready, 1)

    def attn_cumsum(pe, b, r):
        i = b * 2 + r
        pe.wait_ge(outer_ready, i + 1)
        if not (isinstance(i, int) and i == 0):
            pe.wait_ge(cq_ready, i * 2)
        if not (isinstance(i, int) and i < 2):
            pe.wait_ge(x_attn, i - 1)
        for half in range(2):
            cols = slice(half * 512, half * 512 + 512)
            nc.tensor.matmul(ps[half], const("tri_incl"), outer[r][:, cols], start=True, stop=(r == 0))
            if r:
                nc.tensor.matmul(ps[half], const("ones"), outer[0][:, cols], start=False, stop=True)
        last = nc.tensor.matmul(ps[2][:, 0:D], const("tri_incl"), qkv3[:, ds(i, 1), D:2 * D],
                                start=True, stop=(r == 0))
        if r:
            last = nc.tensor.matmul(ps[2][:, 0:D], const("ones"), qkv3[:, ds(i - 1, 1), D:2 * D],
                                    start=False, stop=True)
        last.then_inc(cum_ps, 1)

    def attn_apply(v, b, r):
        i = b * 2 + r
        q = qkv3[:, ds(i, 1), 0:D].rearrange("p a c -> p (a c)")
        v.wait_ge(cum_ps, i + 1)
        nc.vector.tensor_tensor(cqk, ps[2][:, 0:D], q, ALU.mult).then_inc(cq_ready, 1)
        for half in range(2):
            last = nc.vector.tensor_tensor(
                cq[:, half * 512:half * 512 + 512].rearrange("p (c e) -> p c e", e=DH),
                ps[half].rearrange("p (c e) -> p c e", e=DH),
                qkv3[:, ds(i, 1), half * 64:half * 64 + 64].rearrange("p a c -> p (a c)").unsqueeze(2).broadcast_to([P, 64, DH]),
                ALU.mult)
        last.then_inc(cq_ready, 1)

    def attn_divide(v, i):
        v.wait_ge(cq_ready, i * 2 + 1)
        nc.vector.tensor_reduce(den, cqk.rearrange("p (h d) -> p h d", d=DH), AX.X, ALU.add).then_inc(den_ready, 1)
        v.wait_ge(den_ready, i * 2 + 1)
        nc.vector.tensor_scalar(den, den, EPS_DEN, None, ALU.max).then_inc(den_ready, 1)
        v.wait_ge(den_ready, i * 2 + 2)
        nc.vector.reciprocal(rden, den).then_inc(rden_ready, 1)
        v.wait_ge(cq_ready, i * 2 + 2)
        nc.vector.tensor_reduce(num.rearrange("p (h e) -> p h e", e=DH),
                                cq.rearrange("p (h d e) -> p h e d", d=DH, e=DH), AX.X, ALU.add).then_inc(num_ready, 1)
        v.wait_ge(num_ready, i + 1)
        v.wait_ge(rden_ready, i + 1)
        if not (isinstance(i, int) and i == 0):
            v.wait_ge(yT_ps, i)
        nc.vector.tensor_tensor(y_tok.rearrange("p (h e) -> p h e", e=DH), num.rearrange("p (h e) -> p h e", e=DH),
                                rden.unsqueeze(2).broadcast_to([P, H, DH]), ALU.mult).then_inc(y_ready, 1)

    def attn_transpose(pe, i):
        pe.wait_ge(y_ready, i + 1)
        if not (isinstance(i, int) and i == NT - 1):
            pe.wait_ge(cq_ready, i * 2 + 3)
        else:
            pe.wait_ge(x_attn, i)
        nc.tensor.transpose(ps[2][:, P:2 * P], y_tok, ident).then_inc(yT_ps, 1)

    def attn_project(pe, i):
        pe.wait_ge(yT_ready, i + 1)
        nc.tensor.matmul(ps[2][:, 2 * P:3 * P], yT0, wT[:, 3, :], start=True, stop=True).then_inc(o_ps, 1)

    def attn_yT(act, i):
        act.wait_ge(yT_ps, i + 1)
        if not (isinstance(i, int) and i == 0):
            act.wait_ge(o_ps, i)
        nc.scalar.copy(yT0, ps[2][:, P:2 * P]).then_inc(yT_ready, 1)

    def attn_add(v, i):
        v.wait_ge(o_ps, i + 1)
        xi = x_sb[:, ds(i, 1), :].rearrange("p a c -> p (a c)")
        nc.vector.tensor_tensor(xi, ps[2][:, 2 * P:3 * P], xi, ALU.add).then_inc(x_attn, 1)

    at = [0]

    def view(n):
        at[0] += n
        return qkv[:, at[0] - n:at[0]]

    GP = GT * P
    ymoe = [view(GT * TOPK * D) for _ in range(2)]
    xT2 = [view(2 * (T + 1)) for _ in range(2)]
    mix_t = [[view(GP) for _ in range(2)] for _ in range(2)]
    e_q, r_q, phi_q = view(GP), view(GP), view(GP)
    e_k, r_k, phi_k = view(GP), view(GP), view(GP)
    v_aug = view(GT * (D + 1))
    kvm = view(2 * D)
    skm = view(2 * D)
    rcp = view(GP)
    yT1 = view(GP)
    e_r, sig = view(GP), view(GP)
    k_act = view(GP)
    res = [rope_a[p][:, 0:2, :].rearrange("p a b -> p (a b)") for p in range(2)]
    assert at[0] <= NT * 3 * D
    g_exp = sem("g_exp")
    y_in = [sem("y_in0"), sem("y_in1")]
    x1_ready, ln2_stats, ln2_mv, ve2_ready, rstd2_ready = (
        sem("x1_ready"), sem("ln2_stats"), sem("ln2_mv"), sem("ve2_ready"), sem("rstd2_ready"))
    x1_part = sem("x1_part")
    xn2_ready, xT2_ps, xT2_ready, mu_x, mixed = sem("xn2_ready"), sem("xT2_ps"), sem("xT2_ready"), sem("mu_x"), sem("mixed")
    q_ps, kv_ps, r_ps, kf_ps = sem("q_ps"), sem("kv_ps"), sem("r_ps"), sem("kf_ps")
    qparts, kparts, v_ready = sem("qparts"), sem("kparts"), sem("v_ready")
    phiq_ready, phik_ready, kact_ready = sem("phiq_ready"), sem("phik_ready"), sem("kact_ready")
    KV_ps, KV_ready, nd_ps, rcp_ready, yT1_ready = sem("KV_ps"), sem("KV_ready"), sem("nd_ps"), sem("rcp_ready"), sem("yT1_ready")
    er_ready, sig_parts, vf_ps, pr_ps = sem("er_ready"), sem("sig_parts"), sem("vf_ps"), sem("pr_ps")
    out_parts, res_ready = sem("out_parts"), sem("res_ready")
    out_done = [sem("out_done0"), sem("out_done1")]
    pads = sem("pads")

    def late(g):
        return not isinstance(g, int)

    def load_y(sp, it, p):
        g = it * 2 + p
        if late(it):
            sp.wait_ge(x1_ready, g - 1)
        sp.dma_start(ymoe[p].rearrange("p (n c) -> p n c", n=GT),
                     y_dram[0:TOK * TOPK, :].rearrange("(n p k) d -> p n (k d)", p=P, k=TOPK)[:, ds(g * GT, GT), :]
                     ).then_inc(y_in[p], 16)

    def front_vector(v, it, p):
        g = it * 2 + p
        v.wait_ge(y_in[p], (it + 1) * 16)
        for k in range(TOPK):
            for n in range(GT):
                xi = x_sb[:, ds(g * GT + n, 1), :].rearrange("p a c -> p (a c)")
                last = nc.vector.scalar_tensor_tensor(
                    out=xi, in0=ymoe[p][:, (n * TOPK + k) * D:(n * TOPK + k + 1) * D],
                    scalar=sel[k][:, ds(g * GT + n, 1)], in1=xi, op0=ALU.mult, op1=ALU.add)
            last.then_inc(x1_part if k == 0 else x1_ready, 1)
            wait_alone(v, x1_part if k == 0 else x1_ready, g + 1)
        for n in range(GT):
            last = nc.vector.bn_stats(stats[p][:, n, :], x_sb[:, ds(g * GT + n, 1), :])
        last.then_inc(ln2_stats, 1)
        wait_alone(v, ln2_stats, g + 1)
        for n in range(GT):
            last = nc.vector.bn_aggr(mv[p][:, n, :], stats[p][:, n, :])
        last.then_inc(ln2_mv, 1)

    def norm2_vector(v, it, p):
        g = it * 2 + p
        v.wait_ge(rstd2_ready, g + 1)
        if late(it):
            v.wait_ge(xT2_ps, g - 1)
        for n in range(GT):
            last = nc.vector.tensor_scalar(xn[p][:, n, :], x_sb[:, ds(g * GT + n, 1), :].rearrange("p a c -> p (a c)"),
                                           mv[p][:, n, 0:1], rstd[p][:, n:n + 1], ALU.subtract, ALU.mult)
        last.then_inc(xn2_ready, 1)

    def xT2_of(p):
        return xT2[p].rearrange("p (b t) -> p b t", t=T + 1)

    def mix_vector(v, it, p):
        g = it * 2 + p
        v.wait_ge(mu_x, g + 1)
        for m in range(2):
            t = mix_t[p][m].rearrange("p (b t) -> p b t", t=T)
            last = nc.vector.scalar_tensor_tensor(out=t, in0=xT2_of(p)[:, :, 0:T], scalar=one_mu[:, m:m + 1],
                                                  in1=t, op0=ALU.mult, op1=ALU.add)
        last.then_inc(mixed, 1)

    def back_vector(v, it, p):
        g = it * 2 + p
        v.wait_ge(kparts, g + 1)
        nc.vector.scalar_tensor_tensor(out=phi_k, in0=e_k, scalar=1.0, in1=r_k, op0=ALU.min, op1=ALU.add
                                       ).then_inc(phik_ready, 1)
        v.wait_ge(qparts, g + 1)
        nc.vector.scalar_tensor_tensor(out=phi_q, in0=e_q, scalar=1.0, in1=r_q, op0=ALU.min, op1=ALU.add
                                       ).then_inc(phiq_ready, 1)
        v.wait_ge(kf_ps, g + 1)
        nc.vector.tensor_scalar(k_act, ps[5], 0.0, None, ALU.max).then_inc(kact_ready, 1)
        v.wait_ge(kact_ready, g * 2 + 1)
        nc.vector.tensor_tensor(k_act, k_act, k_act, ALU.mult).then_inc(kact_ready, 1)
        v.wait_ge(er_ready, g + 1)
        nc.vector.tensor_scalar(sig, e_r, 1.0, None, ALU.add).then_inc(sig_parts, 1)
        v.wait_ge(KV_ps, g + 1)
        for b in range(2):
            nc.vector.tensor_tensor(kvm[:, b * D:(b + 1) * D], ps[0][:, b * 256:b * 256 + D], const("head_block"), ALU.mult)
            last = nc.vector.tensor_scalar(skm[:, b * D:(b + 1) * D], const("head_block"), ps[0][:, b * 256 + D:b * 256 + D + 1],
                                           None, ALU.mult)
        last.then_inc(KV_ready, 1)
        v.wait_ge(sig_parts, g * 2 + 1)
        nc.vector.reciprocal(sig, sig).then_inc(sig_parts, 1)
        v.wait_ge(nd_ps, g + 1)
        nc.vector.reciprocal(rcp, ps[6]).then_inc(rcp_ready, 1)
        v.wait_ge(rcp_ready, g + 1)
        nc.vector.tensor_tensor(yT1, ps[1], rcp, ALU.mult).then_inc(yT1_ready, 1)
        v.wait_ge(vf_ps, g + 1)
        v.wait_ge(sig_parts, g * 2 + 2)
        if late(it):
            v.wait_ge(out_done[p], it * 16)
        nc.vector.tensor_tensor(res[p], ps[2], sig, ALU.mult).then_inc(out_parts, 1)
        v.wait_ge(out_parts, g * 2 + 1)
        nc.vector.tensor_tensor(res[p], res[p], x_sb[:, ds(g * GT, GT), :].rearrange("p a c -> p (a c)"),
                                ALU.add).then_inc(out_parts, 1)
        v.wait_ge(out_parts, g * 2 + 2)
        v.wait_ge(pr_ps, g + 1)
        nc.vector.tensor_tensor(res[p], ps[3], res[p], ALU.add).then_inc(res_ready, 1)

    def front_scalar(act, it, p):
        g = it * 2 + p
        act.wait_ge(xT2_ps, g + 1)
        if late(it):
            act.wait_ge(kv_ps, g - 1)
            act.wait_ge(mixed, g - 1)
        nc.scalar.copy(xT2_of(p)[:, :, 1:T + 1], ps[7].rearrange("p (b t) -> p b t", t=T)).then_inc(xT2_ready, 1)
        act.wait_ge(xT2_ready, g + 1)
        if late(it):
            act.wait_ge(kf_ps, g - 1)
        for m in range(2):
            last = nc.scalar.activation(mix_t[p][m].rearrange("p (b t) -> p b t", t=T), xT2_of(p)[:, :, 1:T + 1],
                                        ACT.Copy, scale=mu[:, m:m + 1])
        last.then_inc(mu_x, 1)

    def back_scalar(act, it, p):
        g = it * 2 + p
        notfirst = late(it) or p
        act.wait_ge(kv_ps, g + 1)
        if notfirst:
            act.wait_ge(phik_ready, g)
            act.wait_ge(KV_ps, g)
        for hf in range(2):
            kk = ps[2 + hf].rearrange("p (n c) -> p n c", c=2 * D)
            nc.scalar.activation(e_k[:, hf * 256:hf * 256 + 256].rearrange("p (n c) -> p n c", c=D), kk[:, :, 0:D], ACT.Exp)
            last = nc.scalar.activation(r_k[:, hf * 256:hf * 256 + 256].rearrange("p (n c) -> p n c", c=D), kk[:, :, 0:D], ACT.Relu)
        last.then_inc(kparts, 1)
        for hf in range(2):
            kk = ps[2 + hf].rearrange("p (n c) -> p n c", c=2 * D)
            last = nc.scalar.copy(v_aug.rearrange("p (n c) -> p n c", c=D + 1)[:, hf * 2:hf * 2 + 2, 0:D], kk[:, :, D:2 * D])
        last.then_inc(v_ready, 1)
        act.wait_ge(q_ps, g + 1)
        if notfirst:
            act.wait_ge(phiq_ready, g)
        nc.scalar.activation(e_q, ps[1], ACT.Exp)
        nc.scalar.activation(r_q, ps[1], ACT.Relu).then_inc(qparts, 1)
        act.wait_ge(r_ps, g + 1)
        if notfirst:
            act.wait_ge(sig_parts, g * 2 - 1)
        nc.scalar.activation(e_r, ps[4], ACT.Exp, scale=-1.0).then_inc(er_ready, 1)

    def front_tensor(pe, it, p):
        g = it * 2 + p
        pe.wait_ge(xn2_ready, g + 1)
        if late(it) or p:
            pe.wait_ge(xT2_ready, g)
        for n in range(GT):
            last = nc.tensor.transpose(ps[7][:, n * P:(n + 1) * P], xn[p][:, n, :], ident)
        last.then_inc(xT2_ps, 1)

    def back_tensor(pe, it, p):
        g = it * 2 + p
        notfirst = late(it) or p
        pe.wait_ge(xT2_ready, g + 1)
        if notfirst:
            pe.wait_ge(res_ready, g)
        for n in range(GT):
            last = nc.tensor.matmul(ps[2 + n // 2][:, (n % 2) * 256:(n % 2) * 256 + 256],
                                    xT2_of(p)[:, n // 2, 1 + (n % 2) * P:1 + (n % 2) * P + P],
                                    wqkv2[:, D:3 * D], start=True, stop=True)
        last.then_inc(kv_ps, 1)
        if notfirst:
            pe.wait_ge(yT1_ready, g)
        nc.tensor.matmul(ps[1], wqkv2[:, 0:D], xT2_of(p)[:, :, 1:T + 1], start=True, stop=True).then_inc(q_ps, 1)
        pe.wait_ge(mixed, g + 1)
        if notfirst:
            pe.wait_ge(er_ready, g)
        for n in range(GT):
            last = nc.tensor.matmul(ps[4][:, n * P:(n + 1) * P], mix_t[p][0][:, n * P:(n + 1) * P], wT[:, 4, :],
                                    start=True, stop=True)
        last.then_inc(r_ps, 1)
        if notfirst:
            pe.wait_ge(kact_ready, g * 2 - 1)
        nc.tensor.matmul(ps[5], wT[:, 5, :], mix_t[p][1], start=True, stop=True).then_inc(kf_ps, 1)
        pe.wait_ge(phik_ready, g + 1)
        pe.wait_ge(v_ready, g + 1)
        if notfirst:
            pe.wait_ge(KV_ready, g)
        for b in range(2):
            for r in range(2):
                n = 2 * b + r
                last = nc.tensor.matmul(ps[0][:, b * 256:b * 256 + D + 1], phi_k[:, n * D:(n + 1) * D],
                                        v_aug[:, n * (D + 1):(n + 1) * (D + 1)], start=(r == 0), stop=(r == 1))
        last.then_inc(KV_ps, 1)
        pe.wait_ge(kact_ready, g * 2 + 2)
        for n in range(GT):
            last = nc.tensor.matmul(ps[2][:, n * P:(n + 1) * P], k_act[:, n * P:(n + 1) * P], wT[:, 6, :],
                                    start=True, stop=True)
        last.then_inc(vf_ps, 1)
        pe.wait_ge(KV_ready, g + 1)
        pe.wait_ge(phiq_ready, g + 1)
        for b in range(2):
            cols = slice(b * T, b * T + T)
            nc.tensor.matmul(ps[1][:, cols], kvm[:, b * D:(b + 1) * D], phi_q[:, cols], start=True, stop=True)
            last = nc.tensor.matmul(ps[6][:, cols], skm[:, b * D:(b + 1) * D], phi_q[:, cols], start=True, stop=True)
        last.then_inc(nd_ps, 1)
        pe.wait_ge(yT1_ready, g + 1)
        for n in range(GT):
            o = ps[3][:, n * P:(n + 1) * P]
            nc.tensor.matmul(o, yT1[:, n * P:(n + 1) * P], wproj[:, :], start=True, stop=False)
            last = nc.tensor.matmul(o, ones_bf[0:3, :], bias3[:, BIASP:BIASP + D], start=False, stop=True)
        last.then_inc(pr_ps, 1)

    def rstd2(pool, it, p):
        g = it * 2 + p
        pool.wait_ge(ln2_mv, g + 1)
        nc.gpsimd.tensor_tensor(ve[p][:, :], mv[p][:, :, 1], eps_ln[:, :], ALU.add).then_inc(ve2_ready, 1)
        pool.wait_ge(ve2_ready, g + 1)
        nc.gpsimd.tensor_tensor(rstd[p][:, :], ve[p][:, :], mhalf[:, :], ALU.pow).then_inc(rstd2_ready, 1)

    NFULL = NT // 2
    SPI = 4
    TAIL = NS - NFULL * SPI

    with nc.Block() as block:
        @block.sync
        def _(sp):
            for lo, n, s in ((0, 2 * GT, x_first), (2 * GT, NT - 2 * GT, x_rest)):
                sp.dma_start(x_sb[:, lo:lo + n, :],
                             x_in.rearrange("b t d -> (b t) d").rearrange("(n p) d -> p n d", p=P)[:, lo:lo + n, :]
                             ).then_inc(s, 16)
            sp.dma_start(w1_sb[:, :, :], W1.rearrange("e f h -> f e h")).then_inc(late_in, 16)
            sp.dma_start(w2_sb[:, :, :], W2.rearrange("e (c p) f -> p (e c) f", p=P)).then_inc(late_in, 16)

            def save(it):
                for p in range(2):
                    g = it * 2 + p
                    sp.wait_ge(xn_ready, g + 1)
                    sp.dma_start(xn_dram.rearrange("(n p) d -> p n d", p=P)[:, ds(g * GT, GT), :], xn[p][:, :, :]
                                 ).then_inc(xn_saved[p], 16)
            save(0)
            with sp.Fori(1, ITS) as it:
                save(it)
            for n in range(NX):
                sp.wait_ge(ye_out[n], 16 * len(range(n, NS, NX)))
            load_y(sp, 0, 0)
            load_y(sp, 0, 1)
            def save_out(it, p):
                g = it * 2 + p
                sp.wait_ge(res_ready, g + 1)
                sp.dma_start(out.rearrange("b t d -> (b t) d").rearrange("(n p) d -> p n d", p=P)[:, ds(g * GT, GT), :],
                             res[p].rearrange("p (n d) -> p n d", n=GT)).then_inc(out_done[p], 16)
            with sp.Fori(1, ITS) as it:
                for p in range(2):
                    load_y(sp, it, p)
                    save_out(it - 1, p)
            for p in range(2):
                save_out(ITS - 1, p)
                sp.wait_ge(out_done[p], 16 * ITS)

        @block.scalar
        def _(act):
            act.dma_start(cst[:, :], consts).then_inc(consts_in, 16)
            for n, w in enumerate((Wq, Wk, Wv, Wo, W_r, W_k, W_v)):
                act.dma_start(w_raw[:, n, :], w).then_inc(wts_in, 16)
            act.dma_start(wg_sb[:, :], Wg).then_inc(wts_in, 16)
            act.dma_start(bias_sp[:, 0:NE * HID // P], b1.rearrange("e h -> (e h)").rearrange("(p c) -> p c", p=P)).then_inc(bias_in, 16)
            act.dma_start(bias_sp[:, NE * HID // P:BIASP // P], b2.rearrange("e h -> (e h)").rearrange("(p c) -> p c", p=P)).then_inc(bias_in, 16)
            act.dma_start(bias_sp[:, BIASP // P:NBIAS // P], b_proj.rearrange("(p c) -> p c", p=P)).then_inc(bias_in, 16)
            act.dma_start(bg_sb[:, :], bg.rearrange("(a e) -> a e", a=1).broadcast_to([P, NE])).then_inc(bias_in, 16)
            act.dma_start(mu[:, 0:1], mu_r.rearrange("(p c) -> p c", p=P)).then_inc(bias_in, 16)
            act.dma_start(mu[:, 1:2], mu_k.rearrange("(p c) -> p c", p=P)).then_inc(bias_in, 16)
            act.dma_start(wqkv2[:, :], w_qkv).then_inc(late_in, 16)
            act.dma_start(wproj[:, :], w_proj).then_inc(late_in, 16)
            act.wait_ge(wT_ps, 1)
            nc.scalar.copy(wT[:, 0:4, :].rearrange("p a b -> p (a b)"), ps[4]).then_inc(wT_ready, 1)
            nc.scalar.copy(wT[:, 4:7, :].rearrange("p a b -> p (a b)"), ps[5][:, 0:3 * P]).then_inc(wT_ready, 1)
            act.wait_ge(bias_split, 5)
            for n in range(3):
                for lo, hi in ((0, BIAS2), (BIAS2, BIASP), (BIASP, NBIAS)):
                    act.dma_start(bias3[n:n + 1, lo:hi].rearrange("a (p c) -> a p c", p=P),
                                  bias_part[:, n, lo // P:hi // P]).then_inc(bias_rows, 16)
            norm1_scalar(act, 0)
            with act.Fori(1, ITS) as it:
                norm1_scalar(act, it)
            act.wait_ge(gate_in, 1)
            nc.scalar.activation(rt[3][:, :, :], rt[3][:, :, :], ACT.Exp).then_inc(gate_exp, 1)
            def phi(it):
                for p in range(2):
                    g = it * 2 + p
                    act.wait_ge(rot_ready, g + 1)
                    nc.scalar.activation(rope_b[p][:, :, :], rope_a[p][:, :, :], ACT.Exp)
                    nc.scalar.activation(rope_a[p][:, :, :], rope_a[p][:, :, :], ACT.Relu).then_inc(phi_parts, 1)
            with act.Fori(0, ITS) as it:
                phi(it)
            for s in range(-3, 0):
                expert_scalar(act, 0, s)

            def body(b, base):
                for s in range(SPI):
                    expert_scalar(act, base, s)
                    if s % 2 and after_first(b * 2 + s // 2):
                        attn_yT(act, b * 2 + s // 2 - 1)
            body(0, 0)
            with act.Fori(1, NFULL) as b:
                body(b, b * SPI)
            attn_yT(act, NT - 1)
            for j in range(NFULL * SPI, NS):
                expert_scalar(act, 0, j)
            act.wait_ge(pads, 3)
            front_scalar(act, 0, 0)
            front_scalar(act, 0, 1)
            back_scalar(act, 0, 0)
            back_scalar(act, 0, 1)
            with act.Fori(1, ITS) as it:
                for p in range(2):
                    front_scalar(act, it, p)
                    back_scalar(act, it, p)

        @block.gpsimd
        def _(pool):
            nc.gpsimd.memset(mhalf[:, :], -0.5).then_inc(pool_const, 1)
            nc.gpsimd.memset(eps_ln[:, :], EPS_LN).then_inc(pool_const, 1)
            pool.wait_ge(pool_const, 2)
            def rs(it):
                for p in range(2):
                    rstd_pool(pool, it * 2 + p, p)
            rs(0)
            with pool.Fori(1, ITS) as it:
                rs(it)
            pool.wait_ge(consts_in, 16)
            def sine(it):
                for p in range(2):
                    g = it * 2 + p
                    pool.wait_ge(qkv_raw, g * GT + GT)
                    if after_first(it):
                        pool.wait_ge(phi_ready, g - 1)
                    for n in range(2):
                        last = nc.gpsimd.tensor_tensor(
                            rope_b[p][:, 2 * n:2 * n + 2, :], qkv3[:, ds(g * GT + 2 * n, 2), 0:2 * D],
                            const("sin").rearrange("p (t c) -> p t c", t=2), ALU.mult)
                    last.then_inc(ropeb_ready, 1)
            sine(0)
            with pool.Fori(1, ITS) as it:
                sine(it)
            pool.wait_ge(idx_ready, 2)
            for p in range(2):
                pool.wait_ge(xn_saved[p], 16 * ITS)
            for j in range(AHEAD):
                gather(pool, j)
            for j in range(NS):
                if j + AHEAD < NS:
                    gather(pool, j + AHEAD)
                scatter(pool, j)
            for p in range(2):
                rstd2(pool, 0, p)
            with pool.Fori(1, ITS) as it:
                for p in range(2):
                    rstd2(pool, it, p)

        @block.tensor
        def _(pe):
            pe.wait_ge(consts_in, 16)
            pe.wait_ge(wts_in, 16 * 8)
            for n in range(7):
                last = nc.tensor.transpose(ps[4 + n // 4][:, (n % 4) * P:(n % 4 + 1) * P], w_raw[:, n, :], ident)
            last.then_inc(wT_ps, 1)
            pe.wait_ge(wT_ready, 2)
            norm1_tensor(pe, 0)
            with pe.Fori(1, ITS) as it:
                norm1_tensor(pe, it)
            pe.wait_ge(rank_in, 1)
            flat = "p a e -> p (a e)"
            pe.wait_ge(lg_ready, NG)
            nc.tensor.matmul(ps[0][:, 0:NT * NE], tri_bf[:, :], m_bf[:, :, :].rearrange(flat), start=True, stop=False)
            nc.tensor.matmul(ps[0][:, 0:NT * NE], ones_bf[:, :], cex_bf[:, :, :].rearrange(flat), start=False, stop=True)
            nc.tensor.matmul(ps[1][:, 0:NE], ones_bf[:, :], cin_bf[:, :], start=True, stop=True).then_inc(rank_ps, 1)
            def table(it, first):
                for p in range(2):
                    g = it * 2 + p
                    pe.wait_ge(hot_ready, g + 1)
                    for n in range(TOPK * GT):
                        k, i = n // GT, n % GT
                        last = nc.tensor.matmul(ps[2][:, 0:2 * NS], hot_lo[p][:, n, :], hot_val[p][:, :, k, i, :],
                                                start=(first and p == 0 and n == 0), stop=False, skip_group_check=True)
                    last.then_inc(tab_ps, 1)
            table(0, True)
            with pe.Fori(1, ITS) as it:
                table(it, False)
            pe.wait_ge(exp_ready, 1)
            pe.wait_ge(late_in, 16 * 4)
            pe.wait_ge(bias_rows, 16 * 9)
            pe.wait_ge(idx_ready, 2)
            e_up, e_dn = pe.alloc_register("expert_up"), pe.alloc_register("expert_down")

            def expert(reg, j):
                pe.reg_load(reg, slot_exp[0:1, ds(j, 1)])
                return pe.snap(reg, min_val=0, max_val=NE - 1)

            def expert_tensor(base, s, last=NS, between=None):
                if 0 <= s + 3 < last:
                    xg_transpose(pe, base, s + 3)
                if 0 <= s + 2 < last:
                    up(pe, base, s + 2, expert(e_up, base + (s + 2)))
                if 0 <= s + 1 < last:
                    hid_transpose(pe, base, s + 1)
                if between:
                    between()
                if s >= 0:
                    down(pe, base, s, expert(e_dn, base + s))

            def body(b, base):
                for s in range(SPI):
                    i = b * 2 + s // 2
                    if s % 2 == 0:
                        expert_tensor(base, s, between=lambda: attn_cumsum(pe, b, s // 2))
                    elif after_first(i):
                        attn_transpose(pe, i - 1)
                        expert_tensor(base, s)
                        attn_project(pe, i - 1)
                    else:
                        expert_tensor(base, s)
            for s in range(-3, 0):
                expert_tensor(0, s)
            body(0, 0)
            with pe.Fori(1, NFULL) as b:
                body(b, b * SPI)
            attn_transpose(pe, NT - 1)
            attn_project(pe, NT - 1)
            for j in range(NFULL * SPI, NS):
                expert_tensor(0, j)
            pe.wait_ge(pads, 3)
            front_tensor(pe, 0, 0)
            front_tensor(pe, 0, 1)
            back_tensor(pe, 0, 0)
            back_tensor(pe, 0, 1)
            with pe.Fori(1, ITS) as it:
                for p in range(2):
                    front_tensor(pe, it, p)
                    back_tensor(pe, it, p)

        @block.vector
        def _(v):
            TT, TS, RED = nc.vector.tensor_tensor, nc.vector.tensor_scalar, nc.vector.tensor_reduce
            v.wait_ge(consts_in, 16)
            nc.vector.tensor_copy(ones_bf[:, :], const("ones"))
            nc.vector.tensor_copy(tri_bf[:, :], const("tri_excl"))
            nc.vector.tensor_copy(iota_bf[:, :], const("iota")).then_inc(small_ready, 1)
            v.wait_ge(bias_in, 16 * 6)
            TS(one_mu[:, :], mu[:, :], -1.0, 1.0, ALU.mult, ALU.add)
            nc.vector.tensor_copy(bias_part[:, 0, :], bias_sp[:, :]).then_inc(bias_split, 1)
            v.wait_ge(bias_split, 1)
            TT(bias_rest[:, 0, :], bias_sp[:, :], bias_part[:, 0, :], ALU.subtract).then_inc(bias_split, 1)
            v.wait_ge(bias_split, 2)
            nc.vector.tensor_copy(bias_part[:, 1, :], bias_rest[:, 0, :]).then_inc(bias_split, 1)
            v.wait_ge(bias_split, 3)
            TT(bias_rest[:, 1, :], bias_rest[:, 0, :], bias_part[:, 1, :], ALU.subtract).then_inc(bias_split, 1)
            v.wait_ge(bias_split, 4)
            nc.vector.tensor_copy(bias_part[:, 2, :], bias_rest[:, 1, :]).then_inc(bias_split, 1)

            v.wait_ge(x_first, 16)
            norm1_vector(v, 0)
            v.wait_ge(x_rest, 16)
            with v.Fori(1, ITS) as it:
                norm1_vector(v, it)

            n_route = [0]

            def done(ins):
                n_route[0] += 1
                ins.then_inc(route, 1)
                v.wait_ge(route, n_route[0])

            def per_tile(a):
                return a.unsqueeze(2).broadcast_to([P, NT, NE])

            def per_expert(a):
                return a.unsqueeze(1).broadcast_to([P, NT, NE])

            def row(n):
                return r32[:, n, :]

            A3 = [r[:, :, :] for r in rt]
            logits = lgb[:, :, :]
            v.wait_ge(lg_ready, NG)
            done(TT(logits, lg[:, :, :], per_expert(bg_sb[:, :]), ALU.add))
            cur = logits
            for k in range(TOPK):
                done(RED(row(k), cur, AX.X, ALU.max))
                done(TT(A3[0], cur, per_tile(row(k)), ALU.is_equal))
                done(TT(A3[0], A3[0], per_expert(const("first")), ALU.mult))
                done(RED(row(2), A3[0], AX.X, ALU.max))
                done(TT(oh[k][:, :, :], per_expert(const("first")), per_tile(row(2)), ALU.is_equal))
                if k == 0:
                    TT(A3[3], logits, per_tile(row(0)), ALU.subtract).then_inc(gate_in, 1)
                    done(nc.vector.scalar_tensor_tensor(out=A3[1], in0=oh[0][:, :, :], scalar=-BIG, in1=logits,
                                                        op0=ALU.mult, op1=ALU.add))
                    cur = A3[1]
            done(TT(A3[0], oh[0][:, :, :], oh[1][:, :, :], ALU.add))
            nc.vector.tensor_copy(m_bf[:, :, :], A3[0])
            a, b_, sh = 0, 1, 1
            while sh < NT:
                nc.vector.tensor_copy(rt[b_][:, 0:sh, :], rt[a][:, 0:sh, :])
                done(TT(rt[b_][:, sh:, :], rt[a][:, sh:, :], rt[a][:, 0:NT - sh, :], ALU.add))
                a, b_, sh = b_, a, sh * 2
            TT(cex_bf[:, :, :], rt[a][:, :, :], m_bf[:, :, :], ALU.subtract)
            nc.vector.tensor_copy(cin_bf[:, :], rt[a][:, NT - 1, :]).then_inc(rank_in, 1)
            v.wait_ge(rank_ps, 1)
            done(TS(e8[:, 0, :], ps[1][:, 0:NE], float(P - 1), None, ALU.add))
            done(nc.vector.tensor_copy(e8i[:, 0, :], e8[:, 0, :]))
            done(TS(e8i[:, 1, :], e8i[:, 0, :], 7, None, ALU.logical_shift_right))
            done(nc.vector.tensor_copy(e8[:, 1, :], e8i[:, 1, :]))
            a_, b2_ = 1, 2
            for sh in (1, 2, 4):
                nc.vector.tensor_copy(e8[:, b2_, 0:sh], e8[:, a_, 0:sh])
                done(TT(e8[:, b2_, sh:], e8[:, a_, sh:], e8[:, a_, 0:NE - sh], ALU.add))
                a_, b2_ = b2_, b2_ + 1
            ends = e8[:, a_, :]
            done(TT(e8[:, 6, :], ends, e8[:, 1, :], ALU.subtract))
            done(TS(e8[:, 7, :], e8[:, 6, :], float(P), None, ALU.mult))
            done(TT(A3[0], ps[0][:, 0:NT * NE].rearrange("p (a e) -> p a e", e=NE), per_expert(e8[:, 7, :]), ALU.add))
            TT(A3[1], A3[0], oh[0][:, :, :], ALU.mult)
            done(TT(A3[2], A3[0], oh[1][:, :, :], ALU.mult))
            RED(row(3), A3[1], AX.X, ALU.add)
            done(RED(row(4), A3[2], AX.X, ALU.add))
            done(nc.vector.tensor_copy(posi[:, 0, :, :], r32[:, 3:5, :]))
            TS(posi[:, 1, :, :], posi[:, 0, :, :], 7, None, ALU.logical_shift_right)
            done(TS(posi[:, 2, :, :], posi[:, 0, :, :], P - 1, None, ALU.bitwise_and))
            nc.vector.tensor_copy(pos_hi[:, :, :], posi[:, 1, :, :])
            done(nc.vector.tensor_copy(pos_lo[:, :, :], posi[:, 2, :, :]))

            def onehots(it):
                for p in range(2):
                    g = it * 2 + p
                    if after_first(it):
                        v.wait_ge(tab_ps, g - 1)
                    for n in range(TOPK * GT):
                        k, i = n // GT, n % GT
                        TS(hot_lo[p][:, n, :], iota_bf[:, :], pos_lo[:, k, ds(g * GT + i, 1)], None, ALU.is_equal)
                    for k in range(TOPK):
                        last = TT(hot_hi[p][:, k, :, :], iota_bf[:, 0:NS].unsqueeze(1).broadcast_to([P, GT, NS]),
                                  pos_hi[:, k, ds(g * GT, GT)].unsqueeze(2).broadcast_to([P, GT, NS]), ALU.is_equal)
                    last.then_inc(hot_half, 1)
                    v.wait_ge(hot_half, g + 1)
                    for k in range(TOPK):
                        TT(hot_val[p][:, 0, k, :, :], hot_hi[p][:, k, :, :],
                           const("tile_no")[:, ds(g * GT, GT)].unsqueeze(2).broadcast_to([P, GT, NS]), ALU.mult)
                        last = TS(hot_val[p][:, 1, k, :, :], hot_hi[p][:, k, :, :], const("pair_no")[:, k:k + 1], None, ALU.mult)
                    last.then_inc(hot_ready, 1)
            onehots(0)
            with v.Fori(1, ITS) as it:
                onehots(it)
            done(TT(cmp8[:, :, :], const("iota")[:, 0:NS].unsqueeze(2).broadcast_to([P, NS, NE]),
                    ends.unsqueeze(1).broadcast_to([P, NS, NE]), ALU.is_ge))
            done(RED(tab[:, 0, :], cmp8[:, :, :], AX.X, ALU.add))
            done(TS(tab[:, 0, :], tab[:, 0, :], float(NE - 1), None, ALU.min))
            nc.vector.tensor_copy(slot_exp[:, :], tab[:, 0, :]).then_inc(exp_ready, 1)
            v.wait_ge(tab_ps, NG)
            done(TS(tab[:, 1, :], ps[2][:, 0:NS], float(2 * P), -float(2 * P), ALU.mult, ALU.add))
            TS(tab[:, 3, :], ps[2][:, 0:NS], 0.0, None, ALU.is_equal)
            done(TT(tab[:, 2, :], ps[2][:, NS:2 * NS], tab[:, 1, :], ALU.add))
            done(TT(tab[:, 3, :], tab[:, 3, :], const("slot_row"), ALU.mult))
            done(TT(tab[:, 3, :], tab[:, 3, :], tab[:, 2, :], ALU.add))
            nc.vector.tensor_copy(slot_dst[:, :], tab[:, 3, :]).then_inc(idx_ready, 1)
            done(TS(tab[:, 2, :], tab[:, 2, :], 0.0, None, ALU.max))
            done(nc.vector.tensor_copy(tabi[:, :], tab[:, 2, :]))
            TS(slot_tok[:, :], tabi[:, :], 1, None, ALU.logical_shift_right).then_inc(idx_ready, 1)
            v.wait_ge(gate_exp, 1)
            RED(row(5), A3[3], AX.X, ALU.add)
            TT(A3[1], A3[3], oh[0][:, :, :], ALU.mult)
            done(TT(A3[2], A3[3], oh[1][:, :, :], ALU.mult))
            RED(row(6), A3[1], AX.X, ALU.add)
            RED(row(7), A3[2], AX.X, ALU.add)
            done(nc.vector.reciprocal(row(8), row(5)))
            TT(row(6), row(6), row(8), ALU.mult)
            done(TT(row(7), row(7), row(8), ALU.mult))
            done(nc.vector.scalar_tensor_tensor(out=row(9), in0=row(6), scalar=EPS_GATE, in1=row(7), op0=ALU.add, op1=ALU.add))
            done(nc.vector.reciprocal(row(10), row(9)))
            TT(sel[0][:, :], row(6), row(10), ALU.mult)
            done(TT(sel[1][:, :], row(7), row(10), ALU.mult))

            def rotary(it):
                for p in range(2):
                    g = it * 2 + p
                    if after_first(it):
                        v.wait_ge(phi_ready, g - 1)
                    for n in range(2):
                        last = TT(rope_a[p][:, 2 * n:2 * n + 2, :], qkv3[:, ds(g * GT + 2 * n, 2), 0:2 * D],
                                  const("cos").rearrange("p (t c) -> p t c", t=2), ALU.mult)
                    last.then_inc(ropea_ready, 1)
                    v.wait_ge(ropea_ready, g + 1)
                    v.wait_ge(ropeb_ready, g + 1)
                    a4 = rope_a[p][:, :, :].rearrange("p n (c f w) -> p (n c) f w", f=2, w=DH // 2)
                    b4 = rope_b[p][:, :, :].rearrange("p n (c f w) -> p (n c) f w", f=2, w=DH // 2)
                    for f in range(2):
                        last = TT(a4[:, :, f, :], a4[:, :, f, :], b4[:, :, 1 - f, :], ALU.add)
                    last.then_inc(rot_ready, 1)
                for p in range(2):
                    g = it * 2 + p
                    v.wait_ge(phi_parts, g + 1)
                    for n in range(2):
                        last = nc.vector.scalar_tensor_tensor(
                            out=qkv3[:, ds(g * GT + 2 * n, 2), 0:2 * D], in0=rope_b[p][:, 2 * n:2 * n + 2, :], scalar=1.0,
                            in1=rope_a[p][:, 2 * n:2 * n + 2, :], op0=ALU.min, op1=ALU.add)
                    last.then_inc(phi_ready, 1)
            v.wait_ge(qkv_raw, NT)
            rotary(0)
            with v.Fori(1, ITS) as it:
                rotary(it)
            v.wait_ge(phi_ready, NG)

            def tile(b, r, last=False):
                i = b * 2 + r
                attn_apply(v, b, r)
                if not last:
                    attn_outer(v, b + r, 1 - r)
                attn_divide(v, i)
                if after_first(i):
                    attn_add(v, i - 1)
            attn_outer(v, 0, 0)
            for r in range(2):
                tile(0, r)
            with v.Fori(1, NFULL - 1) as b:
                for r in range(2):
                    tile(b, r)
            tile(NFULL - 1, 0)
            tile(NFULL - 1, 1, last=True)
            attn_add(v, NT - 1)

            v.wait_ge(x_attn, NT)
            v.wait_ge(o_ps, NT)
            for p in range(2):
                nc.vector.memset(xT2_of(p)[:, :, 0:1], 0.0).then_inc(pads, 1)
            nc.vector.memset(v_aug.rearrange("p (n c) -> p n c", c=D + 1)[:, :, D:D + 1], 1.0).then_inc(pads, 1)
            for p in range(2):
                front_vector(v, 0, p)
            for p in range(2):
                norm2_vector(v, 0, p)
            for p in range(2):
                mix_vector(v, 0, p)
            for p in range(2):
                back_vector(v, 0, p)
            with v.Fori(1, ITS) as it:
                for p in range(2):
                    front_vector(v, it, p)
                    norm2_vector(v, it, p)
                    mix_vector(v, it, p)
                    back_vector(v, it, p)

    return st


_INS = ['L0_attn_x', 'L0_attn_Wq', 'L0_attn_Wk', 'L0_attn_Wv', 'L0_attn_Wo', 'L0_ffn_Wg', 'L0_ffn_bg', 'L0_ffn_W1',
        'L0_ffn_b1', 'L0_ffn_W2', 'L0_ffn_b2', 'L1_attn_w_qkv', 'L1_attn_w_proj', 'L1_attn_b_proj', 'L1_ffn_W_r',
        'L1_ffn_W_k', 'L1_ffn_W_v', 'L1_ffn_mu_r', 'L1_ffn_mu_k']


def kernel(**inputs):
    import concourse.bacc as _bacc
    from concourse.bass_utils import run_bass_kernel_spmd as _run

    nc = _bacc.Bacc("TRN2", target_bir_lowering=False, num_devices=1)
    arrays, args = {}, []
    for name in _INS:
        a = np.ascontiguousarray(inputs[name])
        arrays[f"in_{name}"] = a
        args.append(nc.dram_tensor(f"in_{name}", a.shape, mybir.dt.from_np(a.dtype), kind="ExternalInput").ap())
    arrays["in_consts"] = constant_table()
    args.append(nc.dram_tensor("in_consts", (P, NCONST), mybir.dt.float32, kind="ExternalInput").ap())
    out = nc.dram_tensor("out_0", (B, T, D), mybir.dt.float32, kind="ExternalOutput").ap()
    build(nc, *args, out)
    r = _run(nc, [arrays], core_ids=[0])
    return r.results[0]["out_0"]
```

```python
from contextlib import ExitStack

import numpy as np
import concourse.bass as bass
from concourse import mybir

P = 128
D = 128
H, DH = 16, 8
B, T = 16, 256
TOK = B * T
NT = TOK // P
GT = 4
NG = NT // GT
NE, HID, TOPK = 8, 512, 2
NC = HID // P
NS = TOK * TOPK // P + NE - 1
EPS_LN, EPS_DEN, EPS_GATE = 1e-5, 1e-6, 1e-8
BIG = 3.0e38
BIASP, NBIAS = NE * D, NE * D + D

CONSTS = {}
_at = 0
for _name, _n in (("ident", P), ("tri_incl", P), ("tri_excl", P), ("ones", P), ("head_mask", P + H),
                  ("iota", P), ("cos", 2 * DH), ("sin", 2 * DH), ("first", NE), ("tile_no", NT),
                  ("pair_no", TOPK), ("slot_row", NS)):
    CONSTS[_name] = (_at, _at + _n)
    _at += _n
NCONST = _at


def constant_table():
    c = np.zeros((P, NCONST), np.float32)
    row, col = np.arange(P)[:, None], np.arange(P)[None, :]

    def put(name, a):
        lo, hi = CONSTS[name]
        c[:, lo:hi] = a

    put("ident", row == col)
    put("tri_incl", row <= col)
    put("tri_excl", row < col)
    put("ones", 1.0)
    put("head_mask", np.concatenate([row // DH == col // DH, row // DH == np.arange(H)[None, :]], 1))
    put("iota", col + 0 * row)
    half = DH // 2
    inv = np.float32(10000.0) ** (-np.arange(half, dtype=np.float32) / np.float32(half))
    ang = (np.arange(T, dtype=np.float32)[:, None] * inv[None, :].astype(np.float32)).astype(np.float32)
    cos, sin = np.cos(ang), np.sin(ang)
    for name, a in (("cos", np.concatenate([cos, cos], 1)), ("sin", np.concatenate([sin, -sin], 1))):
        put(name, a.reshape(2, P, DH).transpose(1, 0, 2).reshape(P, -1))
    put("first", NE - np.arange(NE))
    put("tile_no", 1 + np.arange(NT))
    put("pair_no", 2 * row + np.arange(TOPK))
    put("slot_row", TOK * TOPK + 256 + row + P * np.arange(NS))
    return c


def build(nc, x_in, Wq, Wk, Wv, Wo, Wg, bg, W1, b1, W2, b2, w_qkv, w_proj, b_proj, W_r, W_k, W_v,
          mu_r, mu_k, consts, out):
    f32, bf16, i32 = mybir.dt.float32, mybir.dt.bfloat16, mybir.dt.int32
    ALU, ACT, AX = mybir.AluOpType, mybir.ActivationFunctionType, mybir.AxisListType
    ds = bass.ds
    st = ExitStack()

    def sbuf(name, shape, dt=f32):
        return st.enter_context(nc.sbuf_tensor(name, shape, dt))

    def sem(name):
        return st.enter_context(nc.semaphore(name))

    xn_dram = nc.dram_tensor("xn_rows", (TOK, D), f32, kind="Internal").ap()
    y_dram = nc.dram_tensor("expert_rows", (TOK * TOPK + NS * P, D), f32, kind="Internal").ap()

    cst = sbuf("cst", [P, NCONST])

    def const(name):
        lo, hi = CONSTS[name]
        return cst[:, lo:hi]

    ident = const("ident")
    x_sb = sbuf("x_sb", [P, NT, D])
    xn = [sbuf(f"xn{p}", [P, GT, D]) for p in range(2)]
    xT = [sbuf(f"xT{p}", [P, GT, P]) for p in range(2)]
    NQ = 3 * D + NE
    qkv = sbuf("qkv", [P, NT * NQ])
    qkv3 = qkv[:, :].rearrange("p (n c) -> p n c", c=NQ)
    qk_exp = sbuf("qk_exp", [P, NT, 2 * D])
    NX = 4
    w1 = [sbuf(f"w1_{n}", [P, HID]) for n in range(NX)]
    b1T = sbuf("b1T", [P, NE * NC])
    w2_sb = sbuf("w2_sb", [P, NE * NC, D])
    w_raw = qk_exp[:, 0:4, :].rearrange("p a (b c) -> p (a b) c", c=P)
    wT = sbuf("wT", [P, 7, P])
    w_in = sbuf("w_in", [P, NQ])
    wqkv2 = sbuf("wqkv2", [P, 3 * D])
    wproj = sbuf("wproj", [P, D])
    mu = sbuf("mu", [P, 2])
    one_mu = sbuf("one_mu", [P, 2])
    bg_sb = sbuf("bg_sb", [P, NE])
    bias_sp = sbuf("bias_sp", [P, NBIAS // P])
    bias_rest = sbuf("bias_rest", [P, 2, NBIAS // P])
    bias_part = sbuf("bias_part", [P, 3, NBIAS // P], bf16)
    bias3 = sbuf("bias3", [3, NBIAS], bf16)
    ones_bf = sbuf("ones_bf", [P, P], bf16)
    tri_bf = sbuf("tri_bf", [P, P], bf16)
    iota_bf = sbuf("iota_bf", [P, P], bf16)
    stats = [sbuf(f"stats{p}", [P, GT, 6]) for p in range(2)]
    mv = [sbuf(f"mv{p}", [P, GT, 2]) for p in range(2)]
    ve = [sbuf(f"ve{p}", [P, GT]) for p in range(2)]
    rstd = [sbuf(f"rstd{p}", [P, GT]) for p in range(2)]
    mhalf = sbuf("mhalf", [P, GT])
    eps_ln = sbuf("eps_ln", [P, GT])
    scrap = sbuf("scrap", [1, 1])
    r32 = sbuf("r32", [P, 12, NT])
    sel = [sbuf(f"sel{n}", [P, NT]) for n in range(TOPK)]
    m_bf = sbuf("m_bf", [P, NT, NE], bf16)
    cex_bf = sbuf("cex_bf", [P, NT, NE], bf16)
    cin_bf = sbuf("cin_bf", [P, NE], bf16)
    e8 = sbuf("e8", [P, 8, NE])
    e8i = sbuf("e8i", [P, 2, NE], i32)
    posi = sbuf("posi", [P, 3, TOPK, NT], i32)
    pos_lo = sbuf("pos_lo", [P, TOPK, NT])
    pos_hi = sbuf("pos_hi", [P, TOPK, NT])
    hot_lo = [sbuf(f"hot_lo{p}", [P, TOPK * GT, P], bf16) for p in range(2)]
    hot_hi = [sbuf(f"hot_hi{p}", [P, TOPK, GT, NS], bf16) for p in range(2)]
    hot_val = [sbuf(f"hot_val{p}", [P, 2, TOPK, GT, NS], bf16) for p in range(2)]
    tab = sbuf("tab", [P, 4, NS])
    tabi = sbuf("tabi", [P, NS], i32)
    slot_exp = sbuf("slot_exp", [P, NS], i32)
    slot_tok = sbuf("slot_tok", [P, NS], i32)
    slot_dst = sbuf("slot_dst", [P, NS], i32)
    AHEAD = 6
    xg = [sbuf(f"xg{n}", [P, D]) for n in range(NX)]
    ye = [sbuf(f"ye{n}", [P, D]) for n in range(NX)]
    xgT = [sbuf(f"xgT{n}", [P, P]) for n in range(2)]
    hidT = [sbuf(f"hidT{n}", [P, NC, P]) for n in range(2)]
    outer = [sbuf(f"outer{r}", [P, H * DH * DH])[:, :] for r in range(2)]
    cq = sbuf("cq", [P, H * DH * DH])[:, :]
    spare = [b[:, n * NT * NE:(n + 1) * NT * NE].rearrange("p (a e) -> p a e", e=NE)
             for b in (outer[1], cq) for n in range(4)]
    rt, oh, lgb = spare[0:4], spare[4:6], spare[6]
    cmp8 = outer[0][:, 0:NS * NE].rearrange("p (s e) -> p s e", e=NE)
    att = sbuf("att", [P, 5, D])
    cqk, num, y_tok, yT0, o_tok = (att[:, n, :] for n in range(5))
    dens = sbuf("dens", [P, 2, H])
    den, rden = dens[:, 0, :], dens[:, 1, :]

    ps_all = st.enter_context(nc.psum_tensor("banks", [P, 8 * 512], f32))
    ps = [ps_all[:, n * 512:(n + 1) * 512] for n in range(8)]

    consts_in, wts_in, late_in = sem("consts_in"), sem("wts_in"), sem("late_in")
    x_first, x_rest = sem("x_first"), sem("x_rest")
    wT_ps, wT_ready = sem("wT_ps"), sem("wT_ready")
    bias_in, bias_split, bias_rows = sem("bias_in"), sem("bias_split"), sem("bias_rows")
    small_ready, pool_const = sem("small_ready"), sem("pool_const")
    ln_stats, ln_mv, ve_ready, rstd_ready = sem("ln_stats"), sem("ln_mv"), sem("ve_ready"), sem("rstd_ready")
    xn_ready, xT_ps, xT_ready = sem("xn_ready"), sem("xT_ps"), sem("xT_ready")
    xn_saved = [sem("xn_saved0"), sem("xn_saved1")]
    qkv_ps, qkv_raw = sem("qkv_ps"), sem("qkv_raw")
    route, gate_in, gate_exp = sem("route"), sem("gate_in"), sem("gate_exp")
    rank_in, rank_ps = sem("rank_in"), sem("rank_ps")
    hot_rows, hot_tile, hot_by_tile, hot_by_row, tab_ps, exp_ready, idx_ready = sem("hot_rows"), sem("hot_tile"), sem("hot_by_tile"), sem("hot_by_row"), sem("tab_ps"), sem("exp_ready"), sem("idx_ready")
    sine_ready, cosine_ready, rot_ready, exp_part, phi_parts, phi_ready = (
        sem("sine_ready"), sem("cosine_ready"), sem("rot_ready"), sem("exp_part"), sem("phi_parts"), sem("phi_ready"))
    xg_in = [sem(f"xg_in{n}") for n in range(NX)]
    w1_in = [sem(f"w1_in{n}") for n in range(NX)]
    xgT_ps, xgT_ready, up_ps, gelu_ready = sem("xgT_ps"), sem("xgT_ready"), sem("up_ps"), sem("gelu_ready")
    down_ps, ye_ready = sem("down_ps"), sem("ye_ready")
    ye_out = [sem(f"ye_out{n}") for n in range(NX)]
    outer_ready, cum_ps, cq_ready, num_ready, y_ready = (
        sem("outer_ready"), sem("cum_ps"), sem("cq_ready"), sem("num_ready"), sem("y_ready"))
    den_ready, rden_ready, yT_ps, yT_ready, o_ps, o_ready, x_attn = (
        sem("den_ready"), sem("rden_ready"), sem("yT_ps"), sem("yT_ready"), sem("o_ps"), sem("o_ready"), sem("x_attn"))

    ITS = NG // 2

    def from_(g, n):
        return not isinstance(g, int) or g >= n

    def till(g, n):
        return not isinstance(g, int) or g <= n

    def after_first(it):
        return not (isinstance(it, int) and it == 0)

    def wait_alone(v, s, value):
        v.wait_ge(s, value)
        nc.vector.memset(scrap[:, :], 0.0)

    def stats1_vector(v, g, p):
        for k in range(GT):
            last = nc.vector.bn_stats(stats[p][:, k, :], x_sb[:, ds(g * GT + k, 1), :])
        last.then_inc(ln_stats, 1)
        wait_alone(v, ln_stats, g + 1)
        for k in range(GT):
            last = nc.vector.bn_aggr(mv[p][:, k, :], stats[p][:, k, :])
        last.then_inc(ln_mv, 1)

    def norm1_vector(v, g, p):
        v.wait_ge(rstd_ready, g + 1)
        if not (isinstance(g, int) and g < 2):
            v.wait_ge(xT_ps, g - 1)
            v.wait_ge(xn_saved[p], (g // 2) * 16)
        for k in range(GT):
            last = nc.vector.tensor_scalar(xn[p][:, k, :], x_sb[:, ds(g * GT + k, 1), :].rearrange("p a d -> p (a d)"),
                                           mv[p][:, k, 0:1], rstd[p][:, k:k + 1], ALU.subtract, ALU.mult)
        last.then_inc(xn_ready, 1)

    def rstd_pool(pool, g, p):
        pool.wait_ge(ln_mv, g + 1)
        nc.gpsimd.tensor_tensor(ve[p][:, :], mv[p][:, :, 1], eps_ln[:, :], ALU.add).then_inc(ve_ready, 1)
        pool.wait_ge(ve_ready, g + 1)
        nc.gpsimd.tensor_tensor(rstd[p][:, :], ve[p][:, :], mhalf[:, :], ALU.pow).then_inc(rstd_ready, 1)

    def xT_tensor(pe, g, p):
        pe.wait_ge(xn_ready, g + 1)
        if not (isinstance(g, int) and g < 2):
            pe.wait_ge(xT_ready, g - 1)
        for k in range(GT):
            last = nc.tensor.transpose(ps[p][:, k * P:(k + 1) * P], xn[p][:, k, :], ident)
        last.then_inc(xT_ps, 1)

    def project1_tensor(pe, g, p):
        pe.wait_ge(xT_ready, g + 1)
        for k in range(GT):
            if not (isinstance(g, int) and g < 1):
                pe.wait_ge(qkv_raw, g * GT + k - (GT - 1))
            nc.tensor.matmul(ps[4 + k][:, 0:NQ], xT[p][:, k, :], w_in[:, :], start=True, stop=True
                             ).then_inc(qkv_ps, 1)

    def xT_scalar(act, g, p):
        act.wait_ge(xT_ps, g + 1)
        if not (isinstance(g, int) and g < 2):
            act.wait_ge(qkv_ps, (g - 1) * GT)
        nc.scalar.copy(xT[p][:, :, :].rearrange("p a b -> p (a b)"), ps[p]).then_inc(xT_ready, 1)

    def project1_scalar(act, g, p):
        for k in range(GT):
            act.wait_ge(qkv_ps, g * GT + k + 1)
            nc.scalar.copy(qkv3[:, ds(g * GT + k, 1), :].rearrange("p a c -> p (a c)"),
                           ps[4 + k][:, 0:NQ]).then_inc(qkv_raw, 1)

    def batches_of(a, g):
        for b in range(GT // 2):
            yield a[:, ds(g * GT + 2 * b, 2), 0:2 * D].rearrange("p t (h d) -> p t h d", d=DH)

    def by_position(name):
        return const(name).rearrange("p (t d) -> p t d", d=DH).unsqueeze(2).broadcast_to([P, 2, 2 * H, DH])

    def sine(pool, g):
        pool.wait_ge(qkv_raw, g * GT + GT)
        for q, e in zip(batches_of(qkv3, g), batches_of(qk_exp, g)):
            last = nc.gpsimd.tensor_tensor(e, q, by_position("sin"), ALU.mult)
        last.then_inc(sine_ready, 1)

    def rotate(eng, multiply_add, g):
        eng.wait_ge(sine_ready, g + 1)
        for q in batches_of(qkv3, g):
            last = multiply_add(q, q, by_position("cos"), ALU.mult)
        last.then_inc(cosine_ready, 1)
        eng.wait_ge(cosine_ready, g + 1)
        half = DH // 2
        q = qkv3[:, ds(g * GT, GT), 0:2 * D].rearrange("p t (h d) -> p t h d", d=DH)
        e = qk_exp[:, ds(g * GT, GT), :].rearrange("p t (h d) -> p t h d", d=DH)
        for f in range(2):
            a = q[:, :, :, f * half:(f + 1) * half]
            last = multiply_add(a, a, e[:, :, :, (1 - f) * half:(2 - f) * half], ALU.add)
        last.then_inc(rot_ready, 1)

    def exp_relu(act, g):
        act.wait_ge(rot_ready, g + 1)
        q, e = qkv3[:, ds(g * GT, GT), 0:2 * D], qk_exp[:, ds(g * GT, GT), :]
        nc.scalar.activation(e, q, ACT.Exp).then_inc(exp_part, 1)
        act.wait_ge(exp_part, g + 1)
        nc.scalar.activation(q, q, ACT.Relu).then_inc(phi_parts, 1)

    SINE_LAG, LAG = 3, 4
    BY_VECTOR = NG + 1 - LAG

    def front(eng, step):
        for x in range(4):
            step(eng, x, x % 2)
        with eng.Fori(2, ITS) as it:
            for p in range(2):
                step(eng, it * 2 + p, p)
        step(eng, NG, 0)

    def before_end(x):
        return not isinstance(x, int) or x < NG

    def front_tensor(pe, x, p):
        if before_end(x):
            xT_tensor(pe, x, p)
        if from_(x, 1):
            project1_tensor(pe, x - 1, 1 - p)

    def front_scalar(act, x, p):
        if before_end(x):
            xT_scalar(act, x, p)
        if from_(x, 1):
            project1_scalar(act, x - 1, 1 - p)

    def front_vector(v, x, p):
        if isinstance(x, int) and x == 2:
            v.wait_ge(x_rest, 16)
        if before_end(x):
            stats1_vector(v, x, p)
        if from_(x, 1):
            norm1_vector(v, x - 1, 1 - p)
        if from_(x, LAG):
            rotate(v, nc.vector.tensor_tensor, x - LAG)

    def front_pool(pool, x, p):
        if from_(x, SINE_LAG):
            sine(pool, x - SINE_LAG)
        if before_end(x):
            rstd_pool(pool, x, p)

    def gather(pool, j):
        n = j % NX
        if j >= NX:
            pool.wait_ge(xgT_ps, j - NX + 1)
        pool.indirect_dma_start(out=xg[n][:, :], out_offset=None, in_=xn_dram,
                                in_offset=bass.IndirectOffsetOnAxis(ap=slot_tok[:, j:j + 1], axis=0)
                                ).then_inc(xg_in[n], 16)

    def scatter(pool, j):
        n = j % NX
        pool.wait_ge(ye_ready, j + 1)
        pool.indirect_dma_start(out=y_dram, out_offset=bass.IndirectOffsetOnAxis(ap=slot_dst[:, j:j + 1], axis=0),
                                in_=ye[n][:, :], in_offset=None).then_inc(ye_out[n], 16)

    def slot(base, s):
        return base + s

    def load_w1(sp, base, s, e):
        j, n = slot(base, s), s % NX
        if from_(j, NX):
            sp.wait_ge(up_ps, j - NX + 1)
        sp.dma_start(w1[n][:, :], W1[ds(e, 1), :, :].rearrange("a f h -> f (a h)")).then_inc(w1_in[n], 16)

    def xg_transpose(pe, base, s):
        j, n = slot(base, s), s % NX
        pe.wait_ge(xg_in[n], (base // NX + s // NX + 1) * 16)
        if from_(j, 1):
            pe.wait_ge(xgT_ready, j)
        nc.tensor.transpose(ps[6][:, 0:P], xg[n][:, :], ident).then_inc(xgT_ps, 1)

    def up(pe, base, s):
        j, p, n = slot(base, s), s % 2, s % NX
        pe.wait_ge(w1_in[n], (base // NX + s // NX + 1) * 16)
        pe.wait_ge(xgT_ready, j + 1)
        if from_(j, 2):
            pe.wait_ge(gelu_ready, j - 1)
        for c in range(NC):
            last = nc.tensor.matmul(ps[3 + p][:, c * P:(c + 1) * P], w1[n][:, c * P:(c + 1) * P], xgT[p][:, :],
                                    start=True, stop=True)
        last.then_inc(up_ps, 1)

    def down(pe, base, s, e):
        j, p = slot(base, s), s % 2
        pe.wait_ge(gelu_ready, j + 1)
        if from_(j, 1):
            pe.wait_ge(ye_ready, j)
        y = ps[7][:, 0:D]
        nc.tensor.matmul(y, ones_bf[0:3, :], bias3[:, ds(e * D, D)], start=True, stop=False)
        for c in range(NC):
            last = nc.tensor.matmul(y, hidT[p][:, c, :], w2_sb[:, ds(e * NC + c, 1), :],
                                    start=False, stop=(c == NC - 1))
        last.then_inc(down_ps, 1)

    def xgT_copy(act, base, s):
        j, p = slot(base, s), s % 2
        act.wait_ge(xgT_ps, j + 1)
        if from_(j, 2):
            act.wait_ge(up_ps, j - 1)
        nc.scalar.copy(xgT[p][:, :], ps[6][:, 0:P]).then_inc(xgT_ready, 1)

    def gelu(act, base, s, e):
        j, p = slot(base, s), s % 2
        act.wait_ge(up_ps, j + 1)
        if from_(j, 2):
            act.wait_ge(down_ps, j - 1)
        for c in range(NC):
            last = nc.scalar.activation(hidT[p][:, c, :], ps[3 + p][:, c * P:(c + 1) * P], ACT.Gelu_apprx_tanh,
                                        bias=b1T[:, ds(e * NC + c, 1)])
        last.then_inc(gelu_ready, 1)

    def out_copy(act, base, s):
        j, n = slot(base, s), s % NX
        act.wait_ge(down_ps, j + 1)
        if from_(j, NX):
            act.wait_ge(ye_out[n], (base // NX + s // NX) * 16)
        nc.scalar.copy(ye[n][:, :], ps[7][:, 0:D]).then_inc(ye_ready, 1)

    def some(base, s):
        return not isinstance(base, int) or 0 <= base + s < NS

    def expert_tensor(pe, base, s, expert, between=None):
        if some(base, s + 2):
            xg_transpose(pe, base, s + 2)
        if some(base, s + 1):
            up(pe, base, s + 1)
        if between:
            between()
        if some(base, s):
            down(pe, base, s, expert(base + s))

    def expert_scalar(act, base, s, expert, between=None):
        if some(base, s + 2):
            xgT_copy(act, base, s + 2)
        if some(base, s + 1):
            gelu(act, base, s + 1, expert(base + (s + 1)))
        if between:
            between()
        if some(base, s):
            out_copy(act, base, s)

    def tiles_of(b):
        return qkv3[:, ds(b * 2, 2), 0:2 * D]

    def phi(v, b):
        nc.vector.scalar_tensor_tensor(out=tiles_of(b), in0=qk_exp[:, ds(b * 2, 2), :], scalar=1.0, in1=tiles_of(b),
                                       op0=ALU.min, op1=ALU.add).then_inc(phi_ready, 1)

    def attn_outer(v, b, r):
        i = b * 2 + r
        k = qkv3[:, ds(i, 1), D:2 * D].rearrange("p a (h d) -> p (a h) d", d=DH)
        vv = qkv3[:, ds(i, 1), 2 * D:3 * D].rearrange("p a (h e) -> p (a h) e", e=DH)
        if not (isinstance(b, int) and b == 0):
            v.wait_ge(cum_ps, b * 2)
        if r == 0:
            v.wait_ge(phi_ready, b + 1)
        nc.vector.tensor_tensor(outer[r].rearrange("p (h d e) -> p h d e", d=DH, e=DH),
                                k.unsqueeze(3).broadcast_to([P, H, DH, DH]),
                                vv.unsqueeze(2).broadcast_to([P, H, DH, DH]), ALU.mult).then_inc(outer_ready, 1)

    def attn_cumsum(pe, b, r):
        i = b * 2 + r
        pe.wait_ge(outer_ready, i + 1)
        if not (isinstance(i, int) and i == 0):
            pe.wait_ge(cq_ready, i * 2)
        for half in range(2):
            cols = slice(half * 512, half * 512 + 512)
            nc.tensor.matmul(ps[half], const("tri_incl"), outer[r][:, cols], start=True, stop=(r == 0))
            if r:
                nc.tensor.matmul(ps[half], const("ones"), outer[0][:, cols], start=False, stop=True)
        last = nc.tensor.matmul(ps[2][:, 0:D], const("tri_incl"), qkv3[:, ds(i, 1), D:2 * D],
                                start=True, stop=(r == 0))
        if r:
            last = nc.tensor.matmul(ps[2][:, 0:D], const("ones"), qkv3[:, ds(i - 1, 1), D:2 * D],
                                    start=False, stop=True)
        last.then_inc(cum_ps, 1)

    def attn_apply(v, b, r):
        i = b * 2 + r
        q = qkv3[:, ds(i, 1), 0:D].rearrange("p a c -> p (a c)")
        v.wait_ge(cum_ps, i + 1)
        nc.vector.tensor_tensor(cqk, ps[2][:, 0:D], q, ALU.mult).then_inc(cq_ready, 1)
        for half in range(2):
            last = nc.vector.tensor_tensor(
                cq[:, half * 512:half * 512 + 512].rearrange("p (c e) -> p c e", e=DH),
                ps[half].rearrange("p (c e) -> p c e", e=DH),
                qkv3[:, ds(i, 1), half * 64:half * 64 + 64].rearrange("p a c -> p (a c)").unsqueeze(2).broadcast_to([P, 64, DH]),
                ALU.mult)
        last.then_inc(cq_ready, 1)

    def attn_divide(v, i):
        v.wait_ge(cq_ready, i * 2 + 1)
        nc.vector.tensor_reduce(den, cqk.rearrange("p (h d) -> p h d", d=DH), AX.X, ALU.add).then_inc(den_ready, 1)
        v.wait_ge(den_ready, i * 2 + 1)
        nc.vector.tensor_scalar(den, den, EPS_DEN, None, ALU.max).then_inc(den_ready, 1)
        v.wait_ge(den_ready, i * 2 + 2)
        nc.vector.reciprocal(rden, den).then_inc(rden_ready, 1)
        v.wait_ge(cq_ready, i * 2 + 2)
        nc.vector.tensor_reduce(num.rearrange("p (h e) -> p h e", e=DH),
                                cq.rearrange("p (h d e) -> p h e d", d=DH, e=DH), AX.X, ALU.add).then_inc(num_ready, 1)
        v.wait_ge(num_ready, i + 1)
        v.wait_ge(rden_ready, i + 1)
        if not (isinstance(i, int) and i == 0):
            v.wait_ge(yT_ps, i)
        nc.vector.tensor_tensor(y_tok.rearrange("p (h e) -> p h e", e=DH), num.rearrange("p (h e) -> p h e", e=DH),
                                rden.unsqueeze(2).broadcast_to([P, H, DH]), ALU.mult).then_inc(y_ready, 1)

    def attn_transpose(pe, i):
        pe.wait_ge(y_ready, i + 1)
        if from_(i, 1):
            pe.wait_ge(o_ready, i)
        nc.tensor.transpose(ps[5][:, 0:P], y_tok, ident).then_inc(yT_ps, 1)

    def attn_project(pe, i):
        pe.wait_ge(yT_ready, i + 1)
        nc.tensor.matmul(ps[5][:, 0:D], yT0, wT[:, 3, :], start=True, stop=True).then_inc(o_ps, 1)

    def attn_yT(act, i):
        act.wait_ge(yT_ps, i + 1)
        if from_(i, 1):
            act.wait_ge(o_ps, i)
        nc.scalar.copy(yT0, ps[5][:, 0:P]).then_inc(yT_ready, 1)

    def attn_o(act, i):
        act.wait_ge(o_ps, i + 1)
        if from_(i, 1):
            act.wait_ge(x_attn, i)
        nc.scalar.copy(o_tok, ps[5][:, 0:D]).then_inc(o_ready, 1)

    def steps(eng, expert_step, even, odd):
        def step(b, base, s):
            i = b * 2 + s // 2
            expert_step(eng, base, s, between=(lambda: even(b, s // 2, i)) if s % 2 == 0 else lambda: odd(i))
        for s in range(-2, 0):
            expert_step(eng, 0, s)
        for b in range(2):
            for s in range(SPI):
                step(b, b * SPI, s)
        with eng.Fori(2, NFULL) as b:
            for s in range(SPI):
                step(b, b * SPI, s)
        for j in range(NFULL * SPI, NS):
            i = j // 2
            base, s = j // SPI * SPI, j % SPI
            expert_step(eng, base, s, between=(lambda: even(None, 0, i)) if j % 2 == 0 else lambda: odd(i))

    def attn_add(pool, i):
        pool.wait_ge(o_ready, i + 1)
        nc.gpsimd.tensor_tensor(x_sb[:, i, :], o_tok, x_sb[:, i, :], ALU.add).then_inc(x_attn, 1)

    at = [0]

    def view(n):
        at[0] += n
        return qkv[:, at[0] - n:at[0]]

    GP = GT * P
    DA = D + H
    ymoe = [view(GT * TOPK * D) for _ in range(2)]
    xT2 = [view(2 * (T + 1)) for _ in range(2)]
    mix_t = [[view(GP) for _ in range(2)] for _ in range(2)]
    e_q, r_q, phi_q = view(GP), view(GP), view(GP)
    e_k, r_k, phi_k = view(GP), view(GP), view(GP)
    v_aug = view(GT * DA).rearrange("p (n c) -> p n c", c=DA)
    kvm = view(2 * DA).rearrange("p (b c) -> p b c", c=DA)
    rcp = view(GT * H).rearrange("p (n h) -> p n h", h=H)
    y1 = view(GP)
    yT1 = view(GP)
    tanh_r = view(GP)
    k_relu, k_act = view(GP), view(GP)
    res = [outer[p][:, 0:GP] for p in range(2)]
    assert at[0] <= NT * 3 * D
    kv_bank = ps_all[:, 2 * 512:4 * 512].rearrange("p (n c) -> p n c", c=2 * D)
    nd_bank = ps_all[:, 6 * 512:8 * 512].rearrange("p (n c) -> p n c", c=256)
    g_exp = sem("g_exp")
    y_in = [sem("y_in0"), sem("y_in1")]
    x1_ready, ln2_stats, ln2_mv, ve2_ready, rstd2_ready = (
        sem("x1_ready"), sem("ln2_stats"), sem("ln2_mv"), sem("ve2_ready"), sem("rstd2_ready"))
    x1_part = sem("x1_part")
    xn2_ready, xT2_ps, xT2_ready, mu_x, mixed = sem("xn2_ready"), sem("xT2_ps"), sem("xT2_ready"), sem("mu_x"), sem("mixed")
    q_ps, kv_ps, r_ps, kf_ps = sem("q_ps"), sem("kv_ps"), sem("r_ps"), sem("kf_ps")
    qparts, kparts, v_ready = sem("qparts"), sem("kparts"), sem("v_ready")
    phiq_ready, phik_ready, kact_ready = sem("phiq_ready"), sem("phik_ready"), sem("kact_ready")
    relu_ready = sem("relu_ready")
    KV_ps, KV_ready, nd_ps, rcp_ready, y1_ready = sem("KV_ps"), sem("KV_ready"), sem("nd_ps"), sem("rcp_ready"), sem("y1_ready")
    yT1_ps, yT1_ready = sem("yT1_ps"), sem("yT1_ready")
    tanh_ready, vf_ps, pr_ps = sem("tanh_ready"), sem("vf_ps"), sem("pr_ps")
    ffn_ready, rest_ready, res_ready = sem("ffn_ready"), sem("rest_ready"), sem("res_ready")
    out_done = [sem("out_done0"), sem("out_done1")]
    pads = sem("pads")

    def x1_of(g):
        return x_sb[:, ds(g * GT, GT), :].rearrange("p a c -> p (a c)")

    def load_y(sp, g, p):
        if from_(g, 2):
            sp.wait_ge(x1_ready, g - 1)
        sp.dma_start(ymoe[p].rearrange("p (n c) -> p n c", n=GT),
                     y_dram[0:TOK * TOPK, :].rearrange("(n p k) d -> p n (k d)", p=P, k=TOPK)[:, ds(g * GT, GT), :]
                     ).then_inc(y_in[p], 16)

    def combine(v, g, p):
        v.wait_ge(y_in[p], (g // 2 + 1) * 16)
        for k in range(TOPK):
            for n in range(GT):
                xi = x_sb[:, ds(g * GT + n, 1), :].rearrange("p a c -> p (a c)")
                last = nc.vector.scalar_tensor_tensor(
                    out=xi, in0=ymoe[p][:, (n * TOPK + k) * D:(n * TOPK + k + 1) * D],
                    scalar=sel[k][:, ds(g * GT + n, 1)], in1=xi, op0=ALU.mult, op1=ALU.add)
            last.then_inc(x1_part if k == 0 else x1_ready, 1)
            wait_alone(v, x1_part if k == 0 else x1_ready, g + 1)
        for n in range(GT):
            last = nc.vector.bn_stats(stats[p][:, n, :], x_sb[:, ds(g * GT + n, 1), :])
        last.then_inc(ln2_stats, 1)
        wait_alone(v, ln2_stats, g + 1)
        for n in range(GT):
            last = nc.vector.bn_aggr(mv[p][:, n, :], stats[p][:, n, :])
        last.then_inc(ln2_mv, 1)

    def rstd2(pool, g, p):
        pool.wait_ge(ln2_mv, g + 1)
        nc.gpsimd.tensor_tensor(ve[p][:, :], mv[p][:, :, 1], eps_ln[:, :], ALU.add).then_inc(ve2_ready, 1)
        pool.wait_ge(ve2_ready, g + 1)
        nc.gpsimd.tensor_tensor(rstd[p][:, :], ve[p][:, :], mhalf[:, :], ALU.pow).then_inc(rstd2_ready, 1)

    def norm2(v, g, p):
        v.wait_ge(rstd2_ready, g + 1)
        if from_(g, 2):
            v.wait_ge(xT2_ps, g - 1)
        for n in range(GT):
            last = nc.vector.tensor_scalar(xn[p][:, n, :], x_sb[:, ds(g * GT + n, 1), :].rearrange("p a c -> p (a c)"),
                                           mv[p][:, n, 0:1], rstd[p][:, n:n + 1], ALU.subtract, ALU.mult)
        last.then_inc(xn2_ready, 1)

    def xT2_transpose(pe, g, p):
        pe.wait_ge(xn2_ready, g + 1)
        if from_(g, 2):
            pe.wait_ge(yT1_ready, g - 1)
        elif g == 1:
            pe.wait_ge(xT2_ready, 1)
        for n in range(GT):
            last = nc.tensor.transpose(ps[1][:, n * P:(n + 1) * P], xn[p][:, n, :], ident)
        last.then_inc(xT2_ps, 1)

    def xT2_of(p):
        return xT2[p].rearrange("p (b t) -> p b t", t=T + 1)

    def xT2_copy(act, g, p):
        act.wait_ge(xT2_ps, g + 1)
        if from_(g, 2):
            act.wait_ge(q_ps, g - 1)
            act.wait_ge(mixed, g - 1)
        nc.scalar.copy(xT2_of(p)[:, :, 1:T + 1], ps[1].rearrange("p (b t) -> p b t", t=T)).then_inc(xT2_ready, 1)
        act.wait_ge(xT2_ready, g + 1)
        if from_(g, 2):
            act.wait_ge(kf_ps, g - 1)
        for m in range(2):
            last = nc.scalar.activation(mix_t[p][m].rearrange("p (b t) -> p b t", t=T), xT2_of(p)[:, :, 1:T + 1],
                                        ACT.Copy, scale=mu[:, m:m + 1])
        last.then_inc(mu_x, 1)

    def mix(v, g, p):
        v.wait_ge(mu_x, g + 1)
        for m in range(2):
            t = mix_t[p][m].rearrange("p (b t) -> p b t", t=T)
            last = nc.vector.scalar_tensor_tensor(out=t, in0=xT2_of(p)[:, :, 0:T], scalar=one_mu[:, m:m + 1],
                                                  in1=t, op0=ALU.mult, op1=ALU.add)
        last.then_inc(mixed, 1)

    def phi_k_vector(v, g):
        v.wait_ge(kparts, g + 1)
        if from_(g, 1):
            v.wait_ge(KV_ps, g)
        nc.vector.scalar_tensor_tensor(out=phi_k, in0=e_k, scalar=1.0, in1=r_k, op0=ALU.min, op1=ALU.add
                                       ).then_inc(phik_ready, 1)

    def phi_q_vector(v, g):
        v.wait_ge(qparts, g + 1)
        if from_(g, 1):
            v.wait_ge(nd_ps, g)
        nc.vector.scalar_tensor_tensor(out=phi_q, in0=e_q, scalar=1.0, in1=r_q, op0=ALU.min, op1=ALU.add
                                       ).then_inc(phiq_ready, 1)

    def square_keys(v, g):
        v.wait_ge(relu_ready, g + 1)
        if from_(g, 1):
            v.wait_ge(vf_ps, g)
        nc.vector.tensor_tensor(k_act, k_relu, k_relu, ALU.mult).then_inc(kact_ready, 1)

    def mask_KV(v, g):
        v.wait_ge(KV_ps, g + 1)
        if from_(g, 1):
            v.wait_ge(nd_ps, g)
        nc.vector.tensor_tensor(kvm, ps[0].rearrange("p (b c) -> p b c", b=2)[:, :, 0:DA],
                                const("head_mask").unsqueeze(1).broadcast_to([P, 2, DA]), ALU.mult
                                ).then_inc(KV_ready, 1)

    def divide(v, g):
        v.wait_ge(nd_ps, g + 1)
        nc.vector.reciprocal(rcp, nd_bank[:, :, D:DA]).then_inc(rcp_ready, 1)
        v.wait_ge(rcp_ready, g + 1)
        if from_(g, 1):
            v.wait_ge(yT1_ps, g)
        nc.vector.tensor_tensor(y1.rearrange("p (n h d) -> p n h d", h=H, d=DH),
                                nd_bank[:, :, 0:D].rearrange("p n (h d) -> p n h d", d=DH),
                                rcp.unsqueeze(3).broadcast_to([P, GT, H, DH]), ALU.mult).then_inc(y1_ready, 1)

    def ffn(v, g, p):
        v.wait_ge(vf_ps, g + 1)
        v.wait_ge(tanh_ready, g + 1)
        if from_(g, 2):
            v.wait_ge(out_done[p], g // 2 * 16)
        nc.vector.scalar_tensor_tensor(out=res[p], in0=tanh_r, scalar=1.0, in1=ps[5], op0=ALU.add, op1=ALU.mult
                                       ).then_inc(ffn_ready, 1)

    def add_x1(pool, g, p):
        pool.wait_ge(ffn_ready, g + 1)
        nc.gpsimd.tensor_tensor(res[p], res[p], x1_of(g), ALU.add).then_inc(rest_ready, 1)

    def finish(v, g, p):
        v.wait_ge(rest_ready, g + 1)
        v.wait_ge(pr_ps, g + 1)
        nc.vector.tensor_tensor(res[p], ps[6], res[p], ALU.add).then_inc(res_ready, 1)

    def k_scalar(act, g):
        act.wait_ge(kv_ps, g + 1)
        if from_(g, 1):
            act.wait_ge(phik_ready, g)
            act.wait_ge(KV_ps, g)
        nc.scalar.activation(e_k.rearrange("p (n c) -> p n c", c=D), kv_bank[:, :, 0:D], ACT.Exp)
        nc.scalar.activation(r_k.rearrange("p (n c) -> p n c", c=D), kv_bank[:, :, 0:D], ACT.Relu).then_inc(kparts, 1)
        nc.scalar.copy(v_aug[:, :, 0:D], kv_bank[:, :, D:2 * D]).then_inc(v_ready, 1)

    def q_scalar(act, g):
        act.wait_ge(q_ps, g + 1)
        if from_(g, 1):
            act.wait_ge(phiq_ready, g)
        nc.scalar.activation(e_q, ps[7], ACT.Exp)
        nc.scalar.activation(r_q, ps[7], ACT.Relu).then_inc(qparts, 1)

    def yT1_copy(act, g):
        act.wait_ge(yT1_ps, g + 1)
        if from_(g, 1):
            act.wait_ge(pr_ps, g)
        nc.scalar.copy(yT1, ps[1]).then_inc(yT1_ready, 1)

    def keys_scalar(act, g):
        act.wait_ge(kf_ps, g + 1)
        if from_(g, 1):
            act.wait_ge(kact_ready, g)
        nc.scalar.activation(k_relu, ps[5], ACT.Relu).then_inc(relu_ready, 1)

    def gate_scalar(act, g):
        act.wait_ge(r_ps, g + 1)
        if from_(g, 1):
            act.wait_ge(ffn_ready, g)
        nc.scalar.activation(tanh_r, ps[4], ACT.Tanh, scale=0.5).then_inc(tanh_ready, 1)

    def qkv_tensor(pe, g, p):
        pe.wait_ge(xT2_ready, g + 1)
        if from_(g, 1):
            pe.wait_ge(v_ready, g)
        for n in range(GT):
            last = nc.tensor.matmul(kv_bank[:, n, :], xT2_of(p)[:, n // 2, 1 + (n % 2) * P:1 + (n % 2) * P + P],
                                    wqkv2[:, D:3 * D], start=True, stop=True)
        last.then_inc(kv_ps, 1)
        if from_(g, 1):
            pe.wait_ge(y1_ready, g)
        nc.tensor.matmul(ps[7], wqkv2[:, 0:D], xT2_of(p)[:, :, 1:T + 1], start=True, stop=True).then_inc(q_ps, 1)

    def y1_transpose(pe, g):
        pe.wait_ge(y1_ready, g + 1)
        for n in range(GT):
            last = nc.tensor.transpose(ps[1][:, n * P:(n + 1) * P], y1[:, n * P:(n + 1) * P], ident)
        last.then_inc(yT1_ps, 1)

    def rk_tensor(pe, g, p):
        pe.wait_ge(mixed, g + 1)
        if from_(g, 1):
            pe.wait_ge(tanh_ready, g)
        for n in range(GT):
            last = nc.tensor.matmul(ps[4][:, n * P:(n + 1) * P], mix_t[p][0][:, n * P:(n + 1) * P], wT[:, 4, :],
                                    start=True, stop=True)
        last.then_inc(r_ps, 1)
        if from_(g, 1):
            pe.wait_ge(ffn_ready, g)
        nc.tensor.matmul(ps[5], wT[:, 5, :], mix_t[p][1], start=True, stop=True).then_inc(kf_ps, 1)

    def project2_tensor(pe, g):
        pe.wait_ge(yT1_ready, g + 1)
        for n in range(GT):
            o = ps[6][:, n * P:(n + 1) * P]
            nc.tensor.matmul(o, yT1[:, n * P:(n + 1) * P], wproj[:, :], start=True, stop=False)
            last = nc.tensor.matmul(o, ones_bf[0:3, :], bias3[:, BIASP:BIASP + D], start=False, stop=True)
        last.then_inc(pr_ps, 1)

    def KV_tensor(pe, g):
        pe.wait_ge(phik_ready, g + 1)
        pe.wait_ge(v_ready, g + 1)
        if from_(g, 1):
            pe.wait_ge(KV_ready, g)
        for b in range(2):
            for r in range(2):
                n = 2 * b + r
                last = nc.tensor.matmul(ps[0][:, b * 256:b * 256 + DA], phi_k[:, n * D:(n + 1) * D],
                                        v_aug[:, n, :], start=(r == 0), stop=(r == 1))
        last.then_inc(KV_ps, 1)

    def values_tensor(pe, g):
        pe.wait_ge(kact_ready, g + 1)
        for n in range(GT):
            last = nc.tensor.matmul(ps[5][:, n * P:(n + 1) * P], k_act[:, n * P:(n + 1) * P], wT[:, 6, :],
                                    start=True, stop=True)
        last.then_inc(vf_ps, 1)

    def nd_tensor(pe, g):
        pe.wait_ge(KV_ready, g + 1)
        pe.wait_ge(phiq_ready, g + 1)
        if from_(g, 1):
            pe.wait_ge(res_ready, g)
        for n in range(GT):
            last = nc.tensor.matmul(nd_bank[:, n, 0:DA], phi_q[:, n * P:(n + 1) * P], kvm[:, n // 2, :],
                                    start=True, stop=True)
        last.then_inc(nd_ps, 1)

    def group_tensor(pe, g, p):
        qkv_tensor(pe, g, p)
        if from_(g, 1):
            y1_transpose(pe, g - 1)
        rk_tensor(pe, g, p)
        if till(g, NG - 2):
            xT2_transpose(pe, g + 1, 1 - p)
        if from_(g, 1):
            project2_tensor(pe, g - 1)
        KV_tensor(pe, g)
        values_tensor(pe, g)
        nd_tensor(pe, g)

    def group_vector(v, g, p):
        if till(g, NG - 2):
            norm2(v, g + 1, 1 - p)
        if till(g, NG - 3):
            combine(v, g + 2, p)
        phi_k_vector(v, g)
        square_keys(v, g)
        phi_q_vector(v, g)
        if from_(g, 1):
            finish(v, g - 1, 1 - p)
        mask_KV(v, g)
        if till(g, NG - 2):
            mix(v, g + 1, 1 - p)
        ffn(v, g, p)
        divide(v, g)

    def group_scalar(act, g, p):
        k_scalar(act, g)
        if from_(g, 1):
            yT1_copy(act, g - 1)
        q_scalar(act, g)
        keys_scalar(act, g)
        gate_scalar(act, g)
        if till(g, NG - 2):
            xT2_copy(act, g + 1, 1 - p)

    def group_pool(pool, g, p):
        if till(g, NG - 3):
            rstd2(pool, g + 2, p)
        add_x1(pool, g, p)

    def groups(eng, group):
        for g in range(2):
            group(eng, g, g)
        with eng.Fori(1, ITS - 1) as it:
            for p in range(2):
                group(eng, it * 2 + p, p)
        for g in range(NG - 2, NG):
            group(eng, g, g % 2)

    NFULL = NT // 2
    SPI = 4
    TAIL = NS - NFULL * SPI

    def expert_of(eng, registers=1):
        regs = [eng.alloc_register(f"expert{n}") for n in range(registers)]
        def expert(j):
            regs.append(regs.pop(0))
            eng.reg_load(regs[0], slot_exp[0:1, ds(j, 1)])
            return eng.snap(regs[0], min_val=0, max_val=NE - 1)
        return expert

    with nc.Block() as block:
        @block.sync
        def _(sp):
            for lo, n, s in ((0, 2 * GT, x_first), (2 * GT, NT - 2 * GT, x_rest)):
                sp.dma_start(x_sb[:, lo:lo + n, :],
                             x_in.rearrange("b t d -> (b t) d").rearrange("(n p) d -> p n d", p=P)[:, lo:lo + n, :]
                             ).then_inc(s, 16)

            def save(it):
                for p in range(2):
                    g = it * 2 + p
                    sp.wait_ge(xn_ready, g + 1)
                    sp.dma_start(xn_dram.rearrange("(n p) d -> p n d", p=P)[:, ds(g * GT, GT), :], xn[p][:, :, :]
                                 ).then_inc(xn_saved[p], 16)
            save(0)
            sp.dma_start(w2_sb[:, :, :], W2.rearrange("e (c p) f -> p (e c) f", p=P)).then_inc(late_in, 16)
            with sp.Fori(1, ITS) as it:
                save(it)
            sp.wait_ge(exp_ready, 1)
            expert = expert_of(sp)
            for s in range(NX):
                load_w1(sp, 0, s, expert(s))
            with sp.Fori(1, NS // NX) as it:
                for s in range(NX):
                    load_w1(sp, it * NX, s, expert(it * NX + s))
            for j in range(NS // NX * NX, NS):
                load_w1(sp, j - j % NX, j % NX, expert(j))
            for n in range(NX):
                sp.wait_ge(ye_out[n], 16 * len(range(n, NS, NX)))
            for g in range(3):
                load_y(sp, g, g % 2)

            def save_out(g, p):
                sp.wait_ge(res_ready, g + 1)
                sp.dma_start(out.rearrange("b t d -> (b t) d").rearrange("(n p) d -> p n d", p=P)[:, ds(g * GT, GT), :],
                             res[p].rearrange("p (n d) -> p n d", n=GT)).then_inc(out_done[p], 16)
            with sp.Fori(0, ITS - 2) as it:
                for p in range(2):
                    load_y(sp, it * 2 + (3 + p), 1 - p)
                    save_out(it * 2 + p, p)
            load_y(sp, NG - 1, 1)
            for g in range(NG - 4, NG):
                save_out(g, g % 2)
            for p in range(2):
                sp.wait_ge(out_done[p], 16 * ITS)

        @block.scalar
        def _(act):
            act.dma_start(cst[:, :], consts).then_inc(consts_in, 16)
            for n, w in enumerate((Wq, Wk, Wv, Wo, W_r, W_k, W_v)):
                act.dma_start(w_raw[:, n, :], w).then_inc(wts_in, 16)
            act.dma_start(w_in[:, 3 * D:NQ], Wg).then_inc(wts_in, 16)
            act.dma_start(w_raw[0:NE * NC, 7, :], b1.rearrange("e (c p) -> (e c) p", p=P)).then_inc(wts_in, 16)
            act.dma_start(bias_sp[:, 0:BIASP // P], b2.rearrange("e h -> (e h)").rearrange("(p c) -> p c", p=P)).then_inc(bias_in, 16)
            act.dma_start(bias_sp[:, BIASP // P:NBIAS // P], b_proj.rearrange("(p c) -> p c", p=P)).then_inc(bias_in, 16)
            act.dma_start(bg_sb[:, :], bg.rearrange("(a e) -> a e", a=1).broadcast_to([P, NE])).then_inc(bias_in, 16)
            act.dma_start(mu[:, 0:1], mu_r.rearrange("(p c) -> p c", p=P)).then_inc(bias_in, 16)
            act.dma_start(mu[:, 1:2], mu_k.rearrange("(p c) -> p c", p=P)).then_inc(bias_in, 16)
            act.dma_start(wqkv2[:, :], w_qkv).then_inc(late_in, 16)
            act.dma_start(wproj[:, :], w_proj).then_inc(late_in, 16)
            act.wait_ge(wT_ps, 1)
            nc.scalar.copy(w_in[:, 0:3 * D], ps[4][:, 0:3 * P]).then_inc(wT_ready, 1)
            nc.scalar.copy(wT[:, 3, :], ps[4][:, 3 * P:4 * P])
            nc.scalar.copy(b1T[:, :], ps[6][:, 0:NE * NC])
            nc.scalar.copy(wT[:, 4:6, :].rearrange("p a b -> p (a b)"), ps[5][:, 0:2 * P])
            nc.scalar.activation(wT[:, 6, :], ps[5][:, 2 * P:3 * P], ACT.Copy, scale=0.5).then_inc(wT_ready, 1)
            front(act, front_scalar)
            act.wait_ge(bias_split, 5)
            for n in range(3):
                for lo, hi in ((0, BIASP), (BIASP, NBIAS)):
                    act.dma_start(bias3[n:n + 1, lo:hi].rearrange("a (p c) -> a p c", p=P),
                                  bias_part[:, n, lo // P:hi // P]).then_inc(bias_rows, 16)
            for g in range(BY_VECTOR):
                exp_relu(act, g)
            act.wait_ge(gate_in, 1)
            nc.scalar.activation(rt[3], rt[3], ACT.Exp).then_inc(gate_exp, 1)

            def by_row(it):
                for p in range(2):
                    g = it * 2 + p
                    act.wait_ge(hot_tile, g + 1)
                    if after_first(it):
                        act.wait_ge(tab_ps, g - 1)
                    for k in range(TOPK):
                        last = nc.scalar.activation(hot_val[p][:, 1, k, :, :], hot_hi[p][:, k, :, :], ACT.Copy,
                                                    scale=const("pair_no")[:, k:k + 1])
                    last.then_inc(hot_by_row, 1)
            by_row(0)
            with act.Fori(1, ITS) as it:
                by_row(it)
            for g in range(BY_VECTOR, NG):
                exp_relu(act, g)
            expert = expert_of(act)

            def even(b, r, i):
                if from_(i, 2) and till(i, NT + 1):
                    attn_o(act, i - 2)

            def odd(i):
                if from_(i, 1) and till(i, NT):
                    attn_yT(act, i - 1)
            steps(act, lambda act, base, s, between=None: expert_scalar(act, base, s, expert, between), even, odd)
            act.wait_ge(pads, 3)
            xT2_copy(act, 0, 0)
            groups(act, group_scalar)
            yT1_copy(act, NG - 1)

        @block.gpsimd
        def _(pool):
            nc.gpsimd.memset(mhalf[:, :], -0.5).then_inc(pool_const, 1)
            nc.gpsimd.memset(eps_ln[:, :], EPS_LN).then_inc(pool_const, 1)
            pool.wait_ge(pool_const, 2)
            pool.wait_ge(consts_in, 16)
            front(pool, front_pool)
            for g in range(NG + 1 - SINE_LAG, NG):
                sine(pool, g)
            pool.wait_ge(rot_ready, BY_VECTOR)
            for g in range(BY_VECTOR, NG):
                rotate(pool, nc.gpsimd.tensor_tensor, g)

            def by_tile(it):
                for p in range(2):
                    g = it * 2 + p
                    pool.wait_ge(hot_tile, g + 1)
                    if after_first(it):
                        pool.wait_ge(tab_ps, g - 1)
                    for k in range(TOPK):
                        last = nc.gpsimd.tensor_tensor(
                            hot_val[p][:, 0, k, :, :], hot_hi[p][:, k, :, :],
                            const("tile_no")[:, ds(g * GT, GT)].unsqueeze(2).broadcast_to([P, GT, NS]), ALU.mult)
                    last.then_inc(hot_by_tile, 1)
            by_tile(0)
            with pool.Fori(1, ITS) as it:
                by_tile(it)
            pool.wait_ge(idx_ready, 2)
            for p in range(2):
                pool.wait_ge(xn_saved[p], 16 * ITS)
            for j in range(AHEAD):
                gather(pool, j)
            for j in range(NS):
                if j + AHEAD < NS:
                    gather(pool, j + AHEAD)
                scatter(pool, j)
                if j % 2 == 0 and j // 2 - 2 in range(NT):
                    attn_add(pool, j // 2 - 2)
            for g in range(2):
                rstd2(pool, g, g)
            groups(pool, group_pool)

        @block.tensor
        def _(pe):
            pe.wait_ge(consts_in, 16)
            pe.wait_ge(wts_in, 16 * 9)
            nc.tensor.transpose(ps[6][:, 0:NE * NC], w_raw[0:NE * NC, 7, :], ident[0:NE * NC, 0:NE * NC])
            for n in range(7):
                last = nc.tensor.transpose(ps[4 + n // 4][:, (n % 4) * P:(n % 4 + 1) * P], w_raw[:, n, :], ident)
            last.then_inc(wT_ps, 1)
            pe.wait_ge(wT_ready, 2)
            front(pe, front_tensor)
            pe.wait_ge(rank_in, 1)
            flat = "p a e -> p (a e)"
            pe.wait_ge(qkv_raw, NT)
            pe.wait_ge(xT_ready, NG)
            nc.tensor.matmul(ps[0][:, 0:NT * NE], tri_bf[:, :], m_bf[:, :, :].rearrange(flat), start=True, stop=False)
            nc.tensor.matmul(ps[0][:, 0:NT * NE], ones_bf[:, :], cex_bf[:, :, :].rearrange(flat), start=False, stop=True)
            nc.tensor.matmul(ps[1][:, 0:NE], ones_bf[:, :], cin_bf[:, :], start=True, stop=True).then_inc(rank_ps, 1)
            def table(it, first):
                for p in range(2):
                    g = it * 2 + p
                    pe.wait_ge(hot_rows, g + 1)
                    pe.wait_ge(hot_by_tile, g + 1)
                    pe.wait_ge(hot_by_row, g + 1)
                    for n in range(TOPK * GT):
                        k, i = n // GT, n % GT
                        last = nc.tensor.matmul(ps[2][:, 0:2 * NS], hot_lo[p][:, n, :], hot_val[p][:, :, k, i, :],
                                                start=(first and p == 0 and n == 0), stop=False, skip_group_check=True)
                    last.then_inc(tab_ps, 1)
            table(0, True)
            with pe.Fori(1, ITS) as it:
                table(it, False)
            pe.wait_ge(exp_ready, 1)
            pe.wait_ge(late_in, 16 * 3)
            pe.wait_ge(bias_rows, 16 * 6)
            pe.wait_ge(idx_ready, 2)
            expert = expert_of(pe)

            def even(b, r, i):
                if from_(i, 2) and till(i, NT + 1):
                    attn_project(pe, i - 2)
                if till(i, NT - 1):
                    attn_cumsum(pe, b, r)

            def odd(i):
                if from_(i, 1) and till(i, NT):
                    attn_transpose(pe, i - 1)
            steps(pe, lambda pe, base, s, between=None: expert_tensor(pe, base, s, expert, between), even, odd)
            pe.wait_ge(pads, 3)
            xT2_transpose(pe, 0, 0)
            groups(pe, group_tensor)
            y1_transpose(pe, NG - 1)
            project2_tensor(pe, NG - 1)

        @block.vector
        def _(v):
            TT, TS, RED = nc.vector.tensor_tensor, nc.vector.tensor_scalar, nc.vector.tensor_reduce
            v.wait_ge(consts_in, 16)
            nc.vector.tensor_copy(ones_bf[:, :], const("ones"))
            nc.vector.tensor_copy(tri_bf[:, :], const("tri_excl"))
            nc.vector.tensor_copy(iota_bf[:, :], const("iota")).then_inc(small_ready, 1)
            v.wait_ge(x_first, 16)
            front(v, front_vector)

            v.wait_ge(bias_in, 16 * 5)
            TS(one_mu[:, :], mu[:, :], -1.0, 1.0, ALU.mult, ALU.add)
            nc.vector.tensor_copy(bias_part[:, 0, :], bias_sp[:, :]).then_inc(bias_split, 1)
            v.wait_ge(bias_split, 1)
            TT(bias_rest[:, 0, :], bias_sp[:, :], bias_part[:, 0, :], ALU.subtract).then_inc(bias_split, 1)
            v.wait_ge(bias_split, 2)
            nc.vector.tensor_copy(bias_part[:, 1, :], bias_rest[:, 0, :]).then_inc(bias_split, 1)
            v.wait_ge(bias_split, 3)
            TT(bias_rest[:, 1, :], bias_rest[:, 0, :], bias_part[:, 1, :], ALU.subtract).then_inc(bias_split, 1)
            v.wait_ge(bias_split, 4)
            nc.vector.tensor_copy(bias_part[:, 2, :], bias_rest[:, 1, :]).then_inc(bias_split, 1)

            n_route = [0]

            def done(ins):
                n_route[0] += 1
                ins.then_inc(route, 1)
                v.wait_ge(route, n_route[0])

            def per_tile(a):
                return a.unsqueeze(2).broadcast_to([P, NT, NE])

            def per_expert(a):
                return a.unsqueeze(1).broadcast_to([P, NT, NE])

            def row(n):
                return r32[:, n, :]

            A3, logits = rt, lgb
            v.wait_ge(qkv_raw, NT)
            done(TT(logits, qkv3[:, :, 3 * D:NQ], per_expert(bg_sb[:, :]), ALU.add))
            cur = logits
            for k in range(TOPK):
                done(RED(row(k), cur, AX.X, ALU.max))
                done(TT(A3[0], cur, per_tile(row(k)), ALU.is_equal))
                done(TT(A3[0], A3[0], per_expert(const("first")), ALU.mult))
                done(RED(row(2), A3[0], AX.X, ALU.max))
                done(TT(oh[k], per_expert(const("first")), per_tile(row(2)), ALU.is_equal))
                if k == 0:
                    TT(A3[3], logits, per_tile(row(0)), ALU.subtract).then_inc(gate_in, 1)
                    done(nc.vector.scalar_tensor_tensor(out=A3[1], in0=oh[0], scalar=-BIG, in1=logits,
                                                        op0=ALU.mult, op1=ALU.add))
                    cur = A3[1]
            done(TT(A3[0], oh[0], oh[1], ALU.add))
            nc.vector.tensor_copy(m_bf[:, :, :], A3[0])
            a, b_, sh = 0, 1, 1
            while sh < NT:
                nc.vector.tensor_copy(rt[b_][:, 0:sh, :], rt[a][:, 0:sh, :])
                done(TT(rt[b_][:, sh:, :], rt[a][:, sh:, :], rt[a][:, 0:NT - sh, :], ALU.add))
                a, b_, sh = b_, a, sh * 2
            TT(cex_bf[:, :, :], rt[a][:, :, :], m_bf[:, :, :], ALU.subtract)
            nc.vector.tensor_copy(cin_bf[:, :], rt[a][:, NT - 1, :]).then_inc(rank_in, 1)
            v.wait_ge(rank_ps, 1)
            done(TS(e8[:, 0, :], ps[1][:, 0:NE], float(P - 1), None, ALU.add))
            done(nc.vector.tensor_copy(e8i[:, 0, :], e8[:, 0, :]))
            done(TS(e8i[:, 1, :], e8i[:, 0, :], 7, None, ALU.logical_shift_right))
            done(nc.vector.tensor_copy(e8[:, 1, :], e8i[:, 1, :]))
            a_, b2_ = 1, 2
            for sh in (1, 2, 4):
                nc.vector.tensor_copy(e8[:, b2_, 0:sh], e8[:, a_, 0:sh])
                done(TT(e8[:, b2_, sh:], e8[:, a_, sh:], e8[:, a_, 0:NE - sh], ALU.add))
                a_, b2_ = b2_, b2_ + 1
            ends = e8[:, a_, :]
            done(TT(e8[:, 6, :], ends, e8[:, 1, :], ALU.subtract))
            done(TS(e8[:, 7, :], e8[:, 6, :], float(P), None, ALU.mult))
            done(TT(A3[0], ps[0][:, 0:NT * NE].rearrange("p (a e) -> p a e", e=NE), per_expert(e8[:, 7, :]), ALU.add))
            TT(A3[1], A3[0], oh[0], ALU.mult)
            done(TT(A3[2], A3[0], oh[1], ALU.mult))
            RED(row(3), A3[1], AX.X, ALU.add)
            done(RED(row(4), A3[2], AX.X, ALU.add))
            done(nc.vector.tensor_copy(posi[:, 0, :, :], r32[:, 3:5, :]))
            TS(posi[:, 1, :, :], posi[:, 0, :, :], 7, None, ALU.logical_shift_right)
            done(TS(posi[:, 2, :, :], posi[:, 0, :, :], P - 1, None, ALU.bitwise_and))
            nc.vector.tensor_copy(pos_hi[:, :, :], posi[:, 1, :, :])
            done(nc.vector.tensor_copy(pos_lo[:, :, :], posi[:, 2, :, :]))

            def onehots(it):
                for p in range(2):
                    g = it * 2 + p
                    if after_first(it):
                        v.wait_ge(hot_by_tile, g - 1)
                        v.wait_ge(hot_by_row, g - 1)
                    for k in range(TOPK):
                        last = TT(hot_hi[p][:, k, :, :], iota_bf[:, 0:NS].unsqueeze(1).broadcast_to([P, GT, NS]),
                                  pos_hi[:, k, ds(g * GT, GT)].unsqueeze(2).broadcast_to([P, GT, NS]), ALU.is_equal)
                    last.then_inc(hot_tile, 1)
                    if after_first(it):
                        v.wait_ge(tab_ps, g - 1)
                    for n in range(TOPK * GT):
                        k, i = n // GT, n % GT
                        last = TS(hot_lo[p][:, n, :], iota_bf[:, :], pos_lo[:, k, ds(g * GT + i, 1)], None, ALU.is_equal)
                    last.then_inc(hot_rows, 1)
            onehots(0)
            with v.Fori(1, ITS) as it:
                onehots(it)
            done(TT(cmp8, const("iota")[:, 0:NS].unsqueeze(2).broadcast_to([P, NS, NE]),
                    ends.unsqueeze(1).broadcast_to([P, NS, NE]), ALU.is_ge))
            done(RED(tab[:, 0, :], cmp8, AX.X, ALU.add))
            done(TS(tab[:, 0, :], tab[:, 0, :], float(NE - 1), None, ALU.min))
            nc.vector.tensor_copy(slot_exp[:, :], tab[:, 0, :]).then_inc(exp_ready, 1)
            v.wait_ge(tab_ps, NG)
            done(TS(tab[:, 1, :], ps[2][:, 0:NS], float(2 * P), -float(2 * P), ALU.mult, ALU.add))
            TS(tab[:, 3, :], ps[2][:, 0:NS], 0.0, None, ALU.is_equal)
            done(TT(tab[:, 2, :], ps[2][:, NS:2 * NS], tab[:, 1, :], ALU.add))
            done(TT(tab[:, 3, :], tab[:, 3, :], const("slot_row"), ALU.mult))
            done(TT(tab[:, 3, :], tab[:, 3, :], tab[:, 2, :], ALU.add))
            nc.vector.tensor_copy(slot_dst[:, :], tab[:, 3, :]).then_inc(idx_ready, 1)
            done(TS(tab[:, 2, :], tab[:, 2, :], 0.0, None, ALU.max))
            done(nc.vector.tensor_copy(tabi[:, :], tab[:, 2, :]))
            TS(slot_tok[:, :], tabi[:, :], 1, None, ALU.logical_shift_right).then_inc(idx_ready, 1)
            v.wait_ge(gate_exp, 1)
            RED(row(5), A3[3], AX.X, ALU.add)
            TT(A3[1], A3[3], oh[0], ALU.mult)
            done(TT(A3[2], A3[3], oh[1], ALU.mult))
            RED(row(6), A3[1], AX.X, ALU.add)
            RED(row(7), A3[2], AX.X, ALU.add)
            done(nc.vector.reciprocal(row(8), row(5)))
            TT(row(6), row(6), row(8), ALU.mult)
            done(TT(row(7), row(7), row(8), ALU.mult))
            done(nc.vector.scalar_tensor_tensor(out=row(9), in0=row(6), scalar=EPS_GATE, in1=row(7), op0=ALU.add, op1=ALU.add))
            done(nc.vector.reciprocal(row(10), row(9)))
            TT(sel[0][:, :], row(6), row(10), ALU.mult)
            done(TT(sel[1][:, :], row(7), row(10), ALU.mult))

            def batch(b, more=True):
                attn_apply(v, b, 0)
                attn_outer(v, b, 1)
                attn_divide(v, b * 2)
                if more:
                    phi(v, b + 1)
                attn_apply(v, b, 1)
                if more:
                    attn_outer(v, b + 1, 0)
                attn_divide(v, b * 2 + 1)
            v.wait_ge(phi_parts, NG)
            phi(v, 0)
            attn_outer(v, 0, 0)
            batch(0)
            with v.Fori(1, B - 1) as b:
                batch(b)
            batch(B - 1, more=False)

            v.wait_ge(x_attn, NT)
            for p in range(2):
                nc.vector.memset(xT2_of(p)[:, :, 0:1], 0.0).then_inc(pads, 1)
            nc.vector.memset(v_aug[:, :, D:DA], 1.0).then_inc(pads, 1)
            combine(v, 0, 0)
            norm2(v, 0, 0)
            combine(v, 1, 1)
            mix(v, 0, 0)
            groups(v, group_vector)
            finish(v, NG - 1, 1)

    return st


_INS = ['L0_attn_x', 'L0_attn_Wq', 'L0_attn_Wk', 'L0_attn_Wv', 'L0_attn_Wo', 'L0_ffn_Wg', 'L0_ffn_bg', 'L0_ffn_W1',
        'L0_ffn_b1', 'L0_ffn_W2', 'L0_ffn_b2', 'L1_attn_w_qkv', 'L1_attn_w_proj', 'L1_attn_b_proj', 'L1_ffn_W_r',
        'L1_ffn_W_k', 'L1_ffn_W_v', 'L1_ffn_mu_r', 'L1_ffn_mu_k']


def kernel(**inputs):
    import concourse.bacc as _bacc
    from concourse.bass_utils import run_bass_kernel_spmd as _run

    nc = _bacc.Bacc("TRN2", target_bir_lowering=False, num_devices=1)
    arrays, args = {}, []
    for name in _INS:
        a = np.ascontiguousarray(inputs[name])
        arrays[f"in_{name}"] = a
        args.append(nc.dram_tensor(f"in_{name}", a.shape, mybir.dt.from_np(a.dtype), kind="ExternalInput").ap())
    arrays["in_consts"] = constant_table()
    args.append(nc.dram_tensor("in_consts", (P, NCONST), mybir.dt.float32, kind="ExternalInput").ap())
    out = nc.dram_tensor("out_0", (B, T, D), mybir.dt.float32, kind="ExternalOutput").ap()
    build(nc, *args, out)
    r = _run(nc, [arrays], core_ids=[0])
    return r.results[0]["out_0"]
```

```python
from contextlib import ExitStack

import numpy as np
import concourse.bass as bass
from concourse import mybir

P = 128
D = 128
H, DH = 16, 8
B, T = 16, 256
TOK = B * T
NT = TOK // P
GT = 4
NG = NT // GT
NE, HID, TOPK = 8, 512, 2
NC = HID // P
NS = TOK * TOPK // P + NE - 1
EPS_LN, EPS_DEN, EPS_GATE = 1e-5, 1e-6, 1e-8
BIG = 3.0e38
BIASP, NBIAS = NE * D, NE * D + D

CONSTS = {}
_at = 0
for _name, _n in (("ident", P), ("tri_incl", P), ("tri_excl", P), ("ones", P), ("head_mask", P + H),
                  ("iota", P), ("cos", 2 * DH), ("sin", 2 * DH), ("first", NE), ("tile_no", NT),
                  ("pair_no", TOPK), ("slot_row", NS)):
    CONSTS[_name] = (_at, _at + _n)
    _at += _n
NCONST = _at


def constant_table():
    c = np.zeros((P, NCONST), np.float32)
    row, col = np.arange(P)[:, None], np.arange(P)[None, :]

    def put(name, a):
        lo, hi = CONSTS[name]
        c[:, lo:hi] = a

    put("ident", row == col)
    put("tri_incl", row <= col)
    put("tri_excl", row < col)
    put("ones", 1.0)
    put("head_mask", np.concatenate([row // DH == col // DH, row // DH == np.arange(H)[None, :]], 1))
    put("iota", col + 0 * row)
    half = DH // 2
    inv = np.float32(10000.0) ** (-np.arange(half, dtype=np.float32) / np.float32(half))
    ang = (np.arange(T, dtype=np.float32)[:, None] * inv[None, :].astype(np.float32)).astype(np.float32)
    cos, sin = np.cos(ang), np.sin(ang)
    for name, a in (("cos", np.concatenate([cos, cos], 1)), ("sin", np.concatenate([sin, -sin], 1))):
        put(name, a.reshape(2, P, DH).transpose(1, 0, 2).reshape(P, -1))
    put("first", NE - np.arange(NE))
    put("tile_no", 1 + np.arange(NT))
    put("pair_no", 2 * row + np.arange(TOPK))
    put("slot_row", TOK * TOPK + 256 + row + P * np.arange(NS))
    return c


def build(nc, x_in, Wq, Wk, Wv, Wo, Wg, bg, W1, b1, W2, b2, w_qkv, w_proj, b_proj, W_r, W_k, W_v,
          mu_r, mu_k, consts, out):
    f32, f32r, bf16, i32 = mybir.dt.float32, mybir.dt.float32r, mybir.dt.bfloat16, mybir.dt.int32
    ALU, ACT, AX = mybir.AluOpType, mybir.ActivationFunctionType, mybir.AxisListType
    ds = bass.ds
    st = ExitStack()

    def sbuf(name, shape, dt=f32):
        return st.enter_context(nc.sbuf_tensor(name, shape, dt))

    def sem(name):
        return st.enter_context(nc.semaphore(name))

    xn_dram = nc.dram_tensor("xn_rows", (TOK, D), f32, kind="Internal").ap()
    y_dram = nc.dram_tensor("expert_rows", (TOK * TOPK + NS * P, D), f32, kind="Internal").ap()

    cst = sbuf("cst", [P, NCONST])

    def const(name):
        lo, hi = CONSTS[name]
        return cst[:, lo:hi]

    ident = const("ident")
    x_sb = sbuf("x_sb", [P, NT, D])
    xn = [sbuf(f"xn{p}", [P, GT, D]) for p in range(2)]
    xT = [sbuf(f"xT{p}", [P, GT, P]) for p in range(2)]
    NQ = 3 * D + NE
    DA = D + H
    NW = 2 * D + DA
    qkv = sbuf("qkv", [P, NT * NW])
    qkv3 = qkv[:, :].rearrange("p (n c) -> p n c", c=NW)
    qk_exp = sbuf("qk_exp", [P, NT, 2 * D])
    NX = 4
    w1 = [sbuf(f"w1_{n}", [P, HID]) for n in range(NX)]
    b1T = sbuf("b1T", [P, NE * NC])
    w2_sb = sbuf("w2_sb", [P, NE * NC, D])
    wT = sbuf("wT", [P, 4, P])
    w_in = sbuf("w_in", [P, NQ])
    wqkv2 = sbuf("wqkv2", [P, 3 * D])
    wproj = sbuf("wproj", [P, D])
    mu = sbuf("mu", [P, 2])
    one_mu = sbuf("one_mu", [P, 2])
    bg_sb = sbuf("bg_sb", [P, NE])
    bias_sp = sbuf("bias_sp", [P, NBIAS // P])
    bias_rest = sbuf("bias_rest", [P, 2, NBIAS // P])
    bias_part = sbuf("bias_part", [P, 3, NBIAS // P], bf16)
    bias3 = sbuf("bias3", [3, NBIAS], bf16)
    ones_bf = sbuf("ones_bf", [P, P], bf16)
    tri_bf = sbuf("tri_bf", [P, P], bf16)
    iota_bf = sbuf("iota_bf", [P, P], bf16)
    stats = [sbuf(f"stats{p}", [P, GT, 6]) for p in range(2)]
    mv = [sbuf(f"mv{p}", [P, GT, 2]) for p in range(2)]
    ve = [sbuf(f"ve{p}", [P, GT]) for p in range(2)]
    minus = [sbuf(f"minus{p}", [P, GT]) for p in range(2)]
    rstd = [sbuf(f"rstd{p}", [P, GT]) for p in range(2)]
    shift = [sbuf(f"shift{p}", [P, GT]) for p in range(2)]
    mhalf = sbuf("mhalf", [P, GT])
    scrap = {name: sbuf(f"scrap_{name}", [1, 1])[:, :] for name in ("vector", "pool", "scalar", "zero")}
    r32 = sbuf("r32", [P, 12, NT])
    sel = [sbuf(f"sel{n}", [P, NT]) for n in range(TOPK)]
    m_bf = sbuf("m_bf", [P, NT, NE], bf16)
    cex_bf = sbuf("cex_bf", [P, NT, NE], bf16)
    cin_bf = sbuf("cin_bf", [P, NE], bf16)
    e8 = sbuf("e8", [P, 8, NE])
    e8i = sbuf("e8i", [P, 2, NE], i32)
    posi = sbuf("posi", [P, 3, TOPK, NT], i32)
    pos_lo = sbuf("pos_lo", [P, TOPK, NT])
    pos_hi = sbuf("pos_hi", [P, TOPK, NT])
    hot_lo = [sbuf(f"hot_lo{p}", [P, TOPK * GT, P], bf16) for p in range(2)]
    hot_hi = [sbuf(f"hot_hi{p}", [P, TOPK, GT, NS], bf16) for p in range(2)]
    hot_val = [sbuf(f"hot_val{p}", [P, 2, TOPK, GT, NS], bf16) for p in range(2)]
    tab = sbuf("tab", [P, 4, NS])
    tabi = sbuf("tabi", [P, NS], i32)
    slot_exp = sbuf("slot_exp", [P, NS], i32)
    slot_tok = sbuf("slot_tok", [P, NS], i32)
    slot_dst = sbuf("slot_dst", [P, NS], i32)
    AHEAD = 6
    xg = [sbuf(f"xg{n}", [P, D]) for n in range(NX)]
    ye = [sbuf(f"ye{n}", [P, D]) for n in range(NX)]
    xgT = [sbuf(f"xgT{n}", [P, P]) for n in range(2)]
    hidT = [sbuf(f"hidT{n}", [P, NC, P]) for n in range(2)]
    outer = [sbuf(f"outer{r}", [P, H * DH * DH])[:, :] for r in range(2)]
    w_raw = outer[0].rearrange("p (n c) -> p n c", c=P)
    HALF = H * DH * DH // 2
    high = [sbuf(f"high{r}", [P, 2 * HALF], f32r)[:, :] for r in range(2)]
    low = [sbuf(f"low{r}", [P, 2 * HALF], f32r)[:, :] for r in range(2)]
    tri_r = sbuf("tri_r", [P, P], f32r)
    cq = sbuf("cq", [P, H * (DH + 1) * DH])[:, :]
    cq4 = cq.rearrange("p (h d e) -> p h d e", d=DH + 1, e=DH)
    cqk = sbuf("cqk", [P, H, DH + 1])
    phib = [sbuf(f"phi{p}", [P, 2, 2 * D]) for p in range(2)]
    kv0 = sbuf("kv0", [P, DA])
    qT = sbuf("qT", [P, P])
    spare = [b[:, n * NT * NE:(n + 1) * NT * NE].rearrange("p (a e) -> p a e", e=NE)
             for b in (outer[1], cq) for n in range(4)]
    rt, oh, lgb = spare[0:4], spare[4:6], spare[6]
    cmp8 = outer[0][:, 0:NS * NE].rearrange("p (s e) -> p s e", e=NE)
    att = sbuf("att", [P, 4, D])
    num, y_tok, yT0, o_tok = (att[:, n, :] for n in range(4))
    dens = sbuf("dens", [P, 2, H])
    den, rden = dens[:, 0, :], dens[:, 1, :]

    ps_all = st.enter_context(nc.psum_tensor("banks", [P, 8 * 512], f32))
    ps = [ps_all[:, n * 512:(n + 1) * 512] for n in range(8)]

    consts_in, wts_in, late_in = sem("consts_in"), sem("wts_in"), sem("late_in")
    X_PARTS = ((0, GT), (GT, 2 * GT), (2 * GT, 3 * GT), (3 * GT, NT))
    x_loaded = [sem(f"x_loaded{n}") for n in range(len(X_PARTS))]
    w_late_in, w_late_ps, w_late_ready = sem("w_late_in"), sem("w_late_ps"), sem("w_late_ready")
    wT_ps, wT_ready = sem("wT_ps"), sem("wT_ready")
    bias_in, bias_split, bias_rows = sem("bias_in"), sem("bias_split"), sem("bias_rows")
    small_ready, pool_const, warmed = sem("small_ready"), sem("pool_const"), sem("warmed")
    ln_stats, ln_mv, ve_ready, rstd_part, rstd_ready, xn_ready = (
        [sem(f"{name}{layer}") for layer in range(2)]
        for name in ("ln_stats", "ln_mv", "ve_ready", "rstd_part", "rstd_ready", "xn_ready"))
    xT_ps, xT_ready = sem("xT_ps"), sem("xT_ready")
    xn_saved = [sem("xn_saved0"), sem("xn_saved1")]
    qkv_ps, qkv_raw = sem("qkv_ps"), sem("qkv_raw")
    route, gate_in, gate_exp = sem("route"), sem("gate_in"), sem("gate_exp")
    rank_in, rank_ps = sem("rank_in"), sem("rank_ps")
    hot_rows, hot_tile, hot_by_tile, hot_by_row = sem("hot_rows"), sem("hot_tile"), sem("hot_by_tile"), sem("hot_by_row")
    tab_ps, exp_ready, idx_ready = sem("tab_ps"), sem("exp_ready"), sem("idx_ready")
    sine_ready, cosine_ready, rot_ready, exp_part, phi_parts, phi_ready = (
        sem("sine_ready"), sem("cosine_ready"), sem("rot_ready"), sem("exp_part"), sem("phi_parts"), sem("phi_ready"))
    xg_in = [sem(f"xg_in{n}") for n in range(NX)]
    w1_in = [sem(f"w1_in{n}") for n in range(NX)]
    xgT_ps, xgT_ready, up_ps, gelu_ready = sem("xgT_ps"), sem("xgT_ready"), sem("up_ps"), sem("gelu_ready")
    down_ps, ye_ready = sem("down_ps"), sem("ye_ready")
    ye_out = [sem(f"ye_out{n}") for n in range(NX)]
    ones_ready, kv0_ready, qT_ps, qT_ready = sem("ones_ready"), sem("kv0_ready"), sem("qT_ps"), sem("qT_ready")
    high_ready, low_ready, low2_ready = sem("high_ready"), sem("low_ready"), sem("low2_ready")
    outer_ready, cum_ps, cq_ready, num_ready, y_ready = (
        sem("outer_ready"), sem("cum_ps"), sem("cq_ready"), sem("num_ready"), sem("y_ready"))
    den_ready, rden_ready, yT_ps, yT_ready, o_ps, o_ready, x_attn = (
        sem("den_ready"), sem("rden_ready"), sem("yT_ps"), sem("yT_ready"), sem("o_ps"), sem("o_ready"), sem("x_attn"))

    ITS = NG // 2

    def from_(g, n):
        return not isinstance(g, int) or g >= n

    def till(g, n):
        return not isinstance(g, int) or g <= n

    def wait_alone(v, s, value):
        v.wait_ge(s, value)
        nc.vector.memset(scrap["vector"], 0.0)

    def wait_alone_pool(pool, s, value):
        pool.wait_ge(s, value)
        nc.gpsimd.tensor_tensor(scrap["pool"], mhalf[0:1, 0:1], mhalf[0:1, 0:1], ALU.add)

    def moments(v, layer, g, p):
        for k in range(GT):
            last = nc.vector.bn_stats(stats[p][:, k, :], x_sb[:, ds(g * GT + k, 1), :])
        last.then_inc(ln_stats[layer], 1)
        if from_(g, 2):
            v.wait_ge(xn_ready[layer], g - 1)
        wait_alone(v, ln_stats[layer], g + 1)
        for k in range(GT):
            last = nc.vector.bn_aggr(mv[p][:, k, :], stats[p][:, k, :])
        last.then_inc(ln_mv[layer], 1)
        v.wait_ge(ln_mv[layer], g + 1)
        nc.vector.tensor_scalar(minus[p][:, :], mv[p][:, :, 0], -1.0, None, ALU.mult)
        nc.vector.tensor_scalar(ve[p][:, :], mv[p][:, :, 1], EPS_LN, None, ALU.add).then_inc(ve_ready[layer], 1)

    def deviation(pool, layer, g, p):
        pool.wait_ge(ve_ready[layer], g + 1)
        nc.gpsimd.tensor_tensor(rstd[p][:, :], ve[p][:, :], mhalf[:, :], ALU.pow).then_inc(rstd_part[layer], 1)
        pool.wait_ge(rstd_part[layer], g + 1)
        nc.gpsimd.tensor_tensor(shift[p][:, :], minus[p][:, :], rstd[p][:, :], ALU.mult).then_inc(rstd_ready[layer], 1)

    def normalise(act, layer, g, p):
        act.wait_ge(rstd_ready[layer], g + 1)
        if from_(g, 2):
            act.wait_ge((xT_ps, xT2_ps)[layer], g - 1)
            if layer == 0:
                act.wait_ge(xn_saved[p], (g // 2) * 16)
        for k in range(GT):
            last = nc.scalar.activation(xn[p][:, k, :], x_sb[:, ds(g * GT + k, 1), :].rearrange("p a d -> p (a d)"),
                                        ACT.Identity, scale=rstd[p][:, k:k + 1], bias=shift[p][:, k:k + 1])
        last.then_inc(xn_ready[layer], 1)

    def xT_tensor(pe, g, p):
        pe.wait_ge(xn_ready[0], g + 1)
        if from_(g, 2):
            pe.wait_ge(xT_ready, g - 1)
        for k in range(GT):
            last = nc.tensor.transpose(ps[p][:, k * P:(k + 1) * P], xn[p][:, k, :], ident)
        last.then_inc(xT_ps, 1)

    def project1_tensor(pe, g, p):
        pe.wait_ge(xT_ready, g + 1)
        for k in range(GT):
            if from_(g, 1):
                pe.wait_ge(qkv_raw, g * GT + k - (GT - 1))
            nc.tensor.matmul(ps[4 + k][:, 0:NQ], xT[p][:, k, :], w_in[:, :], start=True, stop=True
                             ).then_inc(qkv_ps, 1)

    def xT_scalar(act, g, p):
        act.wait_ge(xT_ps, g + 1)
        if from_(g, 2):
            act.wait_ge(qkv_ps, (g - 1) * GT)
        nc.scalar.copy(xT[p][:, :, :].rearrange("p a b -> p (a b)"), ps[p]).then_inc(xT_ready, 1)

    def project1_scalar(act, g, p):
        for k in range(GT):
            act.wait_ge(qkv_ps, g * GT + k + 1)
            nc.scalar.copy(qkv3[:, ds(g * GT + k, 1), 0:NQ].rearrange("p a c -> p (a c)"),
                           ps[4 + k][:, 0:NQ]).then_inc(qkv_raw, 1)

    def batches_of(a, g):
        for b in range(GT // 2):
            yield a[:, ds(g * GT + 2 * b, 2), 0:2 * D].rearrange("p t (h d) -> p t h d", d=DH)

    def by_position(name):
        return const(name).rearrange("p (t d) -> p t d", d=DH).unsqueeze(2).broadcast_to([P, 2, 2 * H, DH])

    def sine(pool, g):
        pool.wait_ge(qkv_raw, g * GT + GT)
        for q, e in zip(batches_of(qkv3, g), batches_of(qk_exp, g)):
            last = nc.gpsimd.tensor_tensor(e, q, by_position("sin"), ALU.mult)
        last.then_inc(sine_ready, 1)

    def rotate(eng, multiply_add, g):
        eng.wait_ge(sine_ready, g + 1)
        for q in batches_of(qkv3, g):
            last = multiply_add(q, q, by_position("cos"), ALU.mult)
        last.then_inc(cosine_ready, 1)
        eng.wait_ge(cosine_ready, g + 1)
        half = DH // 2
        q = qkv3[:, ds(g * GT, GT), 0:2 * D].rearrange("p t (h d) -> p t h d", d=DH)
        e = qk_exp[:, ds(g * GT, GT), :].rearrange("p t (h d) -> p t h d", d=DH)
        for f in range(2):
            a = q[:, :, :, f * half:(f + 1) * half]
            last = multiply_add(a, a, e[:, :, :, (1 - f) * half:(2 - f) * half], ALU.add)
        last.then_inc(rot_ready, 1)

    def exp_relu(act, g):
        act.wait_ge(rot_ready, g + 1)
        q, e = qkv3[:, ds(g * GT, GT), 0:2 * D], qk_exp[:, ds(g * GT, GT), :]
        nc.scalar.activation(e, q, ACT.Exp).then_inc(exp_part, 1)
        act.wait_ge(exp_part, g + 1)
        nc.scalar.activation(q, q, ACT.Relu).then_inc(phi_parts, 1)

    SINE_LAG, LAG = 3, 4
    BY_VECTOR = NG + 1 - LAG

    def front(eng, step):
        for x in range(4):
            step(eng, x, x % 2)
        with eng.Fori(2, ITS - 1) as it:
            for p in range(2):
                step(eng, it * 2 + p, p)
        for x in range(NG - 2, NG + 1):
            step(eng, x, x % 2)

    def before_end(x):
        return not isinstance(x, int) or x < NG

    def front_tensor(pe, x, p):
        if before_end(x):
            xT_tensor(pe, x, p)
        if from_(x, 1):
            project1_tensor(pe, x - 1, 1 - p)

    def front_scalar(act, x, p):
        if before_end(x):
            xT_scalar(act, x, p)
        if till(x, NG - 2):
            normalise(act, 0, x + 1, 1 - p)
        if from_(x, 1):
            project1_scalar(act, x - 1, 1 - p)

    def front_vector(v, x, p):
        if isinstance(x, int) and x < len(X_PARTS):
            v.wait_ge(x_loaded[x], 16)
        if before_end(x):
            moments(v, 0, x, p)
        if from_(x, LAG):
            rotate(v, nc.vector.tensor_tensor, x - LAG)

    def front_pool(pool, x, p):
        if before_end(x):
            deviation(pool, 0, x, p)
        if from_(x, SINE_LAG):
            sine(pool, x - SINE_LAG)

    SPI = 4
    SHIFT = 8

    def gather(pool, j):
        n = j % NX
        if j >= NX:
            pool.wait_ge(xgT_ps, j - NX + 1)
        pool.indirect_dma_start(out=xg[n][:, :], out_offset=None, in_=xn_dram,
                                in_offset=bass.IndirectOffsetOnAxis(ap=slot_tok[:, j:j + 1], axis=0)
                                ).then_inc(xg_in[n], 16)

    def scatter(pool, j):
        n = j % NX
        pool.wait_ge(ye_ready, j + 1)
        pool.indirect_dma_start(out=y_dram, out_offset=bass.IndirectOffsetOnAxis(ap=slot_dst[:, j:j + 1], axis=0),
                                in_=ye[n][:, :], in_offset=None).then_inc(ye_out[n], 16)

    def slot(base, s):
        return base + s

    def load_w1(sp, base, s, e):
        j, n = slot(base, s), s % NX
        if from_(j, NX):
            sp.wait_ge(up_ps, j - NX + 1)
        sp.dma_start(w1[n][:, :], W1[ds(e, 1), :, :].rearrange("a f h -> f (a h)")).then_inc(w1_in[n], 16)

    def xg_transpose(pe, base, s):
        j, n = slot(base, s), s % NX
        pe.wait_ge(xg_in[n], (base // NX + s // NX + 1) * 16)
        if from_(j, 1):
            pe.wait_ge(xgT_ready, j)
        nc.tensor.transpose(ps[6][:, 0:P], xg[n][:, :], ident).then_inc(xgT_ps, 1)

    def up(pe, base, s):
        j, p, n = slot(base, s), s % 2, s % NX
        pe.wait_ge(w1_in[n], (base // NX + s // NX + 1) * 16)
        pe.wait_ge(xgT_ready, j + 1)
        if from_(j, 2):
            pe.wait_ge(gelu_ready, j - 1)
        for c in range(NC):
            last = nc.tensor.matmul(ps[3 + p][:, c * P:(c + 1) * P], w1[n][:, c * P:(c + 1) * P], xgT[p][:, :],
                                    start=True, stop=True)
        last.then_inc(up_ps, 1)

    def down(pe, base, s, e):
        j, p = slot(base, s), s % 2
        pe.wait_ge(gelu_ready, j + 1)
        if from_(j, 1):
            pe.wait_ge(ye_ready, j)
        y = ps[7][:, 0:D]
        nc.tensor.matmul(y, ones_bf[0:3, :], bias3[:, ds(e * D, D)], start=True, stop=False)
        for c in range(NC):
            last = nc.tensor.matmul(y, hidT[p][:, c, :], w2_sb[:, ds(e * NC + c, 1), :],
                                    start=False, stop=(c == NC - 1))
        last.then_inc(down_ps, 1)

    def xgT_copy(act, base, s):
        j, p = slot(base, s), s % 2
        act.wait_ge(xgT_ps, j + 1)
        if from_(j, 2):
            act.wait_ge(up_ps, j - 1)
        nc.scalar.copy(xgT[p][:, :], ps[6][:, 0:P]).then_inc(xgT_ready, 1)

    def gelu(act, base, s, e):
        j, p = slot(base, s), s % 2
        act.wait_ge(up_ps, j + 1)
        if from_(j, 2):
            act.wait_ge(down_ps, j - 1)
        for c in range(NC):
            last = nc.scalar.activation(hidT[p][:, c, :], ps[3 + p][:, c * P:(c + 1) * P], ACT.Gelu_apprx_tanh,
                                        bias=b1T[:, ds(e * NC + c, 1)])
        last.then_inc(gelu_ready, 1)

    def out_copy(act, base, s):
        j, n = slot(base, s), s % NX
        act.wait_ge(down_ps, j + 1)
        if from_(j, NX):
            act.wait_ge(ye_out[n], (base // NX + s // NX) * 16)
        nc.scalar.copy(ye[n][:, :], ps[7][:, 0:D]).then_inc(ye_ready, 1)

    def some(base, s):
        return not isinstance(base, int) or 0 <= base + s < NS

    def expert_tensor(pe, base, s, expert, between=None):
        if some(base, s + 2):
            xg_transpose(pe, base, s + 2)
        if some(base, s + 1):
            up(pe, base, s + 1)
        if between:
            between()
        if some(base, s):
            down(pe, base, s, expert(base + s))

    def expert_scalar(act, base, s, expert, between=None):
        if some(base, s + 2):
            xgT_copy(act, base, s + 2)
        if some(base, s + 1):
            gelu(act, base, s + 1, expert(base + (s + 1)))
        if between:
            between()
        if some(base, s):
            out_copy(act, base, s)

    def phi(v, b, p):
        if from_(b, 2):
            v.wait_ge(cum_ps, b * 2 - 2)
            v.wait_ge(qT_ps, b - 1)
        nc.vector.scalar_tensor_tensor(out=phib[p][:, :, :], in0=qk_exp[:, ds(b * 2, 2), :], scalar=1.0,
                                       in1=qkv3[:, ds(b * 2, 2), 0:2 * D], op0=ALU.min, op1=ALU.add).then_inc(phi_ready, 1)

    def attn_outer(v, b, r, p):
        i = b * 2 + r
        k = phib[p][:, r, D:2 * D].rearrange("p (h d) -> p h d", d=DH)
        vv = qkv3[:, ds(i, 1), 2 * D:3 * D].rearrange("p a (h e) -> p (a h) e", e=DH)
        if from_(b, 1):
            v.wait_ge(cum_ps, b * 2 - 1 + r)
        if r == 0:
            v.wait_ge(phi_ready, b + 1)
        nc.vector.tensor_tensor(outer[r].rearrange("p (h d e) -> p h d e", d=DH, e=DH),
                                k.unsqueeze(3).broadcast_to([P, H, DH, DH]),
                                vv.unsqueeze(2).broadcast_to([P, H, DH, DH]), ALU.mult).then_inc(outer_ready, 1)

    def attn_high(act, i, r):
        act.wait_ge(outer_ready, i + 1)
        if from_(i, 2):
            act.wait_ge(cum_ps, i - 1)
        nc.scalar.copy(high[r], outer[r]).then_inc(high_ready, 1)

    def attn_low(v, i, r):
        v.wait_ge(high_ready, i + 1)
        if from_(i, 2):
            v.wait_ge(cum_ps, i - 1)
        nc.vector.tensor_tensor(low[r][:, 0:HALF], outer[r][:, 0:HALF], high[r][:, 0:HALF].bitcast(f32), ALU.subtract
                                ).then_inc(low_ready, 1)

    def attn_low_pool(pool, i, r):
        pool.wait_ge(high_ready, i + 1)
        nc.gpsimd.tensor_tensor(low[r][:, HALF:], outer[r][:, HALF:], high[r][:, HALF:].bitcast(f32), ALU.subtract
                                ).then_inc(low2_ready, 1)

    def attn_cumsum(pe, b, r, p):
        i = b * 2 + r
        pe.wait_ge(outer_ready, i + 1)
        if from_(i, 1):
            pe.wait_ge(cq_ready, i * 2)
        pe.wait_ge(low_ready, i + 1)
        pe.wait_ge(low2_ready, i + 1)
        for half in range(2):
            cols = slice(half * HALF, (half + 1) * HALF)
            nc.tensor.matmul(ps[half], tri_r[:, :], high[r][:, cols], start=True, stop=False)
            nc.tensor.matmul(ps[half], tri_r[:, :], low[r][:, cols], start=False, stop=True)
        nc.tensor.matmul(ps[2][:, 0:D], const("tri_incl"), phib[p][:, r, D:2 * D], start=True, stop=True)
        if r == 0:
            nc.tensor.matmul(ps[2][:, D:D + DA], phib[p][:, 0, D:2 * D], qkv3[:, ds(i, 1), 2 * D:NW],
                             start=True, stop=True).then_inc(cum_ps, 1)
        else:
            pe.wait_ge(kv0_ready, b + 1)
            pe.wait_ge(qT_ready, b + 1)
            nc.tensor.matmul(ps[2][:, D:D + DA], qT[:, :], kv0[:, :], start=True, stop=True).then_inc(cum_ps, 1)

    def attn_apply(v, b, r, p):
        i = b * 2 + r
        v.wait_ge(cum_ps, i + 1)
        if r == 0:
            nc.vector.tensor_tensor(kv0[:, :], ps[2][:, D:D + DA], const("head_mask"), ALU.mult).then_inc(kv0_ready, 1)
        else:
            nc.vector.tensor_copy(cqk[:, :, DH], ps[2][:, 2 * D:D + DA])
            nc.vector.tensor_copy(cq4[:, :, DH, :], ps[2][:, D:2 * D].rearrange("p (h e) -> p h e", e=DH))
        q = phib[p][:, r, 0:D].rearrange("p (h d) -> p h d", d=DH)
        nc.vector.tensor_tensor(cqk[:, :, 0:DH], ps[2][:, 0:D].rearrange("p (h d) -> p h d", d=DH), q, ALU.mult
                                ).then_inc(cq_ready, 1)
        for half in range(2):
            heads = slice(half * H // 2, (half + 1) * H // 2)
            last = nc.vector.tensor_tensor(cq4[:, heads, 0:DH, :], ps[half].rearrange("p (h d e) -> p h d e", d=DH, e=DH),
                                           q[:, heads, :].unsqueeze(3).broadcast_to([P, H // 2, DH, DH]), ALU.mult)
        last.then_inc(cq_ready, 1)

    def attn_divide(v, i, r):
        rows = DH + r
        v.wait_ge(cq_ready, i * 2 + 1)
        nc.vector.tensor_reduce(den, cqk[:, :, 0:rows], AX.X, ALU.add).then_inc(den_ready, 1)
        v.wait_ge(den_ready, i * 2 + 1)
        nc.vector.tensor_scalar(den, den, EPS_DEN, None, ALU.max).then_inc(den_ready, 1)
        v.wait_ge(den_ready, i * 2 + 2)
        nc.vector.reciprocal(rden, den).then_inc(rden_ready, 1)
        v.wait_ge(cq_ready, i * 2 + 2)
        nc.vector.tensor_reduce(num.rearrange("p (h e) -> p h e", e=DH), cq4[:, :, 0:rows, :].rearrange("p h d e -> p h e d"),
                                AX.X, ALU.add).then_inc(num_ready, 1)
        v.wait_ge(num_ready, i + 1)
        v.wait_ge(rden_ready, i + 1)
        if from_(i, 1):
            v.wait_ge(yT_ps, i)
        nc.vector.tensor_tensor(y_tok.rearrange("p (h e) -> p h e", e=DH), num.rearrange("p (h e) -> p h e", e=DH),
                                rden.unsqueeze(2).broadcast_to([P, H, DH]), ALU.mult).then_inc(y_ready, 1)

    def q_transpose(pe, b, p):
        pe.wait_ge(phi_ready, b + 1)
        if from_(b, 1):
            pe.wait_ge(o_ready, b * 2 - 1)
        nc.tensor.transpose(ps[5][:, 0:P], phib[p][:, 1, 0:D], ident).then_inc(qT_ps, 1)

    def qT_copy(act, b):
        act.wait_ge(qT_ps, b + 1)
        if from_(b, 1):
            act.wait_ge(cum_ps, b * 2)
        nc.scalar.copy(qT[:, :], ps[5][:, 0:P]).then_inc(qT_ready, 1)

    def attn_transpose(pe, i, b, r):
        pe.wait_ge(y_ready, i + 1)
        if from_(i, 1):
            pe.wait_ge(o_ready, i)
        if r == 0:
            pe.wait_ge(qT_ready, b + 1)
        nc.tensor.transpose(ps[5][:, 0:P], y_tok, ident).then_inc(yT_ps, 1)

    def attn_project(pe, i):
        pe.wait_ge(yT_ready, i + 1)
        nc.tensor.matmul(ps[5][:, 0:D], yT0, wT[:, 0, :], start=True, stop=True).then_inc(o_ps, 1)

    def attn_yT(act, i):
        act.wait_ge(yT_ps, i + 1)
        if from_(i, 1):
            act.wait_ge(o_ps, i)
        nc.scalar.copy(yT0, ps[5][:, 0:P]).then_inc(yT_ready, 1)

    def attn_o(act, i):
        act.wait_ge(o_ps, i + 1)
        if from_(i, 1):
            act.wait_ge(x_attn, i)
        nc.scalar.copy(o_tok, ps[5][:, 0:D]).then_inc(o_ready, 1)

    def steps(eng, expert_step, even, odd, first=None):
        def step(b, base, s, p):
            part, r = (even, odd)[s % 2], s // 2
            expert_step(eng, base, s, between=lambda: part(b, r, b * 2 + r, p))
        for s in range(-2, SHIFT):
            expert_step(eng, 0, s)
            if first and s == SHIFT - 3:
                first()
        for b in range(2):
            for s in range(SPI):
                step(b, b * SPI + SHIFT, s, b)
        with eng.Fori(1, B // 2 - 1) as bb:
            for p in range(2):
                for s in range(SPI):
                    step(bb * 2 + p, (bb * 2 + p) * SPI + SHIFT, s, p)
        for b in range(B - 2, max(B + 1, -((SHIFT - NS) // SPI))):
            for s in range(SPI):
                step(b, b * SPI + SHIFT, s, b % 2)

    def attn_add(pool, i):
        pool.wait_ge(o_ready, i + 1)
        nc.gpsimd.tensor_tensor(x_sb[:, i, :], o_tok, x_sb[:, i, :], ALU.add).then_inc(x_attn, 1)

    at = [0]

    def view(n):
        at[0] += n
        return qkv[:, at[0] - n:at[0]]

    GP = GT * P
    y_moe = qk_exp[:, :, :].rearrange("p n (k c) -> p n k c", k=TOPK)
    xT2 = [view(2 * (T + 1)) for _ in range(2)]
    mix_t = [[view(GP) for _ in range(2)] for _ in range(2)]
    e_q, r_q, phi_q = view(GP), view(GP), view(GP)
    e_k, r_k, phi_k = view(GP), view(GP), view(GP)
    v_aug = view(GT * DA).rearrange("p (n c) -> p n c", c=DA)
    kvm = view(2 * DA).rearrange("p (b c) -> p b c", c=DA)
    rcp = view(GT * H).rearrange("p (n h) -> p n h", h=H)
    y1 = view(GP)
    yT1 = view(GP)
    tanh_r = view(GP)
    k_relu, k_act = view(GP), view(GP)
    res = [outer[p][:, 0:GP] for p in range(2)]
    assert at[0] <= NT * NW
    kv_bank = ps_all[:, 2 * 512:4 * 512].rearrange("p (n c) -> p n c", c=2 * D)
    nd_bank = ps_all[:, 6 * 512:8 * 512].rearrange("p (n c) -> p n c", c=256)
    Y_PARTS = ((0, 1), (1, 2), (2, 4), (4, NG))
    y_in = [sem(f"y_in{n}") for n in range(len(Y_PARTS))]
    y_part, x1_part, x1_ready = sem("y_part"), sem("x1_part"), sem("x1_ready")
    xT2_ps, xT2_ready, mu_x, mixed = sem("xT2_ps"), sem("xT2_ready"), sem("mu_x"), sem("mixed")
    q_ps, kv_ps, r_ps, kf_ps = sem("q_ps"), sem("kv_ps"), sem("r_ps"), sem("kf_ps")
    qparts, kparts, v_ready = sem("qparts"), sem("kparts"), sem("v_ready")
    phiq_ready, phik_ready, kact_ready = sem("phiq_ready"), sem("phik_ready"), sem("kact_ready")
    relu_ready = sem("relu_ready")
    KV_ps, KV_ready, nd_ps, rcp_ready, y1_ready = sem("KV_ps"), sem("KV_ready"), sem("nd_ps"), sem("rcp_ready"), sem("y1_ready")
    yT1_ps, yT1_ready = sem("yT1_ps"), sem("yT1_ready")
    tanh_ready, vf_ps, pr_ps = sem("tanh_ready"), sem("vf_ps"), sem("pr_ps")
    ffn_ready, rest_ready, res_ready = sem("ffn_ready"), sem("rest_ready"), sem("res_ready")
    out_done = [sem("out_done0"), sem("out_done1")]
    pads = sem("pads")

    def x1_of(g):
        return x_sb[:, ds(g * GT, GT), :].rearrange("p a c -> p (a c)")

    def wait_y(g):
        return y_in[next(n for n, (lo, hi) in enumerate(Y_PARTS) if hi > (g if isinstance(g, int) else 4))]

    def combine(v, g, p):
        v.wait_ge(wait_y(g), 16)
        for k in range(TOPK):
            for n in range(GT):
                last = nc.vector.scalar_tensor_tensor(
                    out=x_sb[:, g * GT + n, :], in0=y_moe[:, g * GT + n, k, :],
                    scalar=sel[k][:, g * GT + n:g * GT + n + 1], in1=x_sb[:, g * GT + n, :], op0=ALU.mult, op1=ALU.add)
            last.then_inc(x1_part if k == 0 else x1_ready, 1)
            v.wait_ge(x1_part if k == 0 else x1_ready, g + 1)
            if k:
                nc.vector.memset(scrap["vector"], 0.0)

    def combine_pool(pool, g, p):
        pool.wait_ge(wait_y(g), 16)
        y = y_moe[:, ds(g * GT, GT), :, :]
        for k in range(TOPK):
            last = nc.gpsimd.tensor_tensor(y[:, :, k, :], y[:, :, k, :],
                                           sel[k][:, ds(g * GT, GT)].unsqueeze(2).broadcast_to([P, GT, D]), ALU.mult)
        last.then_inc(y_part, 1)
        wait_alone_pool(pool, y_part, g - 1)
        x1 = x_sb[:, ds(g * GT, GT), :]
        nc.gpsimd.tensor_tensor(x1, y[:, :, 0, :], x1, ALU.add).then_inc(x1_part, 1)
        wait_alone_pool(pool, x1_part, g + 1)
        nc.gpsimd.tensor_tensor(x1, y[:, :, 1, :], x1, ALU.add).then_inc(x1_ready, 1)

    def xT2_transpose(pe, g, p):
        pe.wait_ge(xn_ready[1], g + 1)
        if from_(g, 1):
            pe.wait_ge(xT2_ready, g)
        if from_(g, 3):
            pe.wait_ge(yT1_ready, g - 2)
        for n in range(GT):
            last = nc.tensor.transpose(ps[1][:, n * P:(n + 1) * P], xn[p][:, n, :], ident)
        last.then_inc(xT2_ps, 1)

    def xT2_of(p):
        return xT2[p].rearrange("p (b t) -> p b t", t=T + 1)

    def xT2_copy(act, g, p):
        act.wait_ge(xT2_ps, g + 1)
        if from_(g, 2):
            act.wait_ge(q_ps, g - 1)
            act.wait_ge(mixed, g - 1)
        nc.scalar.copy(xT2_of(p)[:, :, 1:T + 1], ps[1].rearrange("p (b t) -> p b t", t=T)).then_inc(xT2_ready, 1)

    def mu_scalar(act, g, p):
        act.wait_ge(xT2_ready, g + 1)
        if from_(g, 2):
            act.wait_ge(kf_ps, g - 1)
        for m in range(2):
            last = nc.scalar.activation(mix_t[p][m].rearrange("p (b t) -> p b t", t=T), xT2_of(p)[:, :, 1:T + 1],
                                        ACT.Copy, scale=mu[:, m:m + 1])
        last.then_inc(mu_x, 1)

    def mix(v, g, p):
        v.wait_ge(mu_x, g + 1)
        for m in range(2):
            t = mix_t[p][m].rearrange("p (b t) -> p b t", t=T)
            last = nc.vector.scalar_tensor_tensor(out=t, in0=xT2_of(p)[:, :, 0:T], scalar=one_mu[:, m:m + 1],
                                                  in1=t, op0=ALU.mult, op1=ALU.add)
        last.then_inc(mixed, 1)

    def phi_k_vector(v, g):
        v.wait_ge(kparts, g + 1)
        if from_(g, 1):
            v.wait_ge(KV_ps, g)
        nc.vector.scalar_tensor_tensor(out=phi_k, in0=e_k, scalar=1.0, in1=r_k, op0=ALU.min, op1=ALU.add
                                       ).then_inc(phik_ready, 1)

    def phi_q_vector(v, g):
        v.wait_ge(qparts, g + 1)
        if from_(g, 1):
            v.wait_ge(nd_ps, g)
        nc.vector.scalar_tensor_tensor(out=phi_q, in0=e_q, scalar=1.0, in1=r_q, op0=ALU.min, op1=ALU.add
                                       ).then_inc(phiq_ready, 1)

    def square_keys(v, g):
        v.wait_ge(relu_ready, g + 1)
        if from_(g, 1):
            v.wait_ge(vf_ps, g)
        nc.vector.tensor_tensor(k_act, k_relu, k_relu, ALU.mult).then_inc(kact_ready, 1)

    def mask_KV(v, g):
        v.wait_ge(KV_ps, g + 1)
        if from_(g, 1):
            v.wait_ge(nd_ps, g)
        nc.vector.tensor_tensor(kvm, ps[0].rearrange("p (b c) -> p b c", b=2)[:, :, 0:DA],
                                const("head_mask").unsqueeze(1).broadcast_to([P, 2, DA]), ALU.mult
                                ).then_inc(KV_ready, 1)

    def divide(v, g):
        v.wait_ge(nd_ps, g + 1)
        nc.vector.reciprocal(rcp, nd_bank[:, :, D:DA]).then_inc(rcp_ready, 1)
        v.wait_ge(rcp_ready, g + 1)
        if from_(g, 1):
            v.wait_ge(yT1_ps, g)
        nc.vector.tensor_tensor(y1.rearrange("p (n h d) -> p n h d", h=H, d=DH),
                                nd_bank[:, :, 0:D].rearrange("p n (h d) -> p n h d", d=DH),
                                rcp.unsqueeze(3).broadcast_to([P, GT, H, DH]), ALU.mult).then_inc(y1_ready, 1)

    def ffn(v, g, p):
        v.wait_ge(vf_ps, g + 1)
        v.wait_ge(tanh_ready, g + 1)
        if from_(g, 2):
            v.wait_ge(out_done[p], g // 2 * 16)
        nc.vector.scalar_tensor_tensor(out=res[p], in0=tanh_r, scalar=1.0, in1=ps[5], op0=ALU.add, op1=ALU.mult
                                       ).then_inc(ffn_ready, 1)

    def add_x1(pool, g, p):
        pool.wait_ge(ffn_ready, g + 1)
        nc.gpsimd.tensor_tensor(res[p], res[p], x1_of(g), ALU.add).then_inc(rest_ready, 1)

    def finish(v, g, p):
        v.wait_ge(rest_ready, g + 1)
        v.wait_ge(pr_ps, g + 1)
        nc.vector.tensor_tensor(res[p], ps[4], res[p], ALU.add).then_inc(res_ready, 1)

    def k_scalar(act, g):
        act.wait_ge(kv_ps, g + 1)
        if from_(g, 1):
            act.wait_ge(phik_ready, g)
            act.wait_ge(KV_ps, g)
        nc.scalar.activation(e_k.rearrange("p (n c) -> p n c", c=D), kv_bank[:, :, 0:D], ACT.Exp)
        nc.scalar.activation(r_k.rearrange("p (n c) -> p n c", c=D), kv_bank[:, :, 0:D], ACT.Relu).then_inc(kparts, 1)
        nc.scalar.copy(v_aug[:, :, 0:D], kv_bank[:, :, D:2 * D]).then_inc(v_ready, 1)

    def q_scalar(act, g):
        act.wait_ge(q_ps, g + 1)
        if from_(g, 1):
            act.wait_ge(phiq_ready, g)
        nc.scalar.activation(e_q, ps[7], ACT.Exp)
        nc.scalar.activation(r_q, ps[7], ACT.Relu).then_inc(qparts, 1)

    def yT1_copy(act, g):
        act.wait_ge(yT1_ps, g + 1)
        if from_(g, 1):
            act.wait_ge(pr_ps, g)
        nc.scalar.copy(yT1, ps[1]).then_inc(yT1_ready, 1)

    def keys_scalar(act, g):
        act.wait_ge(kf_ps, g + 1)
        if from_(g, 1):
            act.wait_ge(kact_ready, g)
        nc.scalar.activation(k_relu, ps[5], ACT.Relu).then_inc(relu_ready, 1)

    def gate_scalar(act, g):
        act.wait_ge(r_ps, g + 1)
        if from_(g, 1):
            act.wait_ge(ffn_ready, g)
        nc.scalar.activation(tanh_r, ps[4], ACT.Tanh, scale=0.5).then_inc(tanh_ready, 1)

    def kv_tensor(pe, g, p):
        pe.wait_ge(xT2_ready, g + 1)
        if from_(g, 1):
            pe.wait_ge(v_ready, g)
        for n in range(GT):
            last = nc.tensor.matmul(kv_bank[:, n, :], xT2_of(p)[:, n // 2, 1 + (n % 2) * P:1 + (n % 2) * P + P],
                                    wqkv2[:, D:3 * D], start=True, stop=True)
        last.then_inc(kv_ps, 1)

    def q_tensor(pe, g, p):
        if from_(g, 1):
            pe.wait_ge(y1_ready, g)
        nc.tensor.matmul(ps[7], wqkv2[:, 0:D], xT2_of(p)[:, :, 1:T + 1], start=True, stop=True).then_inc(q_ps, 1)

    def y1_transpose(pe, g):
        pe.wait_ge(y1_ready, g + 1)
        pe.wait_ge(xT2_ready, min(g + 3, NG) if isinstance(g, int) else g + 3)
        for n in range(GT):
            last = nc.tensor.transpose(ps[1][:, n * P:(n + 1) * P], y1[:, n * P:(n + 1) * P], ident)
        last.then_inc(yT1_ps, 1)

    def rk_tensor(pe, g, p):
        pe.wait_ge(mixed, g + 1)
        if from_(g, 1):
            pe.wait_ge(tanh_ready, g)
        if from_(g, 2):
            pe.wait_ge(res_ready, g - 1)
        for n in range(GT):
            last = nc.tensor.matmul(ps[4][:, n * P:(n + 1) * P], mix_t[p][0][:, n * P:(n + 1) * P], wT[:, 1, :],
                                    start=True, stop=True)
        last.then_inc(r_ps, 1)
        if from_(g, 1):
            pe.wait_ge(ffn_ready, g)
        nc.tensor.matmul(ps[5], wT[:, 2, :], mix_t[p][1], start=True, stop=True).then_inc(kf_ps, 1)

    def project2_tensor(pe, g):
        pe.wait_ge(yT1_ready, g + 1)
        pe.wait_ge(tanh_ready, min(g + 2, NG) if isinstance(g, int) else g + 2)
        for n in range(GT):
            o = ps[4][:, n * P:(n + 1) * P]
            nc.tensor.matmul(o, yT1[:, n * P:(n + 1) * P], wproj[:, :], start=True, stop=False)
            last = nc.tensor.matmul(o, ones_bf[0:3, :], bias3[:, BIASP:BIASP + D], start=False, stop=True)
        last.then_inc(pr_ps, 1)

    def KV_tensor(pe, g):
        pe.wait_ge(phik_ready, g + 1)
        pe.wait_ge(v_ready, g + 1)
        if from_(g, 1):
            pe.wait_ge(KV_ready, g)
        for b in range(2):
            for r in range(2):
                n = 2 * b + r
                last = nc.tensor.matmul(ps[0][:, b * 256:b * 256 + DA], phi_k[:, n * D:(n + 1) * D],
                                        v_aug[:, n, :], start=(r == 0), stop=(r == 1))
        last.then_inc(KV_ps, 1)

    def values_tensor(pe, g):
        pe.wait_ge(kact_ready, g + 1)
        for n in range(GT):
            last = nc.tensor.matmul(ps[5][:, n * P:(n + 1) * P], k_act[:, n * P:(n + 1) * P], wT[:, 3, :],
                                    start=True, stop=True)
        last.then_inc(vf_ps, 1)

    def nd_tensor(pe, g):
        pe.wait_ge(KV_ready, g + 1)
        pe.wait_ge(phiq_ready, g + 1)
        if from_(g, 1):
            pe.wait_ge(y1_ready, g)
        for n in range(GT):
            last = nc.tensor.matmul(nd_bank[:, n, 0:DA], phi_q[:, n * P:(n + 1) * P], kvm[:, n // 2, :],
                                    start=True, stop=True)
        last.then_inc(nd_ps, 1)

    def group_tensor(pe, g, p):
        kv_tensor(pe, g, p)
        rk_tensor(pe, g, p)
        if till(g, NG - 2):
            xT2_transpose(pe, g + 1, 1 - p)
        q_tensor(pe, g, p)
        KV_tensor(pe, g)
        if from_(g, 1):
            y1_transpose(pe, g - 1)
        values_tensor(pe, g)
        if from_(g, 1):
            project2_tensor(pe, g - 1)
        nd_tensor(pe, g)

    def group_vector(v, g, p):
        phi_k_vector(v, g)
        square_keys(v, g)
        phi_q_vector(v, g)
        mask_KV(v, g)
        if till(g, NG - 3):
            wait_alone(v, x1_ready, g + 3)
            moments(v, 1, g + 2, p)
        ffn(v, g, p)
        if till(g, NG - 2):
            mix(v, g + 1, 1 - p)
        if from_(g, 1):
            finish(v, g - 1, 1 - p)
        divide(v, g)

    def group_scalar(act, g, p):
        if till(g, NG - 2):
            normalise(act, 1, g + 1, 1 - p)
        k_scalar(act, g)
        keys_scalar(act, g)
        gate_scalar(act, g)
        if till(g, NG - 2):
            xT2_copy(act, g + 1, 1 - p)
        q_scalar(act, g)
        if from_(g, 1):
            yT1_copy(act, g - 1)
        if till(g, NG - 2):
            mu_scalar(act, g + 1, 1 - p)

    def group_pool(pool, g, p):
        if till(g, NG - 3):
            combine_pool(pool, g + 2, p)
            deviation(pool, 1, g + 2, p)
        add_x1(pool, g, p)

    def groups(eng, group):
        for g in range(2):
            group(eng, g, g)
        with eng.Fori(1, ITS - 1) as it:
            for p in range(2):
                group(eng, it * 2 + p, p)
        for g in range(NG - 2, NG):
            group(eng, g, g % 2)


    def expert_of(eng):
        reg = eng.alloc_register("expert")

        def expert(j):
            eng.reg_load(reg, slot_exp[0:1, ds(j, 1)])
            return eng.snap(reg, min_val=0, max_val=NE - 1)
        return expert

    with nc.Block() as block:
        @block.sync
        def _(sp):
            def load_x(n):
                lo, hi = X_PARTS[n]
                sp.dma_start(x_sb[:, lo:hi, :],
                             x_in.rearrange("b t d -> (b t) d").rearrange("(n p) d -> p n d", p=P)[:, lo:hi, :]
                             ).then_inc(x_loaded[n], 16)
            load_x(0)
            load_x(1)
            sp.wait_ge(wts_in, 16 * 4)
            load_x(2)
            load_x(3)
            for n, w in enumerate((Wo, W_r, W_k, W_v)):
                sp.dma_start(w_raw[:, 3 + n, :], w).then_inc(w_late_in, 16)
            sp.dma_start(w_raw[0:NE * NC, 7, :], b1.rearrange("e (c p) -> (e c) p", p=P)).then_inc(w_late_in, 16)
            sp.dma_start(bg_sb[:, :], bg.rearrange("(a e) -> a e", a=1).broadcast_to([P, NE])).then_inc(bias_in, 16)
            sp.dma_start(bias_sp[:, 0:BIASP // P], b2.rearrange("e h -> (e h)").rearrange("(p c) -> p c", p=P)).then_inc(bias_in, 16)
            sp.dma_start(bias_sp[:, BIASP // P:NBIAS // P], b_proj.rearrange("(p c) -> p c", p=P)).then_inc(bias_in, 16)
            sp.dma_start(mu[:, 0:1], mu_r.rearrange("(p c) -> p c", p=P)).then_inc(bias_in, 16)
            sp.dma_start(mu[:, 1:2], mu_k.rearrange("(p c) -> p c", p=P)).then_inc(bias_in, 16)

            def save(it):
                for p in range(2):
                    g = it * 2 + p
                    sp.wait_ge(xn_ready[0], g + 1)
                    sp.dma_start(xn_dram.rearrange("(n p) d -> p n d", p=P)[:, ds(g * GT, GT), :], xn[p][:, :, :]
                                 ).then_inc(xn_saved[p], 16)
            save(0)
            sp.dma_start(wqkv2[:, :], w_qkv).then_inc(late_in, 16)
            sp.dma_start(wproj[:, :], w_proj).then_inc(late_in, 16)
            sp.dma_start(w2_sb[:, :, :], W2.rearrange("e (c p) f -> p (e c) f", p=P)).then_inc(late_in, 16)
            with sp.Fori(1, ITS) as it:
                save(it)
            sp.wait_ge(bias_split, 5)
            for n in range(3):
                for lo, hi in ((0, BIASP), (BIASP, NBIAS)):
                    sp.dma_start(bias3[n:n + 1, lo:hi].rearrange("a (p c) -> a p c", p=P),
                                 bias_part[:, n, lo // P:hi // P]).then_inc(bias_rows, 16)
            sp.wait_ge(exp_ready, 1)
            expert = expert_of(sp)
            for s in range(NX):
                load_w1(sp, 0, s, expert(s))
            with sp.Fori(1, NS // NX) as it:
                for s in range(NX):
                    load_w1(sp, it * NX, s, expert(it * NX + s))
            for j in range(NS // NX * NX, NS):
                load_w1(sp, j - j % NX, j % NX, expert(j))
            for n in range(NX):
                sp.wait_ge(ye_out[n], 16 * len(range(n, NS, NX)))
            sp.wait_ge(phi_ready, B)
            for n, (lo, hi) in enumerate(Y_PARTS):
                sp.dma_start(y_moe[:, lo * GT:hi * GT, :, :].rearrange("p n k c -> p n (k c)"),
                             y_dram[0:TOK * TOPK, :].rearrange("(n p k) d -> p n (k d)", p=P, k=TOPK)[:, lo * GT:hi * GT, :]
                             ).then_inc(y_in[n], 16)

            def save_out(g, p):
                sp.wait_ge(res_ready, g + 1)
                sp.dma_start(out.rearrange("b t d -> (b t) d").rearrange("(n p) d -> p n d", p=P)[:, ds(g * GT, GT), :],
                             res[p].rearrange("p (n d) -> p n d", n=GT)).then_inc(out_done[p], 16)
            with sp.Fori(0, ITS) as it:
                for p in range(2):
                    save_out(it * 2 + p, p)
            for p in range(2):
                sp.wait_ge(out_done[p], 16 * ITS)

        @block.scalar
        def _(act):
            act.dma_start(cst[:, :], consts).then_inc(consts_in, 16)
            for n, w in enumerate((Wq, Wk, Wv)):
                act.dma_start(w_raw[:, n, :], w).then_inc(wts_in, 16)
            act.dma_start(w_in[:, 3 * D:NQ], Wg).then_inc(wts_in, 16)
            act.wait_ge(wT_ps, 1)
            nc.scalar.copy(w_in[:, 0:3 * D], ps[4][:, 0:3 * P]).then_inc(wT_ready, 1)
            normalise(act, 0, 0, 0)
            front(act, front_scalar)
            act.wait_ge(w_late_ps, 1)
            nc.scalar.copy(wT[:, 0:3, :].rearrange("p a b -> p (a b)"), ps[4][:, 0:3 * P])
            nc.scalar.activation(wT[:, 3, :], ps[4][:, 3 * P:4 * P], ACT.Copy, scale=0.5)
            nc.scalar.copy(b1T[:, :], ps[5][:, 0:NE * NC]).then_inc(w_late_ready, 1)
            for g in range(NG - 1):
                if g == BY_VECTOR:
                    act.wait_ge(gate_in, 1)
                    nc.scalar.activation(rt[3], rt[3], ACT.Exp).then_inc(gate_exp, 1)
                exp_relu(act, g)

            def by_row(it):
                for p in range(2):
                    g = it * 2 + p
                    act.wait_ge(hot_tile, g + 1)
                    if from_(it, 1):
                        act.wait_ge(tab_ps, g - 1)
                    for k in range(TOPK):
                        last = nc.scalar.activation(hot_val[p][:, 1, k, :, :], hot_hi[p][:, k, :, :], ACT.Copy,
                                                    scale=const("pair_no")[:, k:k + 1])
                    last.then_inc(hot_by_row, 1)
            by_row(0)
            with act.Fori(1, ITS) as it:
                by_row(it)
            exp_relu(act, NG - 1)
            act.wait_ge(pool_const, 2)
            nc.scalar.activation(scrap["scalar"], scrap["zero"], ACT.Gelu_apprx_tanh).then_inc(warmed, 1)
            expert = expert_of(act)

            def even(b, r, i, p):
                if from_(i, 2) and till(i, NT + 1):
                    attn_o(act, i - 2)
                if r == 0 and till(b, B - 1):
                    qT_copy(act, b)
                if till(i, NT - 2):
                    attn_high(act, i + 1, 1 - r)

            def odd(b, r, i, p):
                if from_(i, 1) and till(i, NT):
                    attn_yT(act, i - 1)
            steps(act, lambda act, base, s, between=None: expert_scalar(act, base, s, expert, between), even, odd,
                  first=lambda: attn_high(act, 0, 0))
            act.wait_ge(warmed, 1)
            nc.scalar.activation(scrap["scalar"], scrap["zero"], ACT.Exp)
            act.wait_ge(pads, 3)
            normalise(act, 1, 0, 0)
            xT2_copy(act, 0, 0)
            mu_scalar(act, 0, 0)
            groups(act, group_scalar)
            yT1_copy(act, NG - 1)

        @block.gpsimd
        def _(pool):
            nc.gpsimd.memset(mhalf[:, :], -0.5).then_inc(pool_const, 1)
            nc.gpsimd.memset(scrap["zero"], 0.0).then_inc(pool_const, 1)
            pool.wait_ge(pool_const, 1)
            pool.wait_ge(consts_in, 16)
            front(pool, front_pool)
            for g in range(NG + 1 - SINE_LAG, NG):
                sine(pool, g)
            pool.wait_ge(rot_ready, BY_VECTOR)
            for g in range(BY_VECTOR, NG):
                rotate(pool, nc.gpsimd.tensor_tensor, g)

            pool.wait_ge(route, 1)
            nc.gpsimd.memset(qkv3[:, :, 3 * D:NW], 1.0).then_inc(ones_ready, 1)

            def by_tile(it):
                for p in range(2):
                    g = it * 2 + p
                    pool.wait_ge(hot_tile, g + 1)
                    if from_(it, 1):
                        pool.wait_ge(tab_ps, g - 1)
                    for k in range(TOPK):
                        last = nc.gpsimd.tensor_tensor(
                            hot_val[p][:, 0, k, :, :], hot_hi[p][:, k, :, :],
                            const("tile_no")[:, ds(g * GT, GT)].unsqueeze(2).broadcast_to([P, GT, NS]), ALU.mult)
                    last.then_inc(hot_by_tile, 1)
            by_tile(0)
            with pool.Fori(1, ITS) as it:
                by_tile(it)
            pool.wait_ge(idx_ready, 1)
            for p in range(2):
                pool.wait_ge(xn_saved[p], 16 * ITS)
            for j in range(AHEAD):
                gather(pool, j)
            pool.wait_ge(idx_ready, 2)
            for j in range(NS):
                if j + AHEAD < NS:
                    gather(pool, j + AHEAD)
                scatter(pool, j)
                if (j - SHIFT) % 2 == 0 and (j - SHIFT) // 2 + 1 in range(NT):
                    i = (j - SHIFT) // 2 + 1
                    attn_low_pool(pool, i, i % 2)
                if (j - SHIFT) % 2 == 0 and (j - SHIFT) // 2 - 2 in range(NT):
                    attn_add(pool, (j - SHIFT) // 2 - 2)
            for i in range((NS - 1 - SHIFT) // 2 - 1, NT):
                attn_add(pool, i)
            for g in range(2):
                deviation(pool, 1, g, g)
            groups(pool, group_pool)

        @block.tensor
        def _(pe):
            pe.wait_ge(consts_in, 16)
            pe.wait_ge(wts_in, 16 * 4)
            for n in range(3):
                last = nc.tensor.transpose(ps[4][:, n * P:(n + 1) * P], w_raw[:, n, :], ident)
            last.then_inc(wT_ps, 1)
            pe.wait_ge(wT_ready, 1)
            front(pe, front_tensor)
            pe.wait_ge(w_late_in, 16 * 5)
            pe.wait_ge(qkv_raw, NT)
            for n in range(4):
                nc.tensor.transpose(ps[4][:, n * P:(n + 1) * P], w_raw[:, 3 + n, :], ident)
            nc.tensor.transpose(ps[5][:, 0:NE * NC], w_raw[0:NE * NC, 7, :], ident[0:NE * NC, 0:NE * NC]
                                ).then_inc(w_late_ps, 1)
            pe.wait_ge(rank_in, 1)
            flat = "p a e -> p (a e)"
            pe.wait_ge(xT_ready, NG)
            nc.tensor.matmul(ps[0][:, 0:NT * NE], tri_bf[:, :], m_bf[:, :, :].rearrange(flat), start=True, stop=False)
            nc.tensor.matmul(ps[0][:, 0:NT * NE], ones_bf[:, :], cex_bf[:, :, :].rearrange(flat), start=False, stop=True)
            nc.tensor.matmul(ps[1][:, 0:NE], ones_bf[:, :], cin_bf[:, :], start=True, stop=True).then_inc(rank_ps, 1)
            def table(it, first):
                for p in range(2):
                    g = it * 2 + p
                    pe.wait_ge(hot_rows, g + 1)
                    pe.wait_ge(hot_by_tile, g + 1)
                    pe.wait_ge(hot_by_row, g + 1)
                    for n in range(TOPK * GT):
                        k, i = n // GT, n % GT
                        last = nc.tensor.matmul(ps[2][:, 0:2 * NS], hot_lo[p][:, n, :], hot_val[p][:, :, k, i, :],
                                                start=(first and p == 0 and n == 0), stop=False, skip_group_check=True)
                    last.then_inc(tab_ps, 1)
            table(0, True)
            with pe.Fori(1, ITS) as it:
                table(it, False)
            pe.wait_ge(ones_ready, 1)
            pe.wait_ge(w_late_ready, 1)
            pe.wait_ge(exp_ready, 1)
            pe.wait_ge(late_in, 16 * 3)
            pe.wait_ge(bias_rows, 16 * 6)
            pe.wait_ge(idx_ready, 2)
            expert = expert_of(pe)

            def even(b, r, i, p):
                if from_(i, 2) and till(i, NT + 1):
                    attn_project(pe, i - 2)
                if till(b, B - 1):
                    attn_cumsum(pe, b, r, p)
                    if r == 0:
                        q_transpose(pe, b, p)

            def odd(b, r, i, p):
                if from_(i, 1) and till(i, NT):
                    attn_transpose(pe, i - 1, b, r if till(b, B - 1) else 1)
            steps(pe, lambda pe, base, s, between=None: expert_tensor(pe, base, s, expert, between), even, odd)
            pe.wait_ge(pads, 3)
            xT2_transpose(pe, 0, 0)
            groups(pe, group_tensor)
            y1_transpose(pe, NG - 1)
            project2_tensor(pe, NG - 1)

        @block.vector
        def _(v):
            TT, TS, RED = nc.vector.tensor_tensor, nc.vector.tensor_scalar, nc.vector.tensor_reduce
            v.wait_ge(consts_in, 16)
            nc.vector.tensor_copy(ones_bf[:, :], const("ones"))
            nc.vector.tensor_copy(tri_bf[:, :], const("tri_excl"))
            nc.vector.tensor_copy(tri_r[:, :], const("tri_incl"))
            nc.vector.tensor_copy(iota_bf[:, :], const("iota")).then_inc(small_ready, 1)
            front(v, front_vector)

            n_route = [0]

            def done(ins):
                n_route[0] += 1
                ins.then_inc(route, 1)
                v.wait_ge(route, n_route[0])

            def per_tile(a):
                return a.unsqueeze(2).broadcast_to([P, NT, NE])

            def per_expert(a):
                return a.unsqueeze(1).broadcast_to([P, NT, NE])

            def row(n):
                return r32[:, n, :]

            A3, logits = rt, lgb
            v.wait_ge(qkv_raw, NT)
            v.wait_ge(bias_in, 16 * 5)
            done(TT(logits, qkv3[:, :, 3 * D:NQ], per_expert(bg_sb[:, :]), ALU.add))
            cur = logits
            for k in range(TOPK):
                done(RED(row(k), cur, AX.X, ALU.max))
                done(TT(A3[0], cur, per_tile(row(k)), ALU.is_equal))
                done(TT(A3[0], A3[0], per_expert(const("first")), ALU.mult))
                done(RED(row(2), A3[0], AX.X, ALU.max))
                done(TT(oh[k], per_expert(const("first")), per_tile(row(2)), ALU.is_equal))
                if k == 0:
                    TT(A3[3], logits, per_tile(row(0)), ALU.subtract).then_inc(gate_in, 1)
                    done(nc.vector.scalar_tensor_tensor(out=A3[1], in0=oh[0], scalar=-BIG, in1=logits,
                                                        op0=ALU.mult, op1=ALU.add))
                    cur = A3[1]
            done(TT(A3[0], oh[0], oh[1], ALU.add))
            nc.vector.tensor_copy(m_bf[:, :, :], A3[0])
            a, b_, sh = 0, 1, 1
            while sh < NT:
                nc.vector.tensor_copy(rt[b_][:, 0:sh, :], rt[a][:, 0:sh, :])
                done(TT(rt[b_][:, sh:, :], rt[a][:, sh:, :], rt[a][:, 0:NT - sh, :], ALU.add))
                a, b_, sh = b_, a, sh * 2
            TT(cex_bf[:, :, :], rt[a][:, :, :], m_bf[:, :, :], ALU.subtract)
            nc.vector.tensor_copy(cin_bf[:, :], rt[a][:, NT - 1, :]).then_inc(rank_in, 1)
            TS(one_mu[:, :], mu[:, :], -1.0, 1.0, ALU.mult, ALU.add)
            nc.vector.tensor_copy(bias_part[:, 0, :], bias_sp[:, :]).then_inc(bias_split, 1)
            v.wait_ge(bias_split, 1)
            TT(bias_rest[:, 0, :], bias_sp[:, :], bias_part[:, 0, :], ALU.subtract).then_inc(bias_split, 1)
            v.wait_ge(bias_split, 2)
            nc.vector.tensor_copy(bias_part[:, 1, :], bias_rest[:, 0, :]).then_inc(bias_split, 1)
            v.wait_ge(bias_split, 3)
            TT(bias_rest[:, 1, :], bias_rest[:, 0, :], bias_part[:, 1, :], ALU.subtract).then_inc(bias_split, 1)
            v.wait_ge(bias_split, 4)
            nc.vector.tensor_copy(bias_part[:, 2, :], bias_rest[:, 1, :]).then_inc(bias_split, 1)
            v.wait_ge(rank_ps, 1)
            done(TS(e8[:, 0, :], ps[1][:, 0:NE], float(P - 1), None, ALU.add))
            done(nc.vector.tensor_copy(e8i[:, 0, :], e8[:, 0, :]))
            done(TS(e8i[:, 1, :], e8i[:, 0, :], 7, None, ALU.logical_shift_right))
            done(nc.vector.tensor_copy(e8[:, 1, :], e8i[:, 1, :]))
            a_, b2_ = 1, 2
            for sh in (1, 2, 4):
                nc.vector.tensor_copy(e8[:, b2_, 0:sh], e8[:, a_, 0:sh])
                done(TT(e8[:, b2_, sh:], e8[:, a_, sh:], e8[:, a_, 0:NE - sh], ALU.add))
                a_, b2_ = b2_, b2_ + 1
            ends = e8[:, a_, :]
            done(TT(e8[:, 6, :], ends, e8[:, 1, :], ALU.subtract))
            done(TS(e8[:, 7, :], e8[:, 6, :], float(P), None, ALU.mult))
            done(TT(A3[0], ps[0][:, 0:NT * NE].rearrange("p (a e) -> p a e", e=NE), per_expert(e8[:, 7, :]), ALU.add))
            TT(A3[1], A3[0], oh[0], ALU.mult)
            done(TT(A3[2], A3[0], oh[1], ALU.mult))
            RED(row(3), A3[1], AX.X, ALU.add)
            done(RED(row(4), A3[2], AX.X, ALU.add))
            done(nc.vector.tensor_copy(posi[:, 0, :, :], r32[:, 3:5, :]))
            TS(posi[:, 1, :, :], posi[:, 0, :, :], 7, None, ALU.logical_shift_right)
            done(TS(posi[:, 2, :, :], posi[:, 0, :, :], P - 1, None, ALU.bitwise_and))
            nc.vector.tensor_copy(pos_hi[:, :, :], posi[:, 1, :, :])
            done(nc.vector.tensor_copy(pos_lo[:, :, :], posi[:, 2, :, :]))

            def onehots(it):
                for p in range(2):
                    g = it * 2 + p
                    if from_(it, 1):
                        v.wait_ge(hot_by_tile, g - 1)
                        v.wait_ge(hot_by_row, g - 1)
                    last = TT(hot_hi[p][:, :, :, :], iota_bf[:, 0:NS].unsqueeze(1).unsqueeze(1).broadcast_to([P, TOPK, GT, NS]),
                              pos_hi[:, :, ds(g * GT, GT)].unsqueeze(3).broadcast_to([P, TOPK, GT, NS]), ALU.is_equal)
                    last.then_inc(hot_tile, 1)
                    if from_(it, 1):
                        v.wait_ge(tab_ps, g - 1)
                    last = TT(hot_lo[p][:, :, :].rearrange("p (k i) r -> p k i r", k=TOPK),
                              iota_bf[:, :].unsqueeze(1).unsqueeze(1).broadcast_to([P, TOPK, GT, P]),
                              pos_lo[:, :, ds(g * GT, GT)].unsqueeze(3).broadcast_to([P, TOPK, GT, P]), ALU.is_equal)
                    last.then_inc(hot_rows, 1)
            onehots(0)
            with v.Fori(1, ITS) as it:
                onehots(it)
            done(TT(cmp8, const("iota")[:, 0:NS].unsqueeze(2).broadcast_to([P, NS, NE]),
                    ends.unsqueeze(1).broadcast_to([P, NS, NE]), ALU.is_ge))
            done(RED(tab[:, 0, :], cmp8, AX.X, ALU.add))
            done(TS(tab[:, 0, :], tab[:, 0, :], float(NE - 1), None, ALU.min))
            nc.vector.tensor_copy(slot_exp[:, :], tab[:, 0, :]).then_inc(exp_ready, 1)
            v.wait_ge(tab_ps, NG)
            done(TS(tab[:, 1, :], ps[2][:, 0:NS], float(2 * P), -float(2 * P), ALU.mult, ALU.add))
            TS(tab[:, 3, :], ps[2][:, 0:NS], 0.0, None, ALU.is_equal)
            done(TT(tab[:, 2, :], ps[2][:, NS:2 * NS], tab[:, 1, :], ALU.add))
            done(TS(tab[:, 1, :], tab[:, 2, :], 0.0, None, ALU.max))
            done(nc.vector.tensor_copy(tabi[:, :], tab[:, 1, :]))
            TS(slot_tok[:, :], tabi[:, :], 1, None, ALU.logical_shift_right).then_inc(idx_ready, 1)
            done(TT(tab[:, 3, :], tab[:, 3, :], const("slot_row"), ALU.mult))
            done(TT(tab[:, 3, :], tab[:, 3, :], tab[:, 2, :], ALU.add))
            nc.vector.tensor_copy(slot_dst[:, :], tab[:, 3, :]).then_inc(idx_ready, 1)
            v.wait_ge(gate_exp, 1)
            RED(row(5), A3[3], AX.X, ALU.add)
            TT(A3[1], A3[3], oh[0], ALU.mult)
            done(TT(A3[2], A3[3], oh[1], ALU.mult))
            RED(row(6), A3[1], AX.X, ALU.add)
            RED(row(7), A3[2], AX.X, ALU.add)
            done(nc.vector.reciprocal(row(8), row(5)))
            TT(row(6), row(6), row(8), ALU.mult)
            done(TT(row(7), row(7), row(8), ALU.mult))
            done(nc.vector.scalar_tensor_tensor(out=row(9), in0=row(6), scalar=EPS_GATE, in1=row(7), op0=ALU.add, op1=ALU.add))
            done(nc.vector.reciprocal(row(10), row(9)))
            TT(sel[0][:, :], row(6), row(10), ALU.mult)
            done(TT(sel[1][:, :], row(7), row(10), ALU.mult))

            def batch(b, p, more=True):
                attn_outer(v, b, 1, p)
                attn_apply(v, b, 0, p)
                attn_low(v, b * 2 + 1, 1)
                if more:
                    phi(v, b + 1, 1 - p)
                attn_divide(v, b * 2, 0)
                if more:
                    attn_outer(v, b + 1, 0, 1 - p)
                attn_apply(v, b, 1, p)
                if more:
                    attn_low(v, b * 2 + 2, 0)
                attn_divide(v, b * 2 + 1, 1)
            v.wait_ge(phi_parts, NG)
            phi(v, 0, 0)
            attn_outer(v, 0, 0, 0)
            attn_low(v, 0, 0)
            for b in range(2):
                batch(b, b)
            with v.Fori(1, B // 2 - 1) as bb:
                for p in range(2):
                    batch(bb * 2 + p, p)
            batch(B - 2, 0)
            batch(B - 1, 1, more=False)

            v.wait_ge(x_attn, NT)
            for p in range(2):
                nc.vector.memset(xT2_of(p)[:, :, 0:1], 0.0).then_inc(pads, 1)
            nc.vector.memset(v_aug[:, :, D:DA], 1.0).then_inc(pads, 1)
            for g in range(2):
                combine(v, g, g)
                moments(v, 1, g, g)
            mix(v, 0, 0)
            groups(v, group_vector)
            finish(v, NG - 1, 1)

    return st


_INS = ['L0_attn_x', 'L0_attn_Wq', 'L0_attn_Wk', 'L0_attn_Wv', 'L0_attn_Wo', 'L0_ffn_Wg', 'L0_ffn_bg', 'L0_ffn_W1',
        'L0_ffn_b1', 'L0_ffn_W2', 'L0_ffn_b2', 'L1_attn_w_qkv', 'L1_attn_w_proj', 'L1_attn_b_proj', 'L1_ffn_W_r',
        'L1_ffn_W_k', 'L1_ffn_W_v', 'L1_ffn_mu_r', 'L1_ffn_mu_k']


def kernel(**inputs):
    import concourse.bacc as _bacc
    from concourse.bass_utils import run_bass_kernel_spmd as _run

    nc = _bacc.Bacc("TRN2", target_bir_lowering=False, num_devices=1)
    arrays, args = {}, []
    for name in _INS:
        a = np.ascontiguousarray(inputs[name])
        arrays[f"in_{name}"] = a
        args.append(nc.dram_tensor(f"in_{name}", a.shape, mybir.dt.from_np(a.dtype), kind="ExternalInput").ap())
    arrays["in_consts"] = constant_table()
    args.append(nc.dram_tensor("in_consts", (P, NCONST), mybir.dt.float32, kind="ExternalInput").ap())
    out = nc.dram_tensor("out_0", (B, T, D), mybir.dt.float32, kind="ExternalOutput").ap()
    build(nc, *args, out)
    r = _run(nc, [arrays], core_ids=[0])
    return r.results[0]["out_0"]
```
